# Optimizing a Trainium2 kernel written in Bass

```python
import numpy as np
import jax
import jax.numpy as jnp

def _softmax(x, axis=-1):
    return jax.nn.softmax(x, axis=axis)

def _gelu(x):
    return jax.nn.gelu(x, approximate=True)

def _silu(x):
    return jax.nn.silu(x)

def _sigmoid(x):
    return jax.nn.sigmoid(x)

def _layernorm(x, axis=-1, eps=1e-05):
    m = jnp.mean(x, axis=axis, keepdims=True)
    v = jnp.var(x, axis=axis, keepdims=True)
    return (x - m) / jnp.sqrt(v + eps)

def _scatter_add(tgt, idx, src, axis=0):
    return tgt.at[idx].add(src)

def _segment_sum(src, seg, n):
    return jax.ops.segment_sum(src, seg, n)
kernel_name = 'mk_sandwich_d1_jaxref_r4_b545b0'

def setup_inputs(seed: int=0):
    np.random.seed(seed)
    _w = jnp.asarray

    def _L0_attn_setup():
        import jax, jax.numpy as jnp
        import numpy as np
        B, S, D = (4, 1024, 512)
        THETA = 10000.0
        LN_EPS = 1e-05

        def _layernorm(x, w, b):
            mu = jnp.mean(x, axis=-1, keepdims=True)
            var = jnp.mean(jnp.square(x - mu), axis=-1, keepdims=True)
            return (x - mu) * jax.lax.rsqrt(var + LN_EPS) * w + b

        def _rope_half(x):
            rot_dim = x.shape[-1] // 2
            seq = x.shape[-2]
            inv_freq = 1.0 / THETA ** (jnp.arange(0, rot_dim, 2, dtype=jnp.float32) / rot_dim)
            freqs = jnp.arange(seq, dtype=jnp.float32)[:, None] * inv_freq[None, :]
            freqs = jnp.repeat(freqs, 2, axis=-1)
            cos, sin = (jnp.cos(freqs), jnp.sin(freqs))
            xl, xr = (x[..., :rot_dim], x[..., rot_dim:])
            x1, x2 = (xl[..., 0::2], xl[..., 1::2])
            rh = jnp.stack((-x2, x1), axis=-1).reshape(xl.shape)
            return jnp.concatenate([xl * cos + rh * sin, xr], axis=-1)

        def _cos_sim(x):
            return x / jnp.linalg.norm(x, axis=-1, keepdims=True)
        key = jax.random.key(seed)
        k0, k1, k2 = jax.random.split(key, 3)
        X = jax.random.normal(k0, (B, S, D), jnp.float32)
        ln_w = jnp.ones((D,), jnp.float32)
        ln_b = jnp.zeros((D,), jnp.float32)
        W_in = jax.random.normal(k1, (D, 3 * D), jnp.float32) * D ** (-0.5)
        b_in = jnp.zeros((3 * D,), jnp.float32)
        W_out = jax.random.normal(k2, (D, D), jnp.float32) * D ** (-0.5)
        b_out = jnp.zeros((D,), jnp.float32)
        return {'X': X, 'ln_w': ln_w, 'ln_b': ln_b, 'W_in': W_in, 'b_in': b_in, 'W_out': W_out, 'b_out': b_out}
    _L0_attn_in = _L0_attn_setup()

    def _L0_ffn_setup():
        import jax, jax.numpy as jnp
        import numpy as np
        K = 2

        def gelu(v):
            return jax.nn.gelu(v, approximate=False)
        key = jax.random.key(seed)
        ks = jax.random.split(key, 10)
        B, S, D, H, E = (4, 512, 512, 256, 8)
        SH = 2 * H
        u = lambda k_, shape, b: jax.random.uniform(k_, shape, jnp.float32, -b, b)
        return {'x': jax.random.normal(ks[0], (B, S, D), jnp.float32), 'gate_w': u(ks[1], (D, E), 1.0 / D), 'w1': u(ks[2], (E, D, H), 1.0 / D), 'b1': u(ks[3], (E, H), 1.0 / np.sqrt(D)), 'w2': u(ks[4], (E, H, D), 1.0 / H), 'b2': u(ks[5], (E, D), 1.0 / np.sqrt(H)), 'shared_w1': u(ks[6], (D, SH), 1.0 / D), 'shared_b1': u(ks[7], (SH,), 1.0 / np.sqrt(D)), 'shared_w2': u(ks[8], (SH, D), 1.0 / SH), 'shared_b2': u(ks[9], (D,), 1.0 / np.sqrt(SH))}
    _L0_ffn_in = _L0_ffn_setup()
    _d = {'L0_attn_X': _L0_attn_in['X'], 'L0_attn_ln_w': _L0_attn_in['ln_w'], 'L0_attn_ln_b': _L0_attn_in['ln_b'], 'L0_attn_W_in': _L0_attn_in['W_in'], 'L0_attn_b_in': _L0_attn_in['b_in'], 'L0_attn_W_out': _L0_attn_in['W_out'], 'L0_attn_b_out': _L0_attn_in['b_out'], 'L0_ffn_gate_w': _L0_ffn_in['gate_w'], 'L0_ffn_w1': _L0_ffn_in['w1'], 'L0_ffn_b1': _L0_ffn_in['b1'], 'L0_ffn_w2': _L0_ffn_in['w2'], 'L0_ffn_b2': _L0_ffn_in['b2'], 'L0_ffn_shared_w1': _L0_ffn_in['shared_w1'], 'L0_ffn_shared_b1': _L0_ffn_in['shared_b1'], 'L0_ffn_shared_w2': _L0_ffn_in['shared_w2'], 'L0_ffn_shared_b2': _L0_ffn_in['shared_b2']}
    _x0 = _d['L0_attn_X']
    _d['L0_attn_X'] = jax.random.normal(jax.random.fold_in(jax.random.key(seed), 1), (2, 2048, 512), dtype=_x0.dtype)
    del _x0
    return _d

def reference(L0_attn_X, L0_attn_ln_w, L0_attn_ln_b, L0_attn_W_in, L0_attn_b_in, L0_attn_W_out, L0_attn_b_out, L0_ffn_gate_w, L0_ffn_w1, L0_ffn_b1, L0_ffn_w2, L0_ffn_b2, L0_ffn_shared_w1, L0_ffn_shared_b1, L0_ffn_shared_w2, L0_ffn_shared_b2):

    def _L0_attn_ref(X, ln_w, ln_b, W_in, b_in, W_out, b_out):
        import jax, jax.numpy as jnp
        import numpy as np
        B, S, D = (4, 1024, 512)
        THETA = 10000.0
        LN_EPS = 1e-05

        def _layernorm(x, w, b):
            mu = jnp.mean(x, axis=-1, keepdims=True)
            var = jnp.mean(jnp.square(x - mu), axis=-1, keepdims=True)
            return (x - mu) * jax.lax.rsqrt(var + LN_EPS) * w + b

        def _rope_half(x):
            rot_dim = x.shape[-1] // 2
            seq = x.shape[-2]
            inv_freq = 1.0 / THETA ** (jnp.arange(0, rot_dim, 2, dtype=jnp.float32) / rot_dim)
            freqs = jnp.arange(seq, dtype=jnp.float32)[:, None] * inv_freq[None, :]
            freqs = jnp.repeat(freqs, 2, axis=-1)
            cos, sin = (jnp.cos(freqs), jnp.sin(freqs))
            xl, xr = (x[..., :rot_dim], x[..., rot_dim:])
            x1, x2 = (xl[..., 0::2], xl[..., 1::2])
            rh = jnp.stack((-x2, x1), axis=-1).reshape(xl.shape)
            return jnp.concatenate([xl * cos + rh * sin, xr], axis=-1)

        def _cos_sim(x):
            return x / jnp.linalg.norm(x, axis=-1, keepdims=True)
        h = _layernorm(X, ln_w, ln_b)
        qkv = h @ W_in + b_in
        Q, K, V = jnp.split(qkv, 3, axis=-1)
        Q = _rope_half(Q)
        K = _rope_half(K)
        A = jnp.sum(_cos_sim(K) * V, axis=-2)
        Y = A[:, None, :] * Q
        Y = Y @ W_out + b_out
        return Y + X

    def _L0_ffn_ref(x, gate_w, w1, b1, w2, b2, shared_w1, shared_b1, shared_w2, shared_b2):
        import jax, jax.numpy as jnp
        import numpy as np
        K = 2

        def gelu(v):
            return jax.nn.gelu(v, approximate=False)
        B, S, D = x.shape
        E = gate_w.shape[1]
        xf = x.reshape(-1, D)
        logits = xf @ gate_w
        top_logits, top_idx = jax.lax.top_k(logits, K)
        top_gates = jax.nn.softmax(top_logits, axis=-1)
        gates = jnp.sum(jax.nn.one_hot(top_idx, E, dtype=xf.dtype) * top_gates[..., None], axis=1)
        h = gelu(jnp.einsum('nd,edh->neh', xf, w1) + b1)
        out_e = jnp.einsum('neh,ehd->ned', h, w2) + b2
        routed = jnp.einsum('ne,ned->nd', gates, out_e)
        shared = gelu(xf @ shared_w1 + shared_b1) @ shared_w2 + shared_b2
        return (routed + shared).reshape(B, S, D)
    x = L0_attn_X
    x = x + _layernorm(_L0_attn_ref(_layernorm(x, axis=-1), L0_attn_ln_w, L0_attn_ln_b, L0_attn_W_in, L0_attn_b_in, L0_attn_W_out, L0_attn_b_out), axis=-1)
    x = x + _layernorm(_L0_ffn_ref(_layernorm(x, axis=-1), L0_ffn_gate_w, L0_ffn_w1, L0_ffn_b1, L0_ffn_w2, L0_ffn_b2, L0_ffn_shared_w1, L0_ffn_shared_b1, L0_ffn_shared_w2, L0_ffn_shared_b2), axis=-1)
    return x

_drawn_inputs = setup_inputs


def setup_inputs(seed=0):
    import zlib

    import numpy as np

    out = dict(_drawn_inputs(seed))
    spreads = {'L0_attn_ln_w': (1.0, 0.2),
     'L0_attn_ln_b': (0.0, 0.1),
     'L0_attn_b_in': (0.0, 0.1),
     'L0_attn_b_out': (0.0, 0.1)}
    factors = {'L0_ffn_w1': 8.0,
     'L0_ffn_b1': 8.0,
     'L0_ffn_w2': 8.0,
     'L0_ffn_shared_w1': 8.0,
     'L0_ffn_shared_b1': 8.0,
     'L0_ffn_shared_w2': 8.0}
    for name, (base, spread) in spreads.items():
        noise = np.random.default_rng([zlib.crc32(name.encode()), seed]).standard_normal(out[name].shape)
        drawn = base * np.exp(spread * noise) if base else spread * noise
        out[name] = jnp.asarray(drawn.astype(out[name].dtype))
    for name, factor in factors.items():
        out[name] = (out[name] * factor).astype(out[name].dtype)
    return out
```

```python
from contextlib import ExitStack

import numpy as np

import concourse.bass as bass
from concourse import mybir

P = 128
F32 = mybir.dt.float32
F32R = mybir.dt.float32r
U32 = mybir.dt.uint32
ALU = mybir.AluOpType
ACT = mybir.ActivationFunctionType
EPS = 1e-5
THETA = 10000.0


def sandwich_kernel(nc, X, ln_w, ln_b, W_in, b_in, W_out, b_out, gate_w, w1, b1, w2, b2,
                    sw1, sb1, sw2, sb2, b_q, rope_tok, rope_feat, identity, out):
    B, S, D = X.shape
    E, _, H = w1.shape
    SH = sw1.shape[1]
    N = B * S
    KD = D // P
    GT = 4
    G = GT * P
    NG = N // G
    GB = NG // B
    NT = N // P
    R = P
    assert D == 4 * P and G == 512 and NG % 2 == 0 and GB % 2 == 0

    def grouped(ap):
        return ap.rearrange("(g t p) d -> g p t d", p=P, t=GT)

    x_groups = grouped(X.rearrange("b s d -> (b s) d"))
    out_groups = grouped(out.rearrange("b s d -> (b s) d"))
    x2_dram = nc.dram_tensor("x2_scratch", (N, D), F32, kind="Internal").ap()
    n3_dram = nc.dram_tensor("n3_scratch", (N, D), F32, kind="Internal").ap()
    x2_groups, n3_groups = grouped(x2_dram), grouped(n3_dram)
    tok_groups = grouped(rope_tok)
    feat_groups = rope_feat.rearrange("c p (g t) -> g p c t", t=G)

    def col(ap):
        return ap.rearrange("(k p) -> p k", p=P)

    top = ExitStack()
    with top:
        def keep(name, shape, dt=F32):
            return top.enter_context(nc.sbuf_tensor(name, shape, dt))

        ident = keep("ident", [P, P])
        logits = keep("logits", [P, NT, E])
        tops = keep("tops", [P, NT, 8])
        top_at = keep("top_at", [P, NT, 8], U32)

        attention(nc, locals())
        ffn(nc, locals())


def value(eng, x):
    return x if isinstance(x, int) else eng.snap(eng.to_reg(x))


def attention(nc, v):
    (B, S, D, E, KD, GT, G, NG, GB, NT, R) = (v[n] for n in "B S D E KD GT G NG GB NT R".split())
    x_groups, x2_groups, n3_groups = v["x_groups"], v["x2_groups"], v["n3_groups"]
    tok_groups, feat_groups, col = v["tok_groups"], v["feat_groups"], v["col"]
    ident, logits, tops, top_at = v["ident"], v["logits"], v["tops"], v["top_at"]
    W_in, W_out, b_in = v["W_in"], v["W_out"], v["b_in"]

    with ExitStack() as ctx:
        def sb(name, shape, dt=F32, where=ctx):
            return where.enter_context(nc.sbuf_tensor(name, shape, dt))

        def sem(name):
            return ctx.enter_context(nc.semaphore(name))

        def bank(name):
            return ctx.enter_context(nc.psum_tensor(name, [P, 512], F32))

        mm = [bank(f"mm{i}") for i in range(4)]
        tp = [bank(f"tp{i}") for i in range(2)]
        gl = bank("gl")
        acol_ps = bank("acol_ps")

        wq_hi, wq_lo = sb("wq_hi", [P, KD, D], F32R), sb("wq_lo", [P, KD, D], F32R)
        wo_hi, wo_lo = sb("wo_hi", [P, B, KD, D], F32R), sb("wo_lo", [P, B, KD, D], F32R)
        gw = sb("gw", [P, KD, E])
        NSTAGE = 3
        stage = [sb(f"stage{i}", [P, D]) for i in range(NSTAGE)]
        lnw, lnb, bq = sb("lnw", [P, KD]), sb("lnb", [P, KD]), sb("bq", [P, KD])
        bkv, bo = sb("bkv", [P, 2, D]), sb("bo", [P, D])
        half = sb("half", [P, 8])
        ones = sb("ones", [P, 1])
        acc = sb("acc", [P, B, D])
        acol = sb("acol", [P, B, KD])

        xg = [sb(f"xg{i}", [P, GT, D]) for i in range(2)]
        hn = sb("hn", [P, GT, D])
        bst = sb("bst", [P, GT, 6])
        mv = [sb(f"mv{i}", [P, GT, 2]) for i in range(2)]
        vp = sb("vp", [P, 2, GT])
        rs = [sb(f"rs{i}", [P, 2, GT]) for i in range(2)]
        nm = [sb(f"nm{i}", [P, GT]) for i in range(2)]
        hb = [sb(f"hb{i}", [P, G]) for i in range(2)]
        h_hi = [sb(f"h_hi{i}", [P, KD, G], F32R) for i in range(2)]
        h_lo = [sb(f"h_lo{i}", [P, KD, G], F32R) for i in range(2)]

        with ExitStack() as first:
            wkv_hi = sb("wkv_hi", [P, 2, KD, D], F32R, first)
            wkv_lo = sb("wkv_lo", [P, 2, KD, D], F32R, first)
            rt = [sb(f"rt{i}", [P, GT, 2, R], where=first) for i in range(2)]
            kb = [sb(f"kb{i}", [P, D], where=first) for i in range(2)]
            vb = [sb(f"vb{i}", [P, D], where=first) for i in range(2)]
            sq = [sb(f"sq{i}", [P, D], where=first) for i in range(2)]
            ssq = [sb(f"ssq{i}", [P, 1], where=first) for i in range(2)]
            rn = [sb(f"rn{i}", [P, 1], where=first) for i in range(2)]
            rot = sb("rot", [P, 2, 2, R], where=first)
            prod = [sb(f"prod{i}", [P, D], where=first) for i in range(2)]
        rf = [sb(f"rf{i}", [P, 2, G]) for i in range(2)]
        qb = sb("qb", [P, KD, G])
        rc, rsn = sb("rc", [P, 2, G]), sb("rsn", [P, 2, G])
        q_hi, q_lo = sb("q_hi", [P, KD, G], F32R), sb("q_lo", [P, KD, G], F32R)
        n1 = sb("n1", [P, GT, D])
        z = sb("z", [P, GT, D])
        n3 = sb("n3", [P, GT, D])
        n3t = sb("n3t", [P, KD, G])
        zst, zmv = sb("zst", [P, GT, 6]), sb("zmv", [P, GT, 2])
        zv, zr, znm = sb("zv", [P, GT]), sb("zr", [P, GT]), sb("znm", [P, GT])
        xst, xmv = sb("xst", [P, GT, 6]), sb("xmv", [P, GT, 2])
        xv, xr, xnm = sb("xv", [P, GT]), sb("xr", [P, GT]), sb("xnm", [P, GT])
        lg = sb("lg", [P, GT, E])
        mx, mi = sb("mx", [P, GT, 8]), sb("mi", [P, GT, 8], U32)

        consts_in = sem("consts_in")
        half_set, ones_set = sem("half_set"), sem("ones_set")
        x_in = [sem(f"x_in{i}") for i in range(2)]
        rt_in = [sem(f"rt_in{i}") for i in range(2)]
        rf_in = [sem(f"rf_in{i}") for i in range(2)]
        raw_in = [sem(f"raw_in{i}") for i in range(NSTAGE)]
        w_hi_done, w_split = sem("w_hi_done"), sem("w_split")
        stats_done, aggr_done, var_ready, rs_ready = sem("stats_done"), sem("aggr_done"), sem("var_ready"), sem("rs_ready")
        nm_ready, h_normed = sem("nm_ready"), sem("h_normed")
        tp_full, tp_free = sem("tp_full"), sem("tp_free")
        h_hi_done, h_split = sem("h_hi_done"), sem("h_split")
        kv_full, kv_free = sem("kv_full"), sem("kv_free")
        k_parts, k_rotated = sem("k_parts"), sem("k_rotated")
        v_biased = sem("v_biased")
        ssq_ready, rn_ready = sem("ssq_ready"), sem("rn_ready")
        prod_ready, acc_done = sem("prod_ready"), sem("acc_done")
        acol_full, acol_ready = sem("acol_full"), sem("acol_ready")
        a_over = sem("a_over")
        q_full, q_free = sem("q_full"), sem("q_free")
        q_biased = q_free
        q_cos, q_sin, q_rotated = sem("q_cos"), sem("q_sin"), sem("q_rotated")
        q_hi_done, q_split = sem("q_hi_done"), sem("q_split")
        n1_raw, n1_ready = sem("n1_raw"), sem("n1_ready")
        y_full, y_free = sem("y_full"), sem("y_free")
        zst_done, zmv_done, zv_ready, zr_ready, znm_ready, zn_ready = (
            sem("zst_done"), sem("zmv_done"), sem("zv_ready"), sem("zr_ready"), sem("znm_ready"), sem("zn_ready"))
        x2_ready, xst_done, xmv_done, xv_ready, xr_ready, xnm_ready, n3_ready = (
            sem("x2_ready"), sem("xst_done"), sem("xmv_done"), sem("xv_ready"), sem("xr_ready"), sem("xnm_ready"),
            sem("n3_ready"))
        x2_stored, n3_stored = sem("x2_stored"), sem("n3_stored")
        n3t_ready, gl_full, lg_ready, mx_ready, mi_ready, tops_kept = (
            sem("n3t_ready"), sem("gl_full"), sem("lg_ready"), sem("mx_ready"), sem("mi_ready"), sem("tops_kept"))

        chunks = [(W_in[k * P:(k + 1) * P, (1 + c) * D:(2 + c) * D], wkv_hi[:, c, k, :], wkv_lo[:, c, k, :], None)
                  for c in range(2) for k in range(KD)]
        N_KV = len(chunks)
        chunks += [(W_in[k * P:(k + 1) * P, 0:D], wq_hi[:, k, :], wq_lo[:, k, :], None) for k in range(KD)]
        N_Q = len(chunks)
        chunks += [(W_out[k * P:(k + 1) * P, :], wo_hi[:, b, k, :], wo_lo[:, b, k, :], (b, k))
                   for b in range(B) for k in range(KD)]
        N_ALL = len(chunks)
        NB_A = 4

        block = ctx.enter_context(nc.Block())

        @block.sync
        def _(sp):
            def load_chunk(n):
                if n >= NSTAGE:
                    sp.wait_ge(w_split, n - NSTAGE + 1)
                sp.dma_start(stage[n % NSTAGE][:, :], chunks[n][0]).then_inc(raw_in[n % NSTAGE], 16)

            sp.dma_start(xg[0][:, :, :], x_groups[0]).then_inc(x_in[0], 16)
            sp.dma_start(ident[:, :], v["identity"]).then_inc(consts_in, 16)
            sp.dma_start(lnw[:, :], v["ln_w"]).then_inc(consts_in, 16)
            sp.dma_start(lnb[:, :], v["ln_b"]).then_inc(consts_in, 16)
            for n in range(NSTAGE):
                load_chunk(n)
            sp.dma_start(bq[:, :], v["b_q"]).then_inc(consts_in, 16)
            sp.dma_start(bkv[:, :, :], b_in[D:3 * D].rearrange("(c d) -> c d", c=2).partition_broadcast(P))\
              .then_inc(consts_in, 16)
            sp.dma_start(bo[:, :], v["b_out"].partition_broadcast(P)).then_inc(consts_in, 16)
            sp.dma_start(gw[:, :, :], v["gate_w"].rearrange("(k p) e -> p k e", p=P)).then_inc(consts_in, 16)
            sp.dma_start(rt[0][:, :, :, :], tok_groups[0].rearrange("p t (c r) -> p t c r", c=2)).then_inc(rt_in[0], 16)
            for n in range(NSTAGE, N_KV):
                load_chunk(n)
            sp.dma_start(xg[1][:, :, :], x_groups[1]).then_inc(x_in[1], 16)
            sp.dma_start(rt[1][:, :, :, :], tok_groups[1 % GB].rearrange("p t (c r) -> p t c r", c=2))\
              .then_inc(rt_in[1], 16)
            with sp.Fori(1, NG // 2) as i:
                for u in range(2):
                    g = 2 * i + u
                    sp.wait_ge(h_normed, g - 1)
                    sp.dma_start(xg[u][:, :, :], x_groups[g]).then_inc(x_in[u], 16)
                    sp.wait_ge(k_rotated, GT * (g - 1))
                    sp.dma_start(rt[u][:, :, :, :], tok_groups[g % GB].rearrange("p t (c r) -> p t c r", c=2))\
                      .then_inc(rt_in[u], 16)
            for u in range(2):
                sp.wait_ge(h_normed, NG - 1 + u)
                sp.dma_start(xg[u][:, :, :], x_groups[u]).then_inc(x_in[u], 16)
            for n in range(N_KV, N_Q):
                load_chunk(n)
            sp.wait_ge(a_over, 4)
            for u in range(2):
                sp.dma_start(rf[u][:, :, :], feat_groups[u]).then_inc(rf_in[u], 16)
            for n in range(N_Q, N_ALL):
                load_chunk(n)

            def stores(g, u):
                sp.wait_ge(x2_ready, GT * (g + 1))
                sp.dma_start(x2_groups[g], z[:, :, :]).then_inc(x2_stored, 16)

            def store_n3(g):
                sp.wait_ge(n3_ready, GT * (g + 1))
                sp.dma_start(n3_groups[g], n3[:, :, :]).then_inc(n3_stored, 16)

            with sp.Fori(0, NG // 2 - 1) as i:
                for u in range(2):
                    g = 2 * i + u
                    stores(g, u)
                    sp.dma_start(xg[u][:, :, :], x_groups[g + 2]).then_inc(x_in[u], 16)
                    sp.wait_ge(q_sin, g + 1)
                    sp.wait_ge(q_cos, g + 1)
                    sp.dma_start(rf[u][:, :, :], feat_groups[(g + 2) % GB]).then_inc(rf_in[u], 16)
                    store_n3(g)
            for u in range(2):
                stores(NG - 2 + u, u)
                store_n3(NG - 2 + u)
            sp.wait_ge(x2_stored, 16 * (NG + 1))
            sp.wait_ge(n3_stored, 16 * (NG + 1))

        @block.vector
        def _(dve):
            def split(n):
                raw, (_, hi, lo, bk) = stage[n % NSTAGE], chunks[n]
                dve.wait_ge(w_hi_done, n + 1)
                if bk is None:
                    dve.tensor_tensor(lo, raw[:, :], hi.bitcast(F32), ALU.subtract).then_inc(w_split, 1)
                else:
                    b, k = bk
                    dve.scalar_tensor_tensor(lo, raw[:, :], acol[:, b, k:k + 1], hi.bitcast(F32),
                                             ALU.mult, ALU.subtract).then_inc(w_split, 1)

            def front_stats(f, u, loads):
                dve.wait_ge(x_in[u], 16 * loads)
                for j in range(GT):
                    last = dve.bn_stats(bst[:, j, :], xg[u][:, j, :])
                last.then_inc(stats_done, 1)
                need = value(dve, f + 1)
                dve.wait_ge(half_set, 1)
                dve.wait_ge(stats_done, need)
                for j in range(GT):
                    last = dve.bn_aggr(mv[u][:, j, :], bst[:, j, :])
                last.then_inc(aggr_done, 1)
                dve.wait_ge(aggr_done, f + 1)
                dve.tensor_scalar(vp[:, 0, :], mv[u][:, :, 1], 1.0 + EPS, EPS * EPS, ALU.mult, ALU.add)
                dve.tensor_scalar(vp[:, 1, :], mv[u][:, :, 1], EPS, None, ALU.add).then_inc(var_ready, 1)

            def front_norm(f, u):
                dve.wait_ge(rs_ready, f + 1)
                if not (isinstance(f, int) and f == 0):
                    dve.wait_ge(tp_full, tp_uses(f))
                for j in range(GT):
                    last = dve.tensor_scalar(hn[:, j, :], xg[u][:, j, :], mv[u][:, j, 0:1], rs[u][:, 0, j:j + 1],
                                             ALU.subtract, ALU.mult)
                last.then_inc(h_normed, 1)

            def tp_uses(f):
                return KD * f

            dve.sem_inc(kv_free, NB_A)
            dve.sem_inc(y_free, 2)
            dve.sem_inc(prod_ready, 2)
            dve.memset(half[:, :], -0.5).then_inc(half_set, 1)
            dve.memset(ones[:, :], 1.0).then_inc(ones_set, 1)
            front_stats(0, 0, 1)
            front_norm(0, 0)
            for n in range(N_KV):
                split(n)
            dve.wait_ge(consts_in, 16 * 7)

            def k_tile(g, u, j):
                t = GT * g + j
                dve.wait_ge(prod_ready, t + 1)
                dve.wait_ge(kv_full, 2 * t + 1)
                kj = kb[j % 2]
                dve.tensor_tensor(kj[:, :], mm[2 * j % NB_A][:, :], bkv[:, 0, :], ALU.add).then_inc(kv_free, 1)
                if j == 0:
                    dve.wait_ge(rt_in[u], 16 * (g // 2 + 1))
                dve.wait_ge(kv_free, NB_A + 2 * t + 1)
                pairs = kj[:, 0:2 * R].rearrange("p (h r) -> p h r", h=2)
                for c in range(2):
                    last = dve.tensor_tensor(rot[:, c, :, :], pairs,
                                             rt[u][:, j, c:c + 1, :].to_broadcast([P, 2, R]), ALU.mult)
                last.then_inc(k_parts, 1)
                dve.wait_ge(k_parts, t + 1)
                dve.tensor_tensor(kj[:, 0:R], rot[:, 0, 0, :], rot[:, 1, 1, :], ALU.subtract)
                dve.tensor_tensor(kj[:, R:2 * R], rot[:, 0, 1, :], rot[:, 1, 0, :], ALU.add).then_inc(k_rotated, 1)

            def v_tile(g, j):
                t = GT * g + j
                dve.wait_ge(kv_full, 2 * t + 2)
                dve.tensor_tensor(vb[j % 2][:, :], mm[(2 * j + 1) % NB_A][:, :], bkv[:, 1, :], ALU.add)\
                   .then_inc(kv_free, 1)

            def kv_prod(g, j):
                t = GT * g + j
                dve.wait_ge(rn_ready, t + 1)
                dve.wait_ge(kv_free, NB_A + 2 * t + 2)
                dve.wait_ge(acc_done, t + 1)
                dve.scalar_tensor_tensor(prod[j % 2][:, :], kb[j % 2][:, :], rn[j % 2][:, 0:1], vb[j % 2][:, :],
                                         ALU.mult, ALU.mult).then_inc(prod_ready, 1)

            with dve.Fori(0, NG // 2) as i:
                for u in range(2):
                    g = 2 * i + u
                    front_stats(g + 1, 1 - u, i + 1 + u)
                    k_tile(g, u, 0)
                    v_tile(g, 0)
                    k_tile(g, u, 1)
                    front_norm(g + 1, 1 - u)
                    kv_prod(g, 0)
                    v_tile(g, 1)
                    k_tile(g, u, 2)
                    kv_prod(g, 1)
                    v_tile(g, 2)
                    k_tile(g, u, 3)
                    kv_prod(g, 2)
                    v_tile(g, 3)
                    kv_prod(g, 3)
            dve.wait_ge(prod_ready, 2 + NT)
            dve.sem_inc(a_over, 1)

            for n in range(N_KV, N_Q):
                split(n)
            dve.wait_ge(acol_full, 1)
            dve.tensor_copy(acol[:, :, :], acol_ps[:, 0:B * KD].rearrange("p (b k) -> p b k", b=B))\
               .then_inc(acol_ready, 1)
            dve.wait_ge(a_over, 4)

            def rotate_q(g, u):
                dve.wait_ge(rf_in[u], 16 * (g // 2 + 1))
                dve.wait_ge(q_biased, 2 + KD * g + 2)
                dve.tensor_tensor(rc[:, :, :], qb[:, 0:2, :], rf[u][:, 0:1, :].to_broadcast([P, 2, G]), ALU.mult)\
                   .then_inc(q_cos, 1)
                dve.wait_ge(q_cos, g + 1)
                dve.wait_ge(q_sin, g + 1)
                dve.tensor_tensor(qb[:, 0, :], rc[:, 0, :], rsn[:, 1, :], ALU.subtract)
                dve.tensor_tensor(qb[:, 1, :], rc[:, 1, :], rsn[:, 0, :], ALU.add).then_inc(q_rotated, 1)

            def split_q(g):
                for n, h in enumerate((1, 0)):
                    dve.wait_ge(q_hi_done, 2 * g + n + 1)
                    s = slice(2 * h, 2 * h + 2)
                    dve.tensor_tensor(q_lo[:, s, :], qb[:, s, :], q_hi[:, s, :].bitcast(F32), ALU.subtract)\
                       .then_inc(q_split, 1)

            def token_tiles(g, u, js):
                for j in js:
                    if j == 0:
                        dve.wait_ge(x2_stored, 16 * (g + 1))
                    dve.wait_ge(y_full, GT * g + j + 1)
                    dve.wait_ge(n1_ready, GT * g + j + 1)
                    dve.tensor_tensor(z[:, j, :], mm[2 + j % 2][:, :], n1[:, j, :], ALU.add).then_inc(y_free, 1)
                    dve.wait_ge(y_free, 2 + GT * g + j + 1)
                    last = dve.bn_stats(zst[:, j, :], z[:, j, :])
                if js[-1] == GT - 1:
                    last.then_inc(zst_done, 1)

            def z_moments(g):
                need = value(dve, g + 1)
                dve.wait_ge(half_set, 1)
                dve.wait_ge(zst_done, need)
                for j in range(GT):
                    last = dve.bn_aggr(zmv[:, j, :], zst[:, j, :])
                last.then_inc(zmv_done, 1)
                dve.wait_ge(zmv_done, g + 1)
                dve.tensor_scalar(zv[:, :], zmv[:, :, 1], EPS, None, ALU.add).then_inc(zv_ready, 1)

            def z_shift(g):
                dve.wait_ge(zr_ready, g + 1)
                dve.scalar_tensor_tensor(znm[:, :], zmv[:, :, 0], -1.0, zr[:, :], ALU.mult, ALU.mult)\
                   .then_inc(znm_ready, 1)

            def x2_tiles(g, u):
                for j in range(GT):
                    dve.wait_ge(zn_ready, GT * g + j + 1)
                    dve.tensor_tensor(z[:, j, :], z[:, j, :], xg[u][:, j, :], ALU.add).then_inc(x2_ready, 1)
                    dve.wait_ge(x2_ready, GT * g + j + 1)
                    last = dve.bn_stats(xst[:, j, :], z[:, j, :])
                last.then_inc(xst_done, 1)
                need = value(dve, g + 1)
                dve.wait_ge(half_set, 1)
                dve.wait_ge(xst_done, need)
                for j in range(GT):
                    last = dve.bn_aggr(xmv[:, j, :], xst[:, j, :])
                last.then_inc(xmv_done, 1)
                dve.wait_ge(xmv_done, g + 1)
                dve.tensor_scalar(xv[:, :], xmv[:, :, 1], EPS, None, ALU.add).then_inc(xv_ready, 1)

            def x2_shift(g):
                dve.wait_ge(xr_ready, g + 1)
                dve.scalar_tensor_tensor(xnm[:, :], xmv[:, :, 0], -1.0, xr[:, :], ALU.mult, ALU.mult)\
                   .then_inc(xnm_ready, 1)

            def front_shift(f, u):
                dve.wait_ge(rs_ready, f + 1)
                dve.scalar_tensor_tensor(nm[u][:, :], mv[u][:, :, 0], -1.0, rs[u][:, 1, :], ALU.mult, ALU.mult)\
                   .then_inc(nm_ready, 1)

            def gate(g):
                dve.wait_ge(gl_full, g + 1)
                dve.tensor_copy(lg[:, :, :], gl[:, 0:GT * E].rearrange("p (t e) -> p t e", t=GT)).then_inc(lg_ready, 1)
                need = value(dve, g + 1)
                dve.wait_ge(half_set, 1)
                dve.wait_ge(lg_ready, need)
                for j in range(GT):
                    last = dve.max(mx[:, j, :], lg[:, j, :])
                last.then_inc(mx_ready, 1)
                need = value(dve, g + 1)
                dve.wait_ge(half_set, 1)
                dve.wait_ge(mx_ready, need)
                for j in range(GT):
                    last = dve.max_index(mi[:, j, :], mx[:, j, :], lg[:, j, :])
                last.then_inc(mi_ready, 1)
                dve.tensor_copy(tops[:, bass.ds(GT * g, GT), :], mx[:, :, :])
                dve.wait_ge(mi_ready, g + 1)
                dve.tensor_copy(top_at[:, bass.ds(GT * g, GT), :], mi[:, :, :]).then_inc(tops_kept, 1)

            front_shift(NG, 0)
            rotate_q(0, 0)
            split_q(0)
            for n in range(N_Q, N_ALL):
                split(n)

            def group(g, u, i, last):
                if not last:
                    front_stats(NG + g + 1, 1 - u, NG // 2 + 1 + i + u)
                token_tiles(g, u, [0, 1])
                if not last:
                    dve.wait_ge(rs_ready, NG + g + 2)
                    for j in range(GT):
                        norm = dve.tensor_scalar(hn[:, j, :], xg[1 - u][:, j, :], mv[1 - u][:, j, 0:1],
                                                 rs[1 - u][:, 0, j:j + 1], ALU.subtract, ALU.mult)
                    norm.then_inc(h_normed, 1)
                    front_shift(NG + g + 1, 1 - u)
                token_tiles(g, u, [2, 3])
                z_moments(g)
                z_shift(g)
                x2_tiles(g, u)
                if not last:
                    rotate_q(g + 1, 1 - u)
                x2_shift(g)
                if not last:
                    split_q(g + 1)
                gate(g)

            with dve.Fori(0, NG // 2 - 1) as i:
                for u in range(2):
                    group(2 * i + u, u, i, False)
            for u in range(2):
                group(NG - 2 + u, u, NG // 2 - 1, u == 1)

        @block.scalar
        def _(act):
            def hi_part(n):
                raw, (_, hi, _, bk) = stage[n % NSTAGE], chunks[n]
                act.wait_ge(raw_in[n % NSTAGE], 16 * (n // NSTAGE + 1))
                if bk is None:
                    act.activation(hi, raw[:, :], ACT.Copy).then_inc(w_hi_done, 1)
                else:
                    b, k = bk
                    act.wait_ge(acol_ready, 1)
                    act.activation(hi, raw[:, :], ACT.Identity, scale=acol[:, b, k:k + 1]).then_inc(w_hi_done, 1)

            def front_split(f, u, n0, reader=None):
                for k in range(KD):
                    act.wait_ge(tp_full, n0 + k + 1)
                    if not isinstance(f, int) or f > 0 or k >= 2:
                        act.wait_ge(h_split, KD * f + k - 1)
                    act.activation(hb[k % 2][:, :], tp[k % 2][:, :], ACT.Identity, bias=lnb[:, k:k + 1],
                                   scale=lnw[:, k:k + 1]).then_inc(tp_free, 1)
                    if k == 0 and reader is not None:
                        act.wait_ge(*reader)
                    act.wait_ge(tp_free, 2 + n0 + k + 1)
                    act.activation(h_hi[u][:, k, :], hb[k % 2][:, :], ACT.Copy).then_inc(h_hi_done, 1)

            act.sem_inc(tp_free, 2)
            act.sem_inc(q_free, 2)
            act.wait_ge(consts_in, 16 * 7)
            front_split(0, 0, 0)
            for n in range(N_KV):
                hi_part(n)

            def norm_k(g, j):
                t = GT * g + j
                act.wait_ge(k_rotated, t + 1)
                act.activation(sq[j % 2][:, :], kb[j % 2][:, :], ACT.Square, accum_out=ssq[j % 2][:, 0:1])\
                   .then_inc(ssq_ready, 1)

            with act.Fori(0, NG // 2) as i:
                for u in range(2):
                    g = 2 * i + u
                    norm_k(g, 0)
                    norm_k(g, 1)
                    norm_k(g, 2)
                    front_split(g + 1, 1 - u, KD * (g + 1), (kv_full, 2 * GT * g + 1))
                    norm_k(g, 3)
            act.wait_ge(ssq_ready, NT)
            act.sem_inc(a_over, 1)

            def bias_q(g):
                for m in range(KD):
                    act.wait_ge(q_full, KD * g + m + 1)
                    act.activation(qb[:, m, :], mm[m % 2][:, :], ACT.Identity, bias=bq[:, m:m + 1]).then_inc(q_free, 1)

            def q_hi_parts(g):
                for h in (1, 0):
                    if h:
                        act.wait_ge(q_free, 2 + KD * (g + 1))
                    else:
                        act.wait_ge(q_rotated, g + 1)
                    s = slice(2 * h, 2 * h + 2)
                    act.activation(q_hi[:, s, :], qb[:, s, :], ACT.Copy).then_inc(q_hi_done, 1)

            def first_norm(g, u):
                act.wait_ge(nm_ready, g + 1)
                act.wait_ge(y_free, 2 + GT * g)
                for j in range(GT):
                    act.activation(n1[:, j, :], xg[u][:, j, :], ACT.Identity, bias=nm[u][:, j:j + 1],
                                   scale=rs[u][:, 1, j:j + 1]).then_inc(n1_raw, 1)

            def norm_z(g):
                act.wait_ge(znm_ready, g + 1)
                for j in range(GT):
                    act.activation(z[:, j, :], z[:, j, :], ACT.Identity, bias=znm[:, j:j + 1],
                                   scale=zr[:, j:j + 1]).then_inc(zn_ready, 1)

            def norm_x2(g):
                act.wait_ge(xnm_ready, g + 1)
                act.wait_ge(n3_stored, 16 * (g + 1))
                for j in range(GT):
                    act.activation(n3[:, j, :], z[:, j, :], ACT.Identity, bias=xnm[:, j:j + 1],
                                   scale=xr[:, j:j + 1]).then_inc(n3_ready, 1)

            def n3_columns(g, n0):
                for k in range(KD):
                    act.wait_ge(tp_full, n0 + k + 1)
                    act.activation(n3t[:, k, :], tp[k % 2][:, :], ACT.Copy).then_inc(tp_free, 1)

            for n in range(N_KV, N_Q):
                hi_part(n)
            act.wait_ge(a_over, 4)
            first_norm(0, 0)
            bias_q(0)
            q_hi_parts(0)
            for n in range(N_Q, N_ALL):
                hi_part(n)

            TB = KD * (NG + 1)

            def group(g, u, last):
                if not last:
                    front_split(NG + g + 1, 1 - u, TB + 2 * KD * g, (q_full, KD * g + 1))
                norm_z(g)
                if not last:
                    bias_q(g + 1)
                norm_x2(g)
                if not last:
                    q_hi_parts(g + 1)
                    first_norm(g + 1, 1 - u)
                n3_columns(g, TB + 2 * KD * g + (0 if last else KD))

            with act.Fori(0, NG // 2 - 1) as i:
                for u in range(2):
                    group(2 * i + u, u, False)
            for u in range(2):
                group(NG - 2 + u, u, u == 1)

        @block.gpsimd
        def _(pool):
            def rsqrt(dst, src, n, ready):
                pool.tensor_tensor(dst, src, n, ALU.pow).then_inc(ready, 1)

            def front_rs(f, u):
                pool.wait_ge(var_ready, f + 1)
                pool.tensor_tensor(rs[u][:, :, :], vp[:, :, :], half[:, 0:2 * GT].rearrange("p (c t) -> p c t", c=2),
                                   ALU.pow).then_inc(rs_ready, 1)

            def front_lo(f, u):
                for k in range(KD):
                    pool.wait_ge(h_hi_done, KD * f + k + 1)
                    pool.tensor_tensor(h_lo[u][:, k, :], hb[k % 2][:, :], h_hi[u][:, k, :].bitcast(F32), ALU.subtract)\
                        .then_inc(h_split, 1)

            for b in range(B):
                pool.memset(acc[:, b, :], 0.0).then_inc(acc_done, 1)
            pool.sem_inc(x2_stored, 16)
            pool.sem_inc(n3_stored, 16)
            pool.wait_ge(half_set, 1)
            front_rs(0, 0)
            front_lo(0, 0)

            def rnorm(g, j):
                pool.wait_ge(ssq_ready, GT * g + j + 1)
                pool.tensor_tensor(rn[j % 2][:, :], ssq[j % 2][:, :], half[:, 0:1], ALU.pow).then_inc(rn_ready, 1)

            def accumulate(g, j):
                t = GT * g + j
                pool.wait_ge(prod_ready, 2 + t + 1)
                need = value(pool, B + t)
                offset = value(pool, g // GB)
                a = acc[:, bass.ds(offset, 1), :]
                pool.wait_ge(half_set, 1)
                pool.wait_ge(acc_done, need)
                pool.tensor_tensor(a, a, prod[j % 2][:, :].rearrange("p (o d) -> p o d", o=1), ALU.add)\
                    .then_inc(acc_done, 1)

            with pool.Fori(0, NG // 2) as i:
                for u in range(2):
                    g = 2 * i + u
                    front_rs(g + 1, 1 - u)
                    rnorm(g, 0)
                    rnorm(g, 1)
                    accumulate(g, 0)
                    rnorm(g, 2)
                    accumulate(g, 1)
                    front_lo(g + 1, 1 - u)
                    rnorm(g, 3)
                    accumulate(g, 2)
                    accumulate(g, 3)
            pool.wait_ge(acc_done, B + NT)
            pool.sem_inc(a_over, 1)
            pool.wait_ge(a_over, 4)

            def q_times_sin(g, u):
                pool.wait_ge(rf_in[u], 16 * (g // 2 + 1))
                pool.wait_ge(q_biased, 2 + KD * g + 2)
                if not isinstance(g, int) or g > 0:
                    pool.wait_ge(q_rotated, g)
                pool.tensor_tensor(rsn[:, :, :], qb[:, 0:2, :], rf[u][:, 1:2, :].to_broadcast([P, 2, G]), ALU.mult)\
                    .then_inc(q_sin, 1)

            def add_b_out(g):
                for j in range(GT):
                    pool.wait_ge(n1_raw, GT * g + j + 1)
                    pool.tensor_tensor(n1[:, j, :], n1[:, j, :], bo[:, :], ALU.add).then_inc(n1_ready, 1)

            def token_rsqrt(dst, src, need, ready, g):
                pool.wait_ge(need, g + 1)
                pool.tensor_tensor(dst[:, :], src[:, :], half[:, 0:GT], ALU.pow).then_inc(ready, 1)

            q_times_sin(0, 0)
            add_b_out(0)

            def group(g, u, last):
                if not last:
                    front_rs(NG + g + 1, 1 - u)
                    front_lo(NG + g + 1, 1 - u)
                token_rsqrt(zr, zv, zv_ready, zr_ready, g)
                if not last:
                    q_times_sin(g + 1, 1 - u)
                token_rsqrt(xr, xv, xv_ready, xr_ready, g)
                if not last:
                    add_b_out(g + 1)

            with pool.Fori(0, NG // 2 - 1) as i:
                for u in range(2):
                    group(2 * i + u, u, False)
            for u in range(2):
                group(NG - 2 + u, u, u == 1)

        @block.tensor
        def _(pe):
            def transposes(src, n0, free_from):
                for k in range(KD):
                    pe.wait_ge(tp_free, n0 + k + 1)
                    for j in range(GT):
                        last = pe.transpose(tp[k % 2][:, j * P:(j + 1) * P], src[:, j, k * P:(k + 1) * P], ident[:, :])
                    last.then_inc(tp_full, 1)

            def product(dst, hi, lo, w_hi, w_lo):
                for k in range(KD):
                    pe.matmul(dst, hi(k), w_hi(k), start=(k == 0), stop=False)
                    pe.matmul(dst, hi(k), w_lo(k), start=False, stop=False)
                    last = pe.matmul(dst, lo(k), w_hi(k), start=False, stop=(k == KD - 1))
                return last

            pe.wait_ge(consts_in, 16 * 7)
            pe.wait_ge(h_normed, 1)
            transposes(hn, 0, 0)

            def kv(g, u, j, c, first):
                n = 2 * (GT * g + j) + c
                s = slice(j * P, (j + 1) * P)
                pe.wait_ge(kv_free, n + 1)
                product(mm[(2 * j + c) % NB_A][:, :], lambda k: h_hi[u][:, k, s], lambda k: h_lo[u][:, k, s],
                        lambda k: wkv_hi[:, c, k, :], lambda k: wkv_lo[:, c, k, :]).then_inc(kv_full, 1)

            pe.wait_ge(w_split, N_KV)
            with pe.Fori(0, NG // 2) as i:
                for u in range(2):
                    g = 2 * i + u
                    pe.wait_ge(h_split, KD * (g + 1))
                    for j in range(GT):
                        if j == 3:
                            pe.wait_ge(h_normed, g + 2)
                            transposes(hn, KD * (g + 1), 0)
                        kv(g, u, j, 0, j == 0)
                        kv(g, u, j, 1, False)
            pe.sem_inc(a_over, 1)

            pe.wait_ge(ones_set, 1)
            pe.wait_ge(acc_done, B + NT)
            for b in range(B):
                for k in range(KD):
                    n = b * KD + k
                    last = pe.matmul(acol_ps[:, n:n + 1], acc[:, b, k * P:(k + 1) * P], ones[:, :],
                                     start=True, stop=True)
            last.then_inc(acol_full, 1)

            def q(g, u):
                for m in range(KD):
                    pe.wait_ge(q_free, KD * g + m + 1)
                    if m == 0:
                        pe.wait_ge(h_split, KD * (NG + g + 1))
                    s = slice(m * P, (m + 1) * P)
                    product(mm[m % 2][:, :], lambda k: wq_hi[:, k, s], lambda k: wq_lo[:, k, s],
                            lambda k: h_hi[u][:, k, :], lambda k: h_lo[u][:, k, :]).then_inc(q_full, 1)

            def y(g, u):
                pe.wait_ge(q_split, 2 * (g + 1))
                for j in range(GT):
                    pe.wait_ge(y_free, GT * g + j + 1)
                    s = slice(j * P, (j + 1) * P)
                    b = g // GB
                    w = lambda t, k: t[:, bass.ds(b, 1), k, :].rearrange("p o d -> p (o d)")
                    product(mm[2 + j % 2][:, :], lambda k: q_hi[:, k, s], lambda k: q_lo[:, k, s],
                            lambda k: w(wo_hi, k), lambda k: w(wo_lo, k)).then_inc(y_full, 1)

            def gate(g, n0):
                pe.wait_ge(n3_ready, GT * (g + 1))
                transposes(n3, n0, 0)
                pe.wait_ge(tp_free, 2 + n0 + KD)
                if not isinstance(g, int) or g > 0:
                    pe.wait_ge(lg_ready, g)
                for j in range(GT):
                    for k in range(KD):
                        last = pe.matmul(gl[:, j * E:(j + 1) * E], n3t[:, k, j * P:(j + 1) * P], gw[:, k, :],
                                         start=(k == 0), stop=(k == KD - 1))
                last.then_inc(gl_full, 1)

            pe.wait_ge(w_split, N_Q)
            q(0, 0)
            pe.wait_ge(w_split, N_ALL)
            TB = KD * (NG + 1)

            def group(g, u, last):
                y(g, u)
                n0 = TB + 2 * KD * g
                if not last:
                    pe.wait_ge(h_normed, NG + g + 2)
                    transposes(hn, n0, 0)
                    q(g + 1, 1 - u)
                    n0 = n0 + KD
                gate(g, n0)

            with pe.Fori(0, NG // 2 - 1) as i:
                for u in range(2):
                    group(2 * i + u, u, False)
            for u in range(2):
                group(NG - 2 + u, u, u == 1)


def ffn(nc, v):
    (D, E, H, SH, KD, GT, G, NG, NT) = (v[n] for n in "D E H SH KD GT G NG NT".split())
    ident, tops, top_at = v["ident"], v["tops"], v["top_at"]
    x2_groups, n3_groups, out_groups, col = v["x2_groups"], v["n3_groups"], v["out_groups"], v["col"]
    with ExitStack() as ctx:
        def sb(name, shape, dt=F32):
            return ctx.enter_context(nc.sbuf_tensor(name, shape, dt))

        def sem(name):
            return ctx.enter_context(nc.semaphore(name))

        ps = [ctx.enter_context(nc.psum_tensor(f"c_ps{i}", [P, 512], F32)) for i in range(8)]
        w1s, w2s = sb("w1s", [P, E, KD, H]), sb("w2s", [P, E, H // P, D])
        s1s, s2s = sb("s1s", [P, KD, SH]), sb("s2s", [P, SH // P, D])
        b1s, sb1s = sb("b1s", [P, E, H // P]), sb("sb1s", [P, SH // P])
        b2s, sb2s, one = sb("b2s", [1, E, D]), sb("sb2s", [1, D]), sb("one", [1, P])
        n3 = sb("c_n3", [P, GT, D])
        n3t = sb("c_n3t", [P, KD, G])
        x2 = sb("c_x2", [P, GT, D])
        h = sb("c_h", [P, 4, G])
        acc = sb("c_acc", [P, GT, D])
        st, mv, va, r, nm = (sb("c_st", [P, GT, 6]), sb("c_mv", [P, GT, 2]), sb("c_va", [P, GT]), sb("c_r", [P, GT]),
                             sb("c_nm", [P, GT]))
        at_f = sb("at_f", [P, NT, 2])
        iota = sb("c_iota", [P, E])
        M1, M2 = sb("M1", [P, NT, E]), sb("M2", [P, NT, E])
        g1, g2, gd = sb("g1", [P, NT]), sb("g2", [P, NT]), sb("gd", [P, NT])
        gates = sb("gates", [P, NT, E])
        half = sb("c_half", [P, GT])

        w_in, n_in, x_in, o_out = sem("c_w_in"), sem("c_n_in"), sem("c_x_in"), sem("c_out")
        dv, pl, ac = sem("c_dv"), sem("c_pl"), sem("c_ac")
        r1, r2, r3, r4 = sem("c_r1"), sem("c_r2"), sem("c_r3"), sem("c_r4")
        t_full, t_free = sem("c_t_full"), sem("c_t_free")
        h_full, h_done, o_full, o_free = sem("c_h_full"), sem("c_h_done"), sem("c_o_full"), sem("c_o_free")
        c_st, c_mv, c_va, c_r, c_nm, c_o, c_nrm = (sem("cs_st"), sem("cs_mv"), sem("cs_va"), sem("cs_r"), sem("cs_nm"),
                                                   sem("cs_o"), sem("cs_nrm"))
        block = ctx.enter_context(nc.Block())
        NW = 9
        J = E + 1

        @block.sync
        def _(sp):
            for ap, src in ((w1s[:, :, :, :], v["w1"].rearrange("e (k p) h -> p e k h", p=P)),
                            (w2s[:, :, :, :], v["w2"].rearrange("e (k p) h -> p e k h", p=P)),
                            (s1s[:, :, :], v["sw1"].rearrange("(k p) h -> p k h", p=P)),
                            (s2s[:, :, :], v["sw2"].rearrange("(k p) h -> p k h", p=P)),
                            (b1s[:, :, :], v["b1"]),
                            (sb1s[:, :], v["sb1"]),
                            (b2s[:, :, :], v["b2"].rearrange("(o e) d -> o e d", o=1)),
                            (sb2s[:, :], v["sb2"].rearrange("(o d) -> o d", o=1)),
                            (n3[:, :, :], n3_groups[0])):
                sp.dma_start(ap, src).then_inc(w_in, 16)
            sp.wait_ge(w_in, 16 * NW)
            with sp.Fori(0, NG) as g:
                sp.wait_ge(c_o, g + 1)
                sp.dma_start(n3[:, :, :], n3_groups[g]).then_inc(n_in, 16)
                sp.dma_start(x2[:, :, :], x2_groups[g]).then_inc(x_in, 16)
                sp.wait_ge(c_nrm, g + 1)
                sp.dma_start(out_groups[g], acc[:, :, :]).then_inc(o_out, 16)
            sp.wait_ge(o_out, 16 * NG)

        @block.vector
        def _(dve):
            dve.sem_inc(c_o, 1)
            n = [0]

            def step(ins):
                n[0] += 1
                ins.then_inc(dv, 1)
                dve.wait_ge(dv, n[0])

            dve.memset(one[:, :], 1.0)
            step(dve.memset(half[:, :], -0.5))
            dve.sem_inc(pl, 1)
            step(dve.tensor_copy(at_f[:, :, :], top_at[:, :, 0:2]))
            dve.wait_ge(r1, 1)
            for M, c in ((M1, 0), (M2, 1)):
                step(dve.tensor_tensor(M[:, :, :], iota[:, :].rearrange("p (o e) -> p o e", o=1).to_broadcast([P, NT, E]),
                                       at_f[:, :, c:c + 1].to_broadcast([P, NT, E]), ALU.is_equal))
            dve.tensor_tensor(gd[:, :], tops[:, :, 1], tops[:, :, 0], ALU.subtract).then_inc(r2, 1)
            dve.wait_ge(r3, 1)
            step(dve.tensor_scalar(g2[:, :], gd[:, :], 1.0, None, ALU.add))
            step(dve.reciprocal(g1[:, :], g2[:, :]))
            step(dve.tensor_tensor(g2[:, :], gd[:, :], g1[:, :], ALU.mult))
            step(dve.tensor_tensor(M1[:, :, :], M1[:, :, :], g1[:, :].rearrange("p (t o) -> p t o", o=1).to_broadcast([P, NT, E]), ALU.mult))
            step(dve.tensor_tensor(M2[:, :, :], M2[:, :, :], g2[:, :].rearrange("p (t o) -> p t o", o=1).to_broadcast([P, NT, E]), ALU.mult))
            step(dve.tensor_tensor(gates[:, :, :], M1[:, :, :], M2[:, :, :], ALU.add))
            k0 = n[0]
            with dve.Fori(0, NG) as g:
                for e in range(J):
                    for j in range(GT):
                        dve.wait_ge(o_full, GT * (J * g + e) + j + 1)
                        if e == 0:
                            last = dve.tensor_copy(acc[:, j, :], ps[4 + j][:, :])
                        else:
                            last = dve.scalar_tensor_tensor(acc[:, j, :], ps[4 + j][:, :],
                                                            gates[:, bass.ds(GT * g + j, 1), e - 1], acc[:, j, :],
                                                            ALU.mult, ALU.add)
                        last.then_inc(o_free, 1)
                    dve.wait_ge(o_free, GT * (J * g + e + 1) + GT)
                for j in range(GT):
                    last = dve.bn_stats(st[:, j, :], acc[:, j, :])
                last.then_inc(c_st, 1)
                need = value(dve, g + 1)
                dve.wait_ge(dv, 1)
                dve.wait_ge(c_st, need)
                for j in range(GT):
                    last = dve.bn_aggr(mv[:, j, :], st[:, j, :])
                last.then_inc(c_mv, 1)
                dve.wait_ge(c_mv, g + 1)
                dve.tensor_scalar(va[:, :], mv[:, :, 1], EPS, None, ALU.add).then_inc(c_va, 1)
                dve.wait_ge(c_r, g + 1)
                for j in range(GT):
                    last = dve.tensor_scalar(acc[:, j, :], acc[:, j, :], mv[:, j, 0:1], r[:, j:j + 1], ALU.subtract, ALU.mult)
                last.then_inc(c_nm, 1)
                dve.wait_ge(c_nm, g + 1)
                dve.wait_ge(x_in, 16 * (g + 1))
                dve.tensor_tensor(acc[:, :, :], acc[:, :, :], x2[:, :, :], ALU.add).then_inc(c_nrm, 1)
                dve.wait_ge(o_out, 16 * (g + 1))
                dve.sem_inc(c_o, 1)

        @block.gpsimd
        def _(pool):
            pool.iota(iota[:, :], [[1, E]], base=0, channel_multiplier=0, allow_small_or_imprecise_dtypes=True).then_inc(r1, 1)
            pool.wait_ge(dv, 1)
            with pool.Fori(0, NG) as g:
                pool.wait_ge(c_va, g + 1)
                pool.tensor_tensor(r[:, :], va[:, :], half[:, :], ALU.pow).then_inc(c_r, 1)

        @block.scalar
        def _(act):
            act.wait_ge(r2, 1)
            act.activation(gd[:, :], gd[:, :], ACT.Exp).then_inc(r3, 1)
            act.wait_ge(w_in, 16 * NW)
            act.sem_inc(t_free, 2)
            act.sem_inc(o_free, GT)
            with act.Fori(0, NG) as g:
                for k in range(KD):
                    act.wait_ge(t_full, KD * g + k + 1)
                    act.activation(n3t[:, k, :], ps[k % 2][:, :], ACT.Copy).then_inc(t_free, 1)
                for e in range(J):
                    M = SH // P if e == 0 else H // P
                    for m in range(M):
                        c = (0 if e == 0 else SH // P + (e - 1) * (H // P)) + m
                        tot = SH // P + E * (H // P)
                        act.wait_ge(h_full, tot * g + c + 1)
                        b = sb1s[:, m:m + 1] if e == 0 else b1s[:, e - 1, m:m + 1]
                        act.activation(h[:, m if e == 0 else (m + 2 * (e % 2)), :], ps[2 + c % 2][:, :], ACT.Gelu, bias=b).then_inc(h_done, 1)

        @block.tensor
        def _(pe):
            pe.wait_ge(w_in, 16 * NW)
            pe.wait_ge(dv, 1)
            pe.sem_inc(h_done, 2)
            tot = SH // P + E * (H // P)
            with pe.Fori(0, NG) as g:
                pe.wait_ge(n_in, 16 * (g + 1))
                for k in range(KD):
                    pe.wait_ge(t_free, KD * g + k + 1)
                    for j in range(GT):
                        last = pe.transpose(ps[k % 2][:, j * P:(j + 1) * P], n3[:, j, k * P:(k + 1) * P], ident[:, :])
                    last.then_inc(t_full, 1)
                pe.wait_ge(t_free, KD * g + KD + 2)
                for e in range(J):
                    M = SH // P if e == 0 else H // P
                    for m in range(M):
                        c = (0 if e == 0 else SH // P + (e - 1) * (H // P)) + m
                        pe.wait_ge(h_done, tot * g + c + 1)
                        for k in range(KD):
                            w = s1s[:, k, m * P:(m + 1) * P] if e == 0 else w1s[:, e - 1, k, m * P:(m + 1) * P]
                            last = pe.matmul(ps[2 + c % 2][:, :], w, n3t[:, k, :], start=(k == 0), stop=(k == KD - 1))
                        last.then_inc(h_full, 1)
                    pe.wait_ge(h_done, tot * g + c + 1 + 2)
                    for j in range(GT):
                        pe.wait_ge(o_free, GT * (J * g + e) + j + 1)
                        for m in range(M):
                            hh = h[:, m if e == 0 else (m + 2 * (e % 2)), j * P:(j + 1) * P]
                            w = s2s[:, m, :] if e == 0 else w2s[:, e - 1, m, :]
                            pe.matmul(ps[4 + j][:, :], hh, w, start=(m == 0), stop=False)
                        w = sb2s[:, :] if e == 0 else b2s[:, e - 1, :]
                        pe.matmul(ps[4 + j][:, :], one[:, :], w, start=False, stop=True).then_inc(o_full, 1)


_NAMES = ["X", "ln_w", "ln_b", "W_in", "b_in", "W_out", "b_out"]
_FFN = ["gate_w", "w1", "b1", "w2", "b2", "shared_w1", "shared_b1", "shared_w2", "shared_b2"]


def _pairs_apart(n):
    return np.concatenate([np.arange(0, n // 2, 2), np.arange(1, n // 2, 2), np.arange(n // 2, n)])


def _angles(seq, n):
    rot = n // 2
    inv = (1.0 / np.float64(THETA) ** (np.arange(0, rot, 2) / rot)).astype(np.float32)
    a = np.arange(seq, dtype=np.float32)[:, None] * inv[None, :]
    return np.cos(a).astype(np.float32), np.sin(a).astype(np.float32)


def _columns(x):
    return np.moveaxis(x.reshape(*x.shape[:-1], -1, P), -1, 0)


def kernel(**inputs):
    import concourse.bacc as _bacc
    from concourse.bass_utils import run_bass_kernel_spmd as _run

    nc = _bacc.Bacc("TRN2", target_bir_lowering=False, num_devices=1)
    a = {k: np.asarray(x) for k, x in inputs.items()}
    Bn, S, D = a["L0_attn_X"].shape
    order = _pairs_apart(D)
    cols = np.concatenate([order + c * D for c in range(3)])
    host = {n: a[f"L0_attn_{n}"] for n in _NAMES}
    host["W_in"] = host["W_in"][:, cols]
    host["b_in"] = host["b_in"][cols]
    host["W_out"] = host["W_out"][order, :]
    host.update({n: a[f"L0_ffn_{n}"] for n in _FFN})
    for n in ("ln_w", "ln_b", "shared_b1", "b1"):
        host[n] = _columns(host[n])
    host["b_q"] = _columns(host["b_in"][:D])
    cos, sin = _angles(S, D)
    host["rope_tok"] = np.concatenate([cos, sin], axis=1)
    host["rope_feat"] = np.stack([cos.T, sin.T])
    host["identity"] = np.eye(P, dtype=np.float32)
    arrays, args = {}, []
    for name, x in host.items():
        x = np.ascontiguousarray(x)
        arrays[f"in_{name}"] = x
        args.append(nc.dram_tensor(f"in_{name}", x.shape, mybir.dt.from_np(x.dtype), kind="ExternalInput").ap())
    out = nc.dram_tensor("out_0", (Bn, S, D), F32, kind="ExternalOutput").ap()
    sandwich_kernel(nc, *args, out)
    r = _run(nc, [arrays], core_ids=[0])
    return r.results[0]["out_0"]
```

```python
from contextlib import ExitStack

import numpy as np

import concourse.bass as bass
from concourse import mybir

P = 128
F32 = mybir.dt.float32
F32R = mybir.dt.float32r
U32 = mybir.dt.uint32
I32 = mybir.dt.int32
AX = mybir.AxisListType
ALU = mybir.AluOpType
ACT = mybir.ActivationFunctionType
EPS = 1e-5
THETA = 10000.0


def sandwich_kernel(nc, X, ln_w, ln_b, W_in, b_in, W_out, b_out, gate_w, w1, b1, w2, b2,
                    sw1, sb1, sw2, sb2, b_q, rope_tok, rope_feat, identity, before, bias_parts,
                    out):
    B, S, D = X.shape
    E, _, H = w1.shape
    SH = sw1.shape[1]
    N = B * S
    KD = D // P
    GT = 4
    G = GT * P
    NG = N // G
    GB = NG // B
    NT = N // P
    R = P
    assert D == 4 * P and G == 512 and NG % 2 == 0 and GB % 2 == 0

    def grouped(ap):
        return ap.rearrange("(g t p) d -> g p t d", p=P, t=GT)

    x_groups = grouped(X.rearrange("b s d -> (b s) d"))
    out_groups = grouped(out.rearrange("b s d -> (b s) d"))
    x2_dram = nc.dram_tensor("x2_scratch", (N, D), F32, kind="Internal").ap()
    n3_dram = nc.dram_tensor("n3_scratch", (N, D), F32, kind="Internal").ap()
    KH = H // P
    NRT = 2 * NT + E
    r_dram = nc.dram_tensor("routed_scratch", ((NRT - 1) * P, D), F32, kind="Internal").ap()
    x2_groups, n3_groups = grouped(x2_dram), grouped(n3_dram)
    tok_groups = grouped(rope_tok)
    feat_groups = rope_feat.rearrange("c p (g t) -> g p c t", t=G)

    def col(ap):
        return ap.rearrange("(k p) -> p k", p=P)

    top = ExitStack()
    with top:
        def keep(name, shape, dt=F32):
            return top.enter_context(nc.sbuf_tensor(name, shape, dt))

        ident = keep("ident", [P, P])
        tops = keep("tops", [P, NT, 8])
        top_at = keep("top_at", [P, NT, 8], U32)

        attention(nc, locals())
        slots = keep("slots", [P, 2, NT], U32)
        picked = keep("picked", [P, 2, NT])
        gsrc = keep("gsrc", [P, NT, 32])
        gate_hi = keep("gate_hi", [P, NT, E], F32R)
        b2_mix = keep("b2_mix", [32, D], F32R)
        routed(nc, locals())
        combined(nc, locals())


def value(eng, x):
    return x if isinstance(x, int) else eng.snap(eng.to_reg(x))


def attention(nc, v):
    (B, S, D, E, KD, GT, G, NG, GB, NT, R) = (v[n] for n in "B S D E KD GT G NG GB NT R".split())
    x_groups, x2_groups, n3_groups = v["x_groups"], v["x2_groups"], v["n3_groups"]
    tok_groups, feat_groups, col = v["tok_groups"], v["feat_groups"], v["col"]
    ident, tops, top_at = v["ident"], v["tops"], v["top_at"]
    W_in, W_out, b_in = v["W_in"], v["W_out"], v["b_in"]

    with ExitStack() as ctx:
        def sb(name, shape, dt=F32, where=ctx):
            return where.enter_context(nc.sbuf_tensor(name, shape, dt))

        def sem(name):
            return ctx.enter_context(nc.semaphore(name))

        def bank(name):
            return ctx.enter_context(nc.psum_tensor(name, [P, 512], F32))

        mm = [bank(f"mm{i}") for i in range(4)]
        tp = [bank(f"tp{i}") for i in range(2)]
        gl = bank("gl")
        acol_ps = bank("acol_ps")

        wq_hi, wq_lo = sb("wq_hi", [P, KD, D], F32R), sb("wq_lo", [P, KD, D], F32R)
        wo_hi, wo_lo = sb("wo_hi", [P, B, KD, D], F32R), sb("wo_lo", [P, B, KD, D], F32R)
        gw = sb("gw", [P, KD, E])
        NSTAGE = 3
        stage = [sb(f"stage{i}", [P, D]) for i in range(NSTAGE)]
        lnw, lnb, bq = sb("lnw", [P, KD]), sb("lnb", [P, KD]), sb("bq", [P, KD])
        bkv, bo = sb("bkv", [P, 2, D]), sb("bo", [P, D])
        half = sb("half", [P, 8])
        ones = sb("ones", [P, 1])
        acc = sb("acc", [P, B, D])
        acol = sb("acol", [P, B, KD])

        xg = [sb(f"xg{i}", [P, GT, D]) for i in range(2)]
        hn = sb("hn", [P, GT, D])
        bst = sb("bst", [P, GT, 6])
        mv = [sb(f"mv{i}", [P, GT, 2]) for i in range(2)]
        vp = sb("vp", [P, 2, GT])
        rs = [sb(f"rs{i}", [P, 2, GT]) for i in range(2)]
        nm = [sb(f"nm{i}", [P, GT]) for i in range(2)]
        hb = [sb(f"hb{i}", [P, G]) for i in range(2)]
        h_hi = [sb(f"h_hi{i}", [P, KD, G], F32R) for i in range(2)]
        h_lo = [sb(f"h_lo{i}", [P, KD, G], F32R) for i in range(2)]

        with ExitStack() as first:
            wkv_hi = sb("wkv_hi", [P, 2, KD, D], F32R, first)
            wkv_lo = sb("wkv_lo", [P, 2, KD, D], F32R, first)
            rt = [sb(f"rt{i}", [P, GT, 2, R], where=first) for i in range(2)]
            kb = [sb(f"kb{i}", [P, D], where=first) for i in range(2)]
            vb = [sb(f"vb{i}", [P, D], where=first) for i in range(2)]
            sq = [sb(f"sq{i}", [P, D], where=first) for i in range(2)]
            ssq = [sb(f"ssq{i}", [P, 1], where=first) for i in range(2)]
            rn = [sb(f"rn{i}", [P, 1], where=first) for i in range(2)]
            rot = sb("rot", [P, 2, 2, R], where=first)
            prod = [sb(f"prod{i}", [P, D], where=first) for i in range(2)]
        rf = [sb(f"rf{i}", [P, 2, G]) for i in range(2)]
        qb = sb("qb", [P, KD, G])
        rc, rsn = sb("rc", [P, 2, G]), sb("rsn", [P, 2, G])
        q_hi, q_lo = sb("q_hi", [P, KD, G], F32R), sb("q_lo", [P, KD, G], F32R)
        n1 = sb("n1", [P, GT, D])
        z = sb("z", [P, GT, D])
        n3 = sb("n3", [P, GT, D])
        n3t = sb("n3t", [P, KD, G])
        zst, zmv = sb("zst", [P, GT, 6]), sb("zmv", [P, GT, 2])
        zv, zr, znm = sb("zv", [P, GT]), sb("zr", [P, GT]), sb("znm", [P, GT])
        xst, xmv = sb("xst", [P, GT, 6]), sb("xmv", [P, GT, 2])
        xv, xr, xnm = sb("xv", [P, GT]), sb("xr", [P, GT]), sb("xnm", [P, GT])
        lg = sb("lg", [P, GT, E])
        mx, mi = sb("mx", [P, GT, 8]), sb("mi", [P, GT, 8], U32)

        consts_in = sem("consts_in")
        half_set, ones_set = sem("half_set"), sem("ones_set")
        x_in = [sem(f"x_in{i}") for i in range(2)]
        rt_in = [sem(f"rt_in{i}") for i in range(2)]
        rf_in = [sem(f"rf_in{i}") for i in range(2)]
        raw_in = [sem(f"raw_in{i}") for i in range(NSTAGE)]
        w_hi_done, w_split = sem("w_hi_done"), sem("w_split")
        stats_done, aggr_done, var_ready, rs_ready = sem("stats_done"), sem("aggr_done"), sem("var_ready"), sem("rs_ready")
        nm_ready, h_normed = sem("nm_ready"), sem("h_normed")
        tp_full, tp_free = sem("tp_full"), sem("tp_free")
        h_hi_done, h_split = sem("h_hi_done"), sem("h_split")
        kv_full, kv_free = sem("kv_full"), sem("kv_free")
        k_parts, k_rotated = sem("k_parts"), sem("k_rotated")
        v_biased = sem("v_biased")
        ssq_ready, rn_ready = sem("ssq_ready"), sem("rn_ready")
        prod_ready, acc_done = sem("prod_ready"), sem("acc_done")
        acol_full, acol_ready = sem("acol_full"), sem("acol_ready")
        a_over = sem("a_over")
        q_full, q_free = sem("q_full"), sem("q_free")
        q_biased = q_free
        q_cos, q_sin, q_rotated = sem("q_cos"), sem("q_sin"), sem("q_rotated")
        q_hi_done, q_split = sem("q_hi_done"), sem("q_split")
        n1_raw, n1_ready = sem("n1_raw"), sem("n1_ready")
        y_full, y_free = sem("y_full"), sem("y_free")
        zst_done, zmv_done, zv_ready, zr_ready, znm_ready, zn_ready = (
            sem("zst_done"), sem("zmv_done"), sem("zv_ready"), sem("zr_ready"), sem("znm_ready"), sem("zn_ready"))
        x2_ready, xst_done, xmv_done, xv_ready, xr_ready, xnm_ready, n3_ready = (
            sem("x2_ready"), sem("xst_done"), sem("xmv_done"), sem("xv_ready"), sem("xr_ready"), sem("xnm_ready"),
            sem("n3_ready"))
        x2_stored, n3_stored = sem("x2_stored"), sem("n3_stored")
        n3t_ready, gl_full, lg_ready, mx_ready, mi_ready, tops_kept = (
            sem("n3t_ready"), sem("gl_full"), sem("lg_ready"), sem("mx_ready"), sem("mi_ready"), sem("tops_kept"))

        chunks = [(W_in[k * P:(k + 1) * P, (1 + c) * D:(2 + c) * D], wkv_hi[:, c, k, :], wkv_lo[:, c, k, :], None)
                  for c in range(2) for k in range(KD)]
        N_KV = len(chunks)
        chunks += [(W_in[k * P:(k + 1) * P, 0:D], wq_hi[:, k, :], wq_lo[:, k, :], None) for k in range(KD)]
        N_Q = len(chunks)
        chunks += [(W_out[k * P:(k + 1) * P, :], wo_hi[:, b, k, :], wo_lo[:, b, k, :], (b, k))
                   for b in range(B) for k in range(KD)]
        N_ALL = len(chunks)
        NB_A = 4

        block = ctx.enter_context(nc.Block())

        @block.sync
        def _(sp):
            def load_chunk(n):
                if n >= NSTAGE:
                    sp.wait_ge(w_split, n - NSTAGE + 1)
                sp.dma_start(stage[n % NSTAGE][:, :], chunks[n][0]).then_inc(raw_in[n % NSTAGE], 16)

            sp.dma_start(xg[0][:, :, :], x_groups[0]).then_inc(x_in[0], 16)
            sp.dma_start(ident[:, :], v["identity"]).then_inc(consts_in, 16)
            sp.dma_start(lnw[:, :], v["ln_w"]).then_inc(consts_in, 16)
            sp.dma_start(lnb[:, :], v["ln_b"]).then_inc(consts_in, 16)
            for n in range(NSTAGE):
                load_chunk(n)
            sp.dma_start(bq[:, :], v["b_q"]).then_inc(consts_in, 16)
            sp.dma_start(bkv[:, :, :], b_in[D:3 * D].rearrange("(c d) -> c d", c=2).partition_broadcast(P))\
              .then_inc(consts_in, 16)
            sp.dma_start(bo[:, :], v["b_out"].partition_broadcast(P)).then_inc(consts_in, 16)
            sp.dma_start(gw[:, :, :], v["gate_w"].rearrange("(k p) e -> p k e", p=P)).then_inc(consts_in, 16)
            sp.dma_start(rt[0][:, :, :, :], tok_groups[0].rearrange("p t (c r) -> p t c r", c=2)).then_inc(rt_in[0], 16)
            for n in range(NSTAGE, N_KV):
                load_chunk(n)
            sp.dma_start(xg[1][:, :, :], x_groups[1]).then_inc(x_in[1], 16)
            sp.dma_start(rt[1][:, :, :, :], tok_groups[1 % GB].rearrange("p t (c r) -> p t c r", c=2))\
              .then_inc(rt_in[1], 16)
            with sp.Fori(1, NG // 2) as i:
                for u in range(2):
                    g = 2 * i + u
                    sp.wait_ge(h_normed, g - 1)
                    sp.dma_start(xg[u][:, :, :], x_groups[g]).then_inc(x_in[u], 16)
                    sp.wait_ge(k_rotated, GT * (g - 1))
                    sp.dma_start(rt[u][:, :, :, :], tok_groups[g % GB].rearrange("p t (c r) -> p t c r", c=2))\
                      .then_inc(rt_in[u], 16)
            for u in range(2):
                sp.wait_ge(h_normed, NG - 1 + u)
                sp.dma_start(xg[u][:, :, :], x_groups[u]).then_inc(x_in[u], 16)
            for n in range(N_KV, N_Q):
                load_chunk(n)
            sp.wait_ge(a_over, 4)
            for u in range(2):
                sp.dma_start(rf[u][:, :, :], feat_groups[u]).then_inc(rf_in[u], 16)
            for n in range(N_Q, N_ALL):
                load_chunk(n)

            def stores(g, u):
                sp.wait_ge(x2_ready, GT * (g + 1))
                sp.dma_start(x2_groups[g], z[:, :, :]).then_inc(x2_stored, 16)

            def store_n3(g):
                sp.wait_ge(n3_ready, GT * (g + 1))
                sp.dma_start(n3_groups[g], n3[:, :, :]).then_inc(n3_stored, 16)

            with sp.Fori(0, NG // 2 - 1) as i:
                for u in range(2):
                    g = 2 * i + u
                    stores(g, u)
                    sp.dma_start(xg[u][:, :, :], x_groups[g + 2]).then_inc(x_in[u], 16)
                    sp.wait_ge(q_sin, g + 1)
                    sp.wait_ge(q_cos, g + 1)
                    sp.dma_start(rf[u][:, :, :], feat_groups[(g + 2) % GB]).then_inc(rf_in[u], 16)
                    store_n3(g)
            for u in range(2):
                stores(NG - 2 + u, u)
                store_n3(NG - 2 + u)
            sp.wait_ge(x2_stored, 16 * (NG + 1))
            sp.wait_ge(n3_stored, 16 * (NG + 1))

        @block.vector
        def _(dve):
            def split(n):
                raw, (_, hi, lo, bk) = stage[n % NSTAGE], chunks[n]
                dve.wait_ge(w_hi_done, n + 1)
                if bk is None:
                    dve.tensor_tensor(lo, raw[:, :], hi.bitcast(F32), ALU.subtract).then_inc(w_split, 1)
                else:
                    b, k = bk
                    dve.scalar_tensor_tensor(lo, raw[:, :], acol[:, b, k:k + 1], hi.bitcast(F32),
                                             ALU.mult, ALU.subtract).then_inc(w_split, 1)

            def front_stats(f, u, loads):
                dve.wait_ge(x_in[u], 16 * loads)
                for j in range(GT):
                    last = dve.bn_stats(bst[:, j, :], xg[u][:, j, :])
                last.then_inc(stats_done, 1)
                need = value(dve, f + 1)
                dve.wait_ge(half_set, 1)
                dve.wait_ge(stats_done, need)
                for j in range(GT):
                    last = dve.bn_aggr(mv[u][:, j, :], bst[:, j, :])
                last.then_inc(aggr_done, 1)
                dve.wait_ge(aggr_done, f + 1)
                dve.tensor_scalar(vp[:, 0, :], mv[u][:, :, 1], 1.0 + EPS, EPS * EPS, ALU.mult, ALU.add)
                dve.tensor_scalar(vp[:, 1, :], mv[u][:, :, 1], EPS, None, ALU.add).then_inc(var_ready, 1)

            def front_norm(f, u):
                dve.wait_ge(rs_ready, f + 1)
                if not (isinstance(f, int) and f == 0):
                    dve.wait_ge(tp_full, tp_uses(f))
                for j in range(GT):
                    last = dve.tensor_scalar(hn[:, j, :], xg[u][:, j, :], mv[u][:, j, 0:1], rs[u][:, 0, j:j + 1],
                                             ALU.subtract, ALU.mult)
                last.then_inc(h_normed, 1)

            def tp_uses(f):
                return KD * f

            dve.sem_inc(kv_free, NB_A)
            dve.sem_inc(y_free, 2)
            dve.sem_inc(prod_ready, 2)
            dve.memset(half[:, :], -0.5).then_inc(half_set, 1)
            dve.memset(ones[:, :], 1.0).then_inc(ones_set, 1)
            front_stats(0, 0, 1)
            front_norm(0, 0)
            for n in range(N_KV):
                split(n)
            dve.wait_ge(consts_in, 16 * 7)

            def k_tile(g, u, j):
                t = GT * g + j
                dve.wait_ge(prod_ready, t + 1)
                dve.wait_ge(kv_full, 2 * t + 1)
                kj = kb[j % 2]
                dve.tensor_tensor(kj[:, :], mm[2 * j % NB_A][:, :], bkv[:, 0, :], ALU.add).then_inc(kv_free, 1)
                if j == 0:
                    dve.wait_ge(rt_in[u], 16 * (g // 2 + 1))
                dve.wait_ge(kv_free, NB_A + 2 * t + 1)
                pairs = kj[:, 0:2 * R].rearrange("p (h r) -> p h r", h=2)
                for c in range(2):
                    last = dve.tensor_tensor(rot[:, c, :, :], pairs,
                                             rt[u][:, j, c:c + 1, :].to_broadcast([P, 2, R]), ALU.mult)
                last.then_inc(k_parts, 1)
                dve.wait_ge(k_parts, t + 1)
                dve.tensor_tensor(kj[:, 0:R], rot[:, 0, 0, :], rot[:, 1, 1, :], ALU.subtract)
                dve.tensor_tensor(kj[:, R:2 * R], rot[:, 0, 1, :], rot[:, 1, 0, :], ALU.add).then_inc(k_rotated, 1)

            def v_tile(g, j):
                t = GT * g + j
                dve.wait_ge(kv_full, 2 * t + 2)
                dve.tensor_tensor(vb[j % 2][:, :], mm[(2 * j + 1) % NB_A][:, :], bkv[:, 1, :], ALU.add)\
                   .then_inc(kv_free, 1)

            def kv_prod(g, j):
                t = GT * g + j
                dve.wait_ge(rn_ready, t + 1)
                dve.wait_ge(kv_free, NB_A + 2 * t + 2)
                dve.wait_ge(acc_done, t + 1)
                dve.scalar_tensor_tensor(prod[j % 2][:, :], kb[j % 2][:, :], rn[j % 2][:, 0:1], vb[j % 2][:, :],
                                         ALU.mult, ALU.mult).then_inc(prod_ready, 1)

            with dve.Fori(0, NG // 2) as i:
                for u in range(2):
                    g = 2 * i + u
                    front_stats(g + 1, 1 - u, i + 1 + u)
                    k_tile(g, u, 0)
                    v_tile(g, 0)
                    k_tile(g, u, 1)
                    front_norm(g + 1, 1 - u)
                    kv_prod(g, 0)
                    v_tile(g, 1)
                    k_tile(g, u, 2)
                    kv_prod(g, 1)
                    v_tile(g, 2)
                    k_tile(g, u, 3)
                    kv_prod(g, 2)
                    v_tile(g, 3)
                    kv_prod(g, 3)
            dve.wait_ge(prod_ready, 2 + NT)
            dve.sem_inc(a_over, 1)

            for n in range(N_KV, N_Q):
                split(n)
            dve.wait_ge(acol_full, 1)
            dve.tensor_copy(acol[:, :, :], acol_ps[:, 0:B * KD].rearrange("p (b k) -> p b k", b=B))\
               .then_inc(acol_ready, 1)
            dve.wait_ge(a_over, 4)

            def rotate_q(g, u):
                dve.wait_ge(rf_in[u], 16 * (g // 2 + 1))
                dve.wait_ge(q_biased, 2 + KD * g + 2)
                dve.tensor_tensor(rc[:, :, :], qb[:, 0:2, :], rf[u][:, 0:1, :].to_broadcast([P, 2, G]), ALU.mult)\
                   .then_inc(q_cos, 1)
                dve.wait_ge(q_cos, g + 1)
                dve.wait_ge(q_sin, g + 1)
                dve.tensor_tensor(qb[:, 0, :], rc[:, 0, :], rsn[:, 1, :], ALU.subtract)
                dve.tensor_tensor(qb[:, 1, :], rc[:, 1, :], rsn[:, 0, :], ALU.add).then_inc(q_rotated, 1)

            def split_q(g):
                for n, h in enumerate((1, 0)):
                    dve.wait_ge(q_hi_done, 2 * g + n + 1)
                    s = slice(2 * h, 2 * h + 2)
                    dve.tensor_tensor(q_lo[:, s, :], qb[:, s, :], q_hi[:, s, :].bitcast(F32), ALU.subtract)\
                       .then_inc(q_split, 1)

            def token_tiles(g, u, js):
                for j in js:
                    if j == 0:
                        dve.wait_ge(x2_stored, 16 * (g + 1))
                    dve.wait_ge(y_full, GT * g + j + 1)
                    dve.wait_ge(n1_ready, GT * g + j + 1)
                    dve.tensor_tensor(z[:, j, :], mm[2 + j % 2][:, :], n1[:, j, :], ALU.add).then_inc(y_free, 1)
                    dve.wait_ge(y_free, 2 + GT * g + j + 1)
                    last = dve.bn_stats(zst[:, j, :], z[:, j, :])
                if js[-1] == GT - 1:
                    last.then_inc(zst_done, 1)

            def z_moments(g):
                need = value(dve, g + 1)
                dve.wait_ge(half_set, 1)
                dve.wait_ge(zst_done, need)
                for j in range(GT):
                    last = dve.bn_aggr(zmv[:, j, :], zst[:, j, :])
                last.then_inc(zmv_done, 1)
                dve.wait_ge(zmv_done, g + 1)
                dve.tensor_scalar(zv[:, :], zmv[:, :, 1], EPS, None, ALU.add).then_inc(zv_ready, 1)

            def z_shift(g):
                dve.wait_ge(zr_ready, g + 1)
                dve.scalar_tensor_tensor(znm[:, :], zmv[:, :, 0], -1.0, zr[:, :], ALU.mult, ALU.mult)\
                   .then_inc(znm_ready, 1)

            def x2_tiles(g, u):
                for j in range(GT):
                    dve.wait_ge(zn_ready, GT * g + j + 1)
                    dve.tensor_tensor(z[:, j, :], z[:, j, :], xg[u][:, j, :], ALU.add).then_inc(x2_ready, 1)
                    dve.wait_ge(x2_ready, GT * g + j + 1)
                    last = dve.bn_stats(xst[:, j, :], z[:, j, :])
                last.then_inc(xst_done, 1)
                need = value(dve, g + 1)
                dve.wait_ge(half_set, 1)
                dve.wait_ge(xst_done, need)
                for j in range(GT):
                    last = dve.bn_aggr(xmv[:, j, :], xst[:, j, :])
                last.then_inc(xmv_done, 1)
                dve.wait_ge(xmv_done, g + 1)
                dve.tensor_scalar(xv[:, :], xmv[:, :, 1], EPS, None, ALU.add).then_inc(xv_ready, 1)

            def x2_shift(g):
                dve.wait_ge(xr_ready, g + 1)
                dve.scalar_tensor_tensor(xnm[:, :], xmv[:, :, 0], -1.0, xr[:, :], ALU.mult, ALU.mult)\
                   .then_inc(xnm_ready, 1)

            def front_shift(f, u):
                dve.wait_ge(rs_ready, f + 1)
                dve.scalar_tensor_tensor(nm[u][:, :], mv[u][:, :, 0], -1.0, rs[u][:, 1, :], ALU.mult, ALU.mult)\
                   .then_inc(nm_ready, 1)

            def gate(g):
                dve.wait_ge(gl_full, g + 1)
                dve.tensor_copy(lg[:, :, :], gl[:, 0:GT * E].rearrange("p (t e) -> p t e", t=GT)).then_inc(lg_ready, 1)
                need = value(dve, g + 1)
                dve.wait_ge(half_set, 1)
                dve.wait_ge(lg_ready, need)
                for j in range(GT):
                    last = dve.max(mx[:, j, :], lg[:, j, :])
                last.then_inc(mx_ready, 1)
                need = value(dve, g + 1)
                dve.wait_ge(half_set, 1)
                dve.wait_ge(mx_ready, need)
                for j in range(GT):
                    last = dve.max_index(mi[:, j, :], mx[:, j, :], lg[:, j, :])
                last.then_inc(mi_ready, 1)
                dve.tensor_copy(tops[:, bass.ds(GT * g, GT), :], mx[:, :, :])
                dve.wait_ge(mi_ready, g + 1)
                dve.tensor_copy(top_at[:, bass.ds(GT * g, GT), :], mi[:, :, :]).then_inc(tops_kept, 1)

            front_shift(NG, 0)
            rotate_q(0, 0)
            split_q(0)
            for n in range(N_Q, N_ALL):
                split(n)

            def group(g, u, i, last):
                if not last:
                    front_stats(NG + g + 1, 1 - u, NG // 2 + 1 + i + u)
                token_tiles(g, u, [0, 1])
                if not last:
                    dve.wait_ge(rs_ready, NG + g + 2)
                    for j in range(GT):
                        norm = dve.tensor_scalar(hn[:, j, :], xg[1 - u][:, j, :], mv[1 - u][:, j, 0:1],
                                                 rs[1 - u][:, 0, j:j + 1], ALU.subtract, ALU.mult)
                    norm.then_inc(h_normed, 1)
                    front_shift(NG + g + 1, 1 - u)
                token_tiles(g, u, [2, 3])
                z_moments(g)
                z_shift(g)
                x2_tiles(g, u)
                if not last:
                    rotate_q(g + 1, 1 - u)
                x2_shift(g)
                if not last:
                    split_q(g + 1)
                gate(g)

            with dve.Fori(0, NG // 2 - 1) as i:
                for u in range(2):
                    group(2 * i + u, u, i, False)
            for u in range(2):
                group(NG - 2 + u, u, NG // 2 - 1, u == 1)

        @block.scalar
        def _(act):
            def hi_part(n):
                raw, (_, hi, _, bk) = stage[n % NSTAGE], chunks[n]
                act.wait_ge(raw_in[n % NSTAGE], 16 * (n // NSTAGE + 1))
                if bk is None:
                    act.activation(hi, raw[:, :], ACT.Copy).then_inc(w_hi_done, 1)
                else:
                    b, k = bk
                    act.wait_ge(acol_ready, 1)
                    act.activation(hi, raw[:, :], ACT.Identity, scale=acol[:, b, k:k + 1]).then_inc(w_hi_done, 1)

            def front_split(f, u, n0, reader=None):
                for k in range(KD):
                    act.wait_ge(tp_full, n0 + k + 1)
                    if not isinstance(f, int) or f > 0 or k >= 2:
                        act.wait_ge(h_split, KD * f + k - 1)
                    act.activation(hb[k % 2][:, :], tp[k % 2][:, :], ACT.Identity, bias=lnb[:, k:k + 1],
                                   scale=lnw[:, k:k + 1]).then_inc(tp_free, 1)
                    if k == 0 and reader is not None:
                        act.wait_ge(*reader)
                    act.wait_ge(tp_free, 2 + n0 + k + 1)
                    act.activation(h_hi[u][:, k, :], hb[k % 2][:, :], ACT.Copy).then_inc(h_hi_done, 1)

            act.sem_inc(tp_free, 2)
            act.sem_inc(q_free, 2)
            act.wait_ge(consts_in, 16 * 7)
            front_split(0, 0, 0)
            for n in range(N_KV):
                hi_part(n)

            def norm_k(g, j):
                t = GT * g + j
                act.wait_ge(k_rotated, t + 1)
                act.activation(sq[j % 2][:, :], kb[j % 2][:, :], ACT.Square, accum_out=ssq[j % 2][:, 0:1])\
                   .then_inc(ssq_ready, 1)

            with act.Fori(0, NG // 2) as i:
                for u in range(2):
                    g = 2 * i + u
                    norm_k(g, 0)
                    norm_k(g, 1)
                    norm_k(g, 2)
                    front_split(g + 1, 1 - u, KD * (g + 1), (kv_full, 2 * GT * g + 1))
                    norm_k(g, 3)
            act.wait_ge(ssq_ready, NT)
            act.sem_inc(a_over, 1)

            def bias_q(g):
                for m in range(KD):
                    act.wait_ge(q_full, KD * g + m + 1)
                    act.activation(qb[:, m, :], mm[m % 2][:, :], ACT.Identity, bias=bq[:, m:m + 1]).then_inc(q_free, 1)

            def q_hi_parts(g):
                for h in (1, 0):
                    if h:
                        act.wait_ge(q_free, 2 + KD * (g + 1))
                    else:
                        act.wait_ge(q_rotated, g + 1)
                    s = slice(2 * h, 2 * h + 2)
                    act.activation(q_hi[:, s, :], qb[:, s, :], ACT.Copy).then_inc(q_hi_done, 1)

            def first_norm(g, u):
                act.wait_ge(nm_ready, g + 1)
                act.wait_ge(y_free, 2 + GT * g)
                for j in range(GT):
                    act.activation(n1[:, j, :], xg[u][:, j, :], ACT.Identity, bias=nm[u][:, j:j + 1],
                                   scale=rs[u][:, 1, j:j + 1]).then_inc(n1_raw, 1)

            def norm_z(g):
                act.wait_ge(znm_ready, g + 1)
                for j in range(GT):
                    act.activation(z[:, j, :], z[:, j, :], ACT.Identity, bias=znm[:, j:j + 1],
                                   scale=zr[:, j:j + 1]).then_inc(zn_ready, 1)

            def norm_x2(g):
                act.wait_ge(xnm_ready, g + 1)
                act.wait_ge(n3_stored, 16 * (g + 1))
                for j in range(GT):
                    act.activation(n3[:, j, :], z[:, j, :], ACT.Identity, bias=xnm[:, j:j + 1],
                                   scale=xr[:, j:j + 1]).then_inc(n3_ready, 1)

            def n3_columns(g, n0):
                for k in range(KD):
                    act.wait_ge(tp_full, n0 + k + 1)
                    act.activation(n3t[:, k, :], tp[k % 2][:, :], ACT.Copy).then_inc(tp_free, 1)

            for n in range(N_KV, N_Q):
                hi_part(n)
            act.wait_ge(a_over, 4)
            first_norm(0, 0)
            bias_q(0)
            q_hi_parts(0)
            for n in range(N_Q, N_ALL):
                hi_part(n)

            TB = KD * (NG + 1)

            def group(g, u, last):
                if not last:
                    front_split(NG + g + 1, 1 - u, TB + 2 * KD * g, (q_full, KD * g + 1))
                norm_z(g)
                if not last:
                    bias_q(g + 1)
                norm_x2(g)
                if not last:
                    q_hi_parts(g + 1)
                    first_norm(g + 1, 1 - u)
                n3_columns(g, TB + 2 * KD * g + (0 if last else KD))

            with act.Fori(0, NG // 2 - 1) as i:
                for u in range(2):
                    group(2 * i + u, u, False)
            for u in range(2):
                group(NG - 2 + u, u, u == 1)

        @block.gpsimd
        def _(pool):
            def rsqrt(dst, src, n, ready):
                pool.tensor_tensor(dst, src, n, ALU.pow).then_inc(ready, 1)

            def front_rs(f, u):
                pool.wait_ge(var_ready, f + 1)
                pool.tensor_tensor(rs[u][:, :, :], vp[:, :, :], half[:, 0:2 * GT].rearrange("p (c t) -> p c t", c=2),
                                   ALU.pow).then_inc(rs_ready, 1)

            def front_lo(f, u):
                for k in range(KD):
                    pool.wait_ge(h_hi_done, KD * f + k + 1)
                    pool.tensor_tensor(h_lo[u][:, k, :], hb[k % 2][:, :], h_hi[u][:, k, :].bitcast(F32), ALU.subtract)\
                        .then_inc(h_split, 1)

            for b in range(B):
                pool.memset(acc[:, b, :], 0.0).then_inc(acc_done, 1)
            pool.sem_inc(x2_stored, 16)
            pool.sem_inc(n3_stored, 16)
            pool.wait_ge(half_set, 1)
            front_rs(0, 0)
            front_lo(0, 0)

            def rnorm(g, j):
                pool.wait_ge(ssq_ready, GT * g + j + 1)
                pool.tensor_tensor(rn[j % 2][:, :], ssq[j % 2][:, :], half[:, 0:1], ALU.pow).then_inc(rn_ready, 1)

            def accumulate(g, j):
                t = GT * g + j
                pool.wait_ge(prod_ready, 2 + t + 1)
                need = value(pool, B + t)
                offset = value(pool, g // GB)
                a = acc[:, bass.ds(offset, 1), :]
                pool.wait_ge(half_set, 1)
                pool.wait_ge(acc_done, need)
                pool.tensor_tensor(a, a, prod[j % 2][:, :].rearrange("p (o d) -> p o d", o=1), ALU.add)\
                    .then_inc(acc_done, 1)

            with pool.Fori(0, NG // 2) as i:
                for u in range(2):
                    g = 2 * i + u
                    front_rs(g + 1, 1 - u)
                    rnorm(g, 0)
                    rnorm(g, 1)
                    accumulate(g, 0)
                    rnorm(g, 2)
                    accumulate(g, 1)
                    front_lo(g + 1, 1 - u)
                    rnorm(g, 3)
                    accumulate(g, 2)
                    accumulate(g, 3)
            pool.wait_ge(acc_done, B + NT)
            pool.sem_inc(a_over, 1)
            pool.wait_ge(a_over, 4)

            def q_times_sin(g, u):
                pool.wait_ge(rf_in[u], 16 * (g // 2 + 1))
                pool.wait_ge(q_biased, 2 + KD * g + 2)
                if not isinstance(g, int) or g > 0:
                    pool.wait_ge(q_rotated, g)
                pool.tensor_tensor(rsn[:, :, :], qb[:, 0:2, :], rf[u][:, 1:2, :].to_broadcast([P, 2, G]), ALU.mult)\
                    .then_inc(q_sin, 1)

            def add_b_out(g):
                for j in range(GT):
                    pool.wait_ge(n1_raw, GT * g + j + 1)
                    pool.tensor_tensor(n1[:, j, :], n1[:, j, :], bo[:, :], ALU.add).then_inc(n1_ready, 1)

            def token_rsqrt(dst, src, need, ready, g):
                pool.wait_ge(need, g + 1)
                pool.tensor_tensor(dst[:, :], src[:, :], half[:, 0:GT], ALU.pow).then_inc(ready, 1)

            q_times_sin(0, 0)
            add_b_out(0)

            def group(g, u, last):
                if not last:
                    front_rs(NG + g + 1, 1 - u)
                    front_lo(NG + g + 1, 1 - u)
                token_rsqrt(zr, zv, zv_ready, zr_ready, g)
                if not last:
                    q_times_sin(g + 1, 1 - u)
                token_rsqrt(xr, xv, xv_ready, xr_ready, g)
                if not last:
                    add_b_out(g + 1)

            with pool.Fori(0, NG // 2 - 1) as i:
                for u in range(2):
                    group(2 * i + u, u, False)
            for u in range(2):
                group(NG - 2 + u, u, u == 1)

        @block.tensor
        def _(pe):
            def transposes(src, n0, free_from):
                for k in range(KD):
                    pe.wait_ge(tp_free, n0 + k + 1)
                    for j in range(GT):
                        last = pe.transpose(tp[k % 2][:, j * P:(j + 1) * P], src[:, j, k * P:(k + 1) * P], ident[:, :])
                    last.then_inc(tp_full, 1)

            def product(dst, hi, lo, w_hi, w_lo):
                for k in range(KD):
                    pe.matmul(dst, hi(k), w_hi(k), start=(k == 0), stop=False)
                    pe.matmul(dst, hi(k), w_lo(k), start=False, stop=False)
                    last = pe.matmul(dst, lo(k), w_hi(k), start=False, stop=(k == KD - 1))
                return last

            pe.wait_ge(consts_in, 16 * 7)
            pe.wait_ge(h_normed, 1)
            transposes(hn, 0, 0)

            def kv(g, u, j, c, first):
                n = 2 * (GT * g + j) + c
                s = slice(j * P, (j + 1) * P)
                pe.wait_ge(kv_free, n + 1)
                product(mm[(2 * j + c) % NB_A][:, :], lambda k: h_hi[u][:, k, s], lambda k: h_lo[u][:, k, s],
                        lambda k: wkv_hi[:, c, k, :], lambda k: wkv_lo[:, c, k, :]).then_inc(kv_full, 1)

            pe.wait_ge(w_split, N_KV)
            with pe.Fori(0, NG // 2) as i:
                for u in range(2):
                    g = 2 * i + u
                    pe.wait_ge(h_split, KD * (g + 1))
                    for j in range(GT):
                        if j == 3:
                            pe.wait_ge(h_normed, g + 2)
                            transposes(hn, KD * (g + 1), 0)
                        kv(g, u, j, 0, j == 0)
                        kv(g, u, j, 1, False)
            pe.sem_inc(a_over, 1)

            pe.wait_ge(ones_set, 1)
            pe.wait_ge(acc_done, B + NT)
            for b in range(B):
                for k in range(KD):
                    n = b * KD + k
                    last = pe.matmul(acol_ps[:, n:n + 1], acc[:, b, k * P:(k + 1) * P], ones[:, :],
                                     start=True, stop=True)
            last.then_inc(acol_full, 1)

            def q(g, u):
                for m in range(KD):
                    pe.wait_ge(q_free, KD * g + m + 1)
                    if m == 0:
                        pe.wait_ge(h_split, KD * (NG + g + 1))
                    s = slice(m * P, (m + 1) * P)
                    product(mm[m % 2][:, :], lambda k: wq_hi[:, k, s], lambda k: wq_lo[:, k, s],
                            lambda k: h_hi[u][:, k, :], lambda k: h_lo[u][:, k, :]).then_inc(q_full, 1)

            def y(g, u):
                pe.wait_ge(q_split, 2 * (g + 1))
                for j in range(GT):
                    pe.wait_ge(y_free, GT * g + j + 1)
                    s = slice(j * P, (j + 1) * P)
                    b = g // GB
                    w = lambda t, k: t[:, bass.ds(b, 1), k, :].rearrange("p o d -> p (o d)")
                    product(mm[2 + j % 2][:, :], lambda k: q_hi[:, k, s], lambda k: q_lo[:, k, s],
                            lambda k: w(wo_hi, k), lambda k: w(wo_lo, k)).then_inc(y_full, 1)

            def gate(g, n0):
                pe.wait_ge(n3_ready, GT * (g + 1))
                transposes(n3, n0, 0)
                pe.wait_ge(tp_free, 2 + n0 + KD)
                if not isinstance(g, int) or g > 0:
                    pe.wait_ge(lg_ready, g)
                for j in range(GT):
                    for k in range(KD):
                        last = pe.matmul(gl[:, j * E:(j + 1) * E], n3t[:, k, j * P:(j + 1) * P], gw[:, k, :],
                                         start=(k == 0), stop=(k == KD - 1))
                last.then_inc(gl_full, 1)

            pe.wait_ge(w_split, N_Q)
            q(0, 0)
            pe.wait_ge(w_split, N_ALL)
            TB = KD * (NG + 1)

            def group(g, u, last):
                y(g, u)
                n0 = TB + 2 * KD * g
                if not last:
                    pe.wait_ge(h_normed, NG + g + 2)
                    transposes(hn, n0, 0)
                    q(g + 1, 1 - u)
                    n0 = n0 + KD
                gate(g, n0)

            with pe.Fori(0, NG // 2 - 1) as i:
                for u in range(2):
                    group(2 * i + u, u, False)
            for u in range(2):
                group(NG - 2 + u, u, u == 1)


def routed(nc, v):
    (D, E, H, SH, KD, GT, NG, NT, NRT, KH) = (v[n] for n in "D E H SH KD GT NG NT NRT KH".split())
    ident, tops, top_at, gsrc, slots, picked = (v[n] for n in "ident tops top_at gsrc slots picked".split())
    b2_mix = v["b2_mix"]
    n3_dram, r_dram = v["n3_dram"], v["r_dram"]
    with ExitStack() as ctx:
        def sb(name, shape, dt=F32):
            return ctx.enter_context(nc.sbuf_tensor(name, shape, dt))

        def sem(name):
            return ctx.enter_context(nc.semaphore(name))

        xt_ps, th_ps, h_ps, o_ps = ([ctx.enter_context(nc.psum_tensor(f"{n}{i}", [P, 512], F32)) for i in range(2)]
                                    for n in ("xt_ps", "th_ps", "h_ps", "o_ps"))
        rank_ps, total_ps, ids_ps = h_ps[0], h_ps[1], o_ps[0]
        w1_hi, w1_lo = sb("w1_hi", [P, E, KD, H], F32R), sb("w1_lo", [P, E, KD, H], F32R)
        w2_hi, w2_lo = sb("w2_hi", [P, E, KH, D], F32R), sb("w2_lo", [P, E, KH, D], F32R)
        NST = 4
        CH = D
        raw = [sb(f"raw{i}", [P, CH]) for i in range(NST)]

        def flat(t, e, ks):
            return t[:, e, ks, :].rearrange("p k h -> p (k h)")

        chunks = []
        for e in range(E):
            for src, hi, lo, K_, per in ((v["w1"], w1_hi, w1_lo, KD, CH // H), (v["w2"], w2_hi, w2_lo, KH, CH // D)):
                for k in range(0, K_, per):
                    ks = slice(k, k + per)
                    chunks.append((src[e].rearrange("(k p) h -> p k h", p=P)[:, ks, :], flat(hi, e, ks), flat(lo, e, ks)))
        NC = len(chunks)

        b1_mix = sb("b1_mix", [2, E * H], F32R)
        ones_r = sb("ones_r", [2, P], F32R)
        owner, ids = sb("owner", [P, NRT], I32), sb("ids", [P, NRT], U32)
        g1, g2 = picked[:, 0, :], picked[:, 1, :]

        with ExitStack() as early:
            def eb(name, shape, dt=F32):
                return early.enter_context(nc.sbuf_tensor(name, shape, dt))

            b1_raw, b2_raw = eb("b1_raw", [2, E * H]), eb("b2_raw", [32, D])
            sel1, sel2 = eb("sel1", [2, 2]), eb("sel2", [32, 2])
            ones_f, upper = eb("ones_f", [P, P]), eb("upper", [P, P])
            at_f = eb("at_f", [P, NT, 2])
            iota_e, iota_a, iota_q = eb("iota_e", [P, E]), eb("iota_a", [P, NRT]), eb("iota_q", [P, P])
            iota_c, token = eb("iota_c", [P, NT]), eb("token", [P, NT])
            m1, m2, ms, mk = (eb(n, [P, E, NT]) for n in ("m1", "m2", "ms", "mk"))
            total, upto, slot, more = (eb(n, [P, E, NT]) for n in ("total", "upto", "slot", "more"))
            tiles, tiles_to, base, one_e = (eb(n, [P, E]) for n in ("tiles", "tiles_to", "base", "one_e"))
            slot_f, slot_i = eb("slot_f", [P, 2, NT]), eb("slot_i", [P, 2, NT], I32)
            a_i, q_i = eb("a_i", [P, 2, NT], I32), eb("q_i", [P, 2, NT], I32)
            a_f, q_f = eb("a_f", [P, 2, NT]), eb("q_f", [P, 2, NT])
            owner_cmp, owner_f = eb("owner_cmp", [P, NRT, E]), eb("owner_f", [P, NRT])
            hot_q, hot_a = [[eb(f"{n}{i}", [P, w], F32R) for i in range(2)] for n, w in (("hot_q", P), ("hot_a", NRT))]
            zero_q, zero_a = eb("zero_q", [P, P], F32R), eb("zero_a", [P, NRT], F32R)
            gd, gm = eb("gd", [P, NT]), eb("gm", [P, NT, E])
        idx = [sb(f"idx{i}", [P, 1], U32) for i in range(2)]
        xr = [sb(f"xr{i}", [P, D]) for i in range(2)]
        x_hi, x_lo = [[sb(f"{n}{i}", [P, D], F32R) for i in range(2)] for n in ("x_hi", "x_lo")]
        hg = [sb(f"hg{i}", [P, H]) for i in range(2)]
        g_hi, g_lo = [[sb(f"{n}{i}", [P, H], F32R) for i in range(2)] for n in ("g_hi", "g_lo")]
        ro = [sb(f"ro{i}", [P, D]) for i in range(2)]

        raw_in = [sem(f"wraw_in{i}") for i in range(NST)]
        w_hi_done, w_split = sem("ww_hi_done"), sem("ww_split")
        small_in, zeros_set, iotas_set, step = sem("small_in"), sem("zeros_set"), sem("iotas_set"), sem("route_step")
        marks_ready, counts_full, slots_known, gap_ready, exp_ready = (
            sem("marks_ready"), sem("counts_full"), sem("slots_known"), sem("gap_ready"), sem("exp_ready"))
        hot_ready, hot_used, ids_full, ids_ready, owner_ready = (
            sem("hot_ready"), sem("hot_used"), sem("ids_full"), sem("ids_ready"), sem("owner_ready"))
        idx_set, row_in, may_gather = sem("idx_set"), [sem(f"row_in{i}") for i in range(2)], sem("may_gather")
        xt_full, xt_free, x_hi_done = sem("xt_full"), sem("xt_free"), sem("x_hi_done")
        h_full, h_free = sem("h_full"), sem("h_free")
        th_full, th_free, g_hi_done = sem("th_full"), sem("th_free"), sem("g_hi_done")
        o_full, o_free = sem("o_full"), sem("o_free")
        r_stored = [sem(f"r_stored{i}") for i in range(2)]
        PRE = NRT - 2

        block = ctx.enter_context(nc.Block())

        @block.sync
        def _(sp):
            def load_chunk(n):
                if n >= NST:
                    sp.wait_ge(w_split, n - NST + 1)
                src = chunks[n][0]
                sp.dma_start(raw[n % NST][:, :].rearrange("p (k h) -> p k h", k=src.shape[1]), src)\
                  .then_inc(raw_in[n % NST], 16)

            for n in range(NST):
                load_chunk(n)
            b1_row = v["b1"].rearrange("e h -> (e h)").partition_broadcast(2)
            sb2_row = v["sb2"].partition_broadcast(2)
            sp.dma_start(b1_raw[:, :], b1_row).then_inc(small_in, 16)
            sp.wait_ge(zeros_set, 1)
            for r in range(3):
                sp.dma_start(b2_raw[r * E:(r + 1) * E, :], v["b2"]).then_inc(small_in, 16)
            sp.dma_start(b2_raw[3 * E:3 * E + 2, :], sb2_row).then_inc(small_in, 16)
            sp.dma_start(sel1[:, :], v["identity"][0:2, 0:2]).then_inc(small_in, 16)
            sp.dma_start(sel2[:, :], v["bias_parts"]).then_inc(small_in, 16)
            sp.dma_start(upper[:, :], v["before"]).then_inc(small_in, 16)
            for n in range(NST, NC):
                load_chunk(n)

            def store(i, u):
                sp.wait_ge(o_free, 2 + i + 1)
                sp.dma_start(r_dram[bass.ds(i * P, P), :], ro[u][:, :]).then_inc(r_stored[u], 16)

            with sp.Fori(0, NRT // 2 - 1) as n:
                for u in range(2):
                    store(2 * n + u, u)
            store(NRT - 2, 0)
            sp.wait_ge(r_stored[0], 16 * (NRT // 2 + 1))
            sp.wait_ge(r_stored[1], 16 * (NRT // 2))

        @block.vector
        def _(dve):
            count = [0]

            def done(ins):
                count[0] += 1
                ins.then_inc(step, 1)
                dve.wait_ge(step, count[0])

            def lo_part(n):
                _, hi, lo = chunks[n]
                dve.wait_ge(w_hi_done, n + 1)
                dve.tensor_tensor(lo, raw[n % NST][:, :], hi.bitcast(F32), ALU.subtract).then_inc(w_split, 1)

            def bc(ap, shape):
                return ap.to_broadcast(shape)

            def by_expert(ap):
                return bc(ap.rearrange("p (e o) -> p e o", o=1), [P, E, NT])

            dve.memset(b2_raw[:, :], 0.0).then_inc(zeros_set, 1)
            dve.memset(zero_q[:, :].bitcast(F32), 0.0)
            dve.memset(zero_a[:, :].bitcast(F32), 0.0)
            dve.memset(ones_r[:, :].bitcast(F32), 1.0)
            dve.memset(ones_f[:, :], 1.0)
            dve.memset(one_e[:, :], 1.0)
            dve.memset(gsrc[:, :, :], 0.0)
            done(dve.memset(mk[:, :, :], 1.0))
            dve.memset(mk[:, :, 0:1], 0.0)
            dve.memset(gsrc[:, :, 3 * E:3 * E + 2], 1.0)
            done(dve.tensor_copy(at_f[:, :, :], top_at[:, :, 0:2]))
            dve.wait_ge(iotas_set, 5)
            for m, c in ((m1, 0), (m2, 1)):
                at = at_f[:, :, c].rearrange("p (o t) -> p o t", o=1)
                last = dve.tensor_tensor(m[:, :, :], by_expert(iota_e[:, :]), bc(at, [P, E, NT]), ALU.is_equal)
            done(last)
            dve.tensor_tensor(ms[:, :, :], m1[:, :, :], m2[:, :, :], ALU.add).then_inc(marks_ready, 1)
            dve.tensor_tensor(gd[:, :], tops[:, :, 1], tops[:, :, 0], ALU.subtract).then_inc(gap_ready, 1)
            dve.wait_ge(small_in, 16 * 8)
            for mix, raw_, sel in ((b1_mix[:, :], b1_raw[:, :], sel1), (b2_mix[:, :], b2_raw[:, :], sel2)):
                done(dve.tensor_copy(mix, raw_))
                done(dve.tensor_tensor(raw_, raw_, mix.bitcast(F32), ALU.subtract))
                done(dve.tensor_scalar(mix, mix.bitcast(F32), sel[:, 0:1], None, ALU.mult))
                done(dve.scalar_tensor_tensor(mix, raw_, sel[:, 1:2], mix.bitcast(F32), ALU.mult, ALU.add))
            dve.wait_ge(counts_full, 1)
            done(dve.tensor_copy(total[:, :, :], total_ps[:, 0:E * NT].rearrange("p (e t) -> p e t", e=E)))
            done(dve.tensor_tensor_scan(upto[:, :, :].rearrange("p e t -> p (e t)"),
                                        mk[:, :, :].rearrange("p e t -> p (e t)"),
                                        total[:, :, :].rearrange("p e t -> p (e t)"), 0.0, ALU.mult, ALU.add))
            done(dve.tensor_tensor(more[:, :, :], bc(upto[:, :, NT - 1:NT], [P, E, NT]),
                                   bc(iota_c[:, :].rearrange("p (o t) -> p o t", o=1), [P, E, NT]), ALU.is_gt))
            done(dve.tensor_reduce(tiles[:, :], more[:, :, :], AX.X, ALU.add))
            done(dve.tensor_tensor_scan(tiles_to[:, :], one_e[:, :], tiles[:, :], 0.0, ALU.mult, ALU.add))
            done(dve.tensor_tensor(base[:, :], tiles_to[:, :], tiles[:, :], ALU.subtract))
            dve.tensor_tensor(upto[:, :, :], upto[:, :, :], total[:, :, :], ALU.subtract)
            done(dve.tensor_scalar(base[:, :], base[:, :], float(P), None, ALU.mult))
            done(dve.tensor_tensor(slot[:, :, :], rank_ps[:, 0:E * NT].rearrange("p (e t) -> p e t", e=E),
                                   upto[:, :, :], ALU.add))
            done(dve.tensor_tensor(slot[:, :, :], slot[:, :, :], by_expert(base[:, :]), ALU.add))
            dve.tensor_tensor(ms[:, :, :], m1[:, :, :], slot[:, :, :], ALU.mult)
            done(dve.tensor_tensor(upto[:, :, :], m2[:, :, :], slot[:, :, :], ALU.mult))
            dve.tensor_reduce(slot_f[:, 0, :], ms[:, :, :].rearrange("p e t -> p t e"), AX.X, ALU.add)
            done(dve.tensor_reduce(slot_f[:, 1, :], upto[:, :, :].rearrange("p e t -> p t e"), AX.X, ALU.add))
            dve.tensor_copy(slots[:, :, :], slot_f[:, :, :])
            done(dve.tensor_copy(slot_i[:, :, :], slot_f[:, :, :]))
            dve.tensor_scalar(a_i[:, :, :], slot_i[:, :, :], 7, None, ALU.arith_shift_right)
            done(dve.tensor_scalar(q_i[:, :, :], slot_i[:, :, :], P - 1, None, ALU.bitwise_and))
            dve.tensor_copy(a_f[:, :, :], a_i[:, :, :])
            done(dve.tensor_copy(q_f[:, :, :], q_i[:, :, :]))
            done(dve.tensor_tensor(owner_cmp[:, :, :], bc(iota_a[:, :].rearrange("p (a o) -> p a o", o=1), [P, NRT, E]),
                                   bc(tiles_to[:, :].rearrange("p (o e) -> p o e", o=1), [P, NRT, E]), ALU.is_ge))
            done(dve.tensor_reduce(owner_f[:, :], owner_cmp[:, :, :], AX.X, ALU.add))
            dve.tensor_scalar(owner[:, :], owner_f[:, :], float(E - 1), None, ALU.min).then_inc(owner_ready, 1)
            dve.sem_inc(hot_used, 2)
            with dve.Fori(0, NT) as t:
                for c in range(2):
                    dve.wait_ge(hot_used, 2 * t + c + 1)
                    dve.tensor_scalar(hot_q[c][:, :], iota_q[:, :], q_f[:, c, bass.ds(t, 1)], None, ALU.is_equal)
                    dve.tensor_scalar(hot_a[c][:, :], iota_a[:, :], a_f[:, c, bass.ds(t, 1)], token[:, bass.ds(t, 1)],
                                      ALU.is_equal, ALU.mult).then_inc(hot_ready, 1)
            dve.wait_ge(exp_ready, 1)
            done(dve.tensor_scalar(g2, gd[:, :], 1.0, None, ALU.add))
            done(dve.reciprocal(g1, g2))
            done(dve.tensor_tensor(g2, gd[:, :], g1, ALU.mult))
            by_token = lambda m: m[:, :, :].rearrange("p e t -> p t e")
            spread = lambda x: bc(x.rearrange("p (t o) -> p t o", o=1), [P, NT, E])
            dve.tensor_tensor(gm[:, :, :], by_token(m1), spread(g1), ALU.mult)
            done(dve.tensor_tensor(owner_cmp[:, 0:NT, :], by_token(m2), spread(g2), ALU.mult))
            done(dve.tensor_tensor(gm[:, :, :], gm[:, :, :], owner_cmp[:, 0:NT, :], ALU.add))
            done(dve.tensor_copy(v["gate_hi"][:, :, :], gm[:, :, :]))
            dve.tensor_copy(gsrc[:, :, 0:E], v["gate_hi"][:, :, :].bitcast(F32))
            dve.tensor_copy(gsrc[:, :, 2 * E:3 * E], v["gate_hi"][:, :, :].bitcast(F32))
            dve.tensor_tensor(gsrc[:, :, E:2 * E], gm[:, :, :], v["gate_hi"][:, :, :].bitcast(F32), ALU.subtract)
            dve.wait_ge(ids_full, 1)
            dve.tensor_copy(ids[:, :], ids_ps[:, 0:NRT]).then_inc(ids_ready, 1)
            for n in range(NC):
                lo_part(n)

            def x_lo_part(i, u):
                dve.wait_ge(x_hi_done, i + 1)
                dve.tensor_tensor(x_lo[u][:, :], xt_ps[u][:, :], x_hi[u][:, :].bitcast(F32), ALU.subtract)\
                   .then_inc(xt_free, 1)

            def g_lo_part(i, u):
                dve.wait_ge(g_hi_done, i + 1)
                dve.tensor_tensor(g_lo[u][:, :], th_ps[u][:, 0:H], g_hi[u][:, :].bitcast(F32), ALU.subtract)\
                   .then_inc(th_free, 1)

            def o_out(i, u):
                dve.wait_ge(r_stored[u], 16 * (i // 2 + 1))
                dve.wait_ge(o_full, i + 1)
                dve.tensor_copy(ro[u][:, :], o_ps[u][:, :]).then_inc(o_free, 1)

            x_lo_part(0, 0)
            x_lo_part(1, 1)
            with dve.Fori(0, PRE // 2) as n:
                for s in range(2):
                    i, u = 2 * n + 1 + s, (1 + s) % 2
                    x_lo_part(i + 1, 1 - u)
                    g_lo_part(i - 1, 1 - u)
                    o_out(i - 1, 1 - u)
            g_lo_part(PRE, PRE % 2)
            o_out(PRE, PRE % 2)

        @block.scalar
        def _(act):
            def hi_part(n):
                act.wait_ge(raw_in[n % NST], 16 * (n // NST + 1))
                act.activation(chunks[n][1], raw[n % NST][:, :], ACT.Copy).then_inc(w_hi_done, 1)

            act.sem_inc(h_free, 2)
            act.wait_ge(gap_ready, 1)
            act.activation(gd[:, :], gd[:, :], ACT.Exp).then_inc(exp_ready, 1)
            for n in range(NC):
                hi_part(n)

            def x_hi_part(i, u):
                act.wait_ge(xt_full, i + 1)
                act.activation(x_hi[u][:, :], xt_ps[u][:, :], ACT.Copy).then_inc(x_hi_done, 1)

            def gelu(i, u):
                act.wait_ge(h_full, i + 1)
                act.activation(hg[u][:, :], h_ps[u][:, 0:H], ACT.Gelu).then_inc(h_free, 1)

            def g_hi_part(i, u):
                act.wait_ge(th_full, i + 1)
                act.activation(g_hi[u][:, :], th_ps[u][:, 0:H], ACT.Copy).then_inc(g_hi_done, 1)

            x_hi_part(0, 0)
            x_hi_part(1, 1)
            gelu(0, 0)
            with act.Fori(0, PRE // 2) as n:
                for s in range(2):
                    i, u = 2 * n + 1 + s, (1 + s) % 2
                    x_hi_part(i + 1, 1 - u)
                    g_hi_part(i - 1, 1 - u)
                    gelu(i, u)
            g_hi_part(PRE, PRE % 2)

        @block.gpsimd
        def _(pool):
            small = dict(allow_small_or_imprecise_dtypes=True)
            pool.iota(iota_e[:, :], [[1, E]], base=0, channel_multiplier=0, **small).then_inc(iotas_set, 1)
            pool.iota(iota_a[:, :], [[1, NRT]], base=0, channel_multiplier=0, **small).then_inc(iotas_set, 1)
            pool.iota(iota_q[:, :], [[1, P]], base=0, channel_multiplier=0, **small).then_inc(iotas_set, 1)
            pool.iota(iota_c[:, :], [[P, NT]], base=0, channel_multiplier=0, **small).then_inc(iotas_set, 1)
            pool.iota(token[:, :], [[P, NT]], base=0, channel_multiplier=1, **small).then_inc(iotas_set, 1)
            pool.sem_inc(r_stored[0], 16)
            pool.sem_inc(r_stored[1], 16)
            pool.wait_ge(ids_ready, 1)

            def gather(i, u):
                pool.tensor_copy(idx[u][:, :], ids[:, bass.ds(i, 1)]).then_inc(idx_set, 1)
                pool.wait_ge(idx_set, i + 1)
                pool.sem_inc(may_gather, 1)
                pool.indirect_dma_start(xr[u][:, :], None, n3_dram,
                                        bass.IndirectOffsetOnAxis(idx[u][:, 0:1], 0)).then_inc(row_in[u], 16)

            for i in range(2):
                gather(i, i)
            with pool.Fori(1, NRT // 2) as n:
                for u in range(2):
                    i = 2 * n + u
                    pool.wait_ge(xt_full, i - 1)
                    pool.sem_inc(may_gather, 1)
                    gather(i, u)

        @block.tensor
        def _(pe):
            pe.wait_ge(small_in, 16 * 8)
            pe.wait_ge(marks_ready, 1)
            marks = ms[:, :, :].rearrange("p e t -> p (e t)")
            pe.matmul(rank_ps[:, 0:E * NT], upper[:, :], marks, start=True, stop=True)
            pe.matmul(total_ps[:, 0:E * NT], ones_f[:, :], marks, start=True, stop=True).then_inc(counts_full, 1)
            pe.matmul(ids_ps[:, 0:NRT], zero_q[:, :], zero_a[:, :], start=True, stop=False)
            with pe.Fori(0, NT) as t:
                for c in range(2):
                    pe.wait_ge(hot_ready, 2 * t + c + 1)
                    pe.matmul(ids_ps[:, 0:NRT], hot_q[c][:, :], hot_a[c][:, :], start=False, stop=False)\
                      .then_inc(hot_used, 1)
            pe.matmul(ids_ps[:, 0:NRT], zero_q[:, :], zero_a[:, :], start=False, stop=True).then_inc(ids_full, 1)

            def x_turn(i, u):
                pe.wait_ge(row_in[u], 16 * (i // 2 + 1))
                if not isinstance(i, int):
                    pe.wait_ge(xt_free, i - 1)
                for k in range(KD):
                    last = pe.transpose(xt_ps[u][:, k * P:(k + 1) * P], xr[u][:, k * P:(k + 1) * P], ident[:, :])
                last.then_inc(xt_full, 1)

            def h_of(i, u, e):
                pe.wait_ge(xt_free, i + 1)
                pe.wait_ge(h_free, i + 1)
                out = h_ps[u][:, 0:H]
                w = lambda t, k: t[:, bass.ds(e, 1), k, :].rearrange("p o h -> p (o h)")
                for k in range(KD):
                    s = slice(k * P, (k + 1) * P)
                    pe.matmul(out, x_hi[u][:, s], w(w1_hi, k), start=(k == 0), stop=False)
                    pe.matmul(out, x_hi[u][:, s], w(w1_lo, k), start=False, stop=False)
                    pe.matmul(out, x_lo[u][:, s], w(w1_hi, k), start=False, stop=False)
                pe.matmul(out, ones_r[:, :], b1_mix[:, bass.ds(e * H, H)], start=False, stop=True).then_inc(h_full, 1)

            def h_turn(i, u):
                pe.wait_ge(h_free, 2 + i + 1)
                if not isinstance(i, int):
                    pe.wait_ge(th_free, i + 1)
                for k in range(KH):
                    last = pe.transpose(th_ps[u][:, k * P:(k + 1) * P], hg[u][:, k * P:(k + 1) * P], ident[:, :])
                last.then_inc(th_full, 1)

            def o_of(i, u, e):
                pe.wait_ge(th_free, 2 + i + 1)
                pe.wait_ge(o_free, i + 1)
                w = lambda t, k: t[:, bass.ds(e, 1), k, :].rearrange("p o d -> p (o d)")
                for k in range(KH):
                    s = slice(k * P, (k + 1) * P)
                    pe.matmul(o_ps[u][:, :], g_hi[u][:, s], w(w2_hi, k), start=(k == 0), stop=False)
                    pe.matmul(o_ps[u][:, :], g_hi[u][:, s], w(w2_lo, k), start=False, stop=False)
                    last = pe.matmul(o_ps[u][:, :], g_lo[u][:, s], w(w2_hi, k), start=False, stop=(k == KH - 1))
                last.then_inc(o_full, 1)

            def expert(i):
                return pe.value_load(owner[0:1, bass.ds(i, 1)], min_val=0, max_val=E - 1)

            pe.sem_inc(th_free, 2)
            pe.sem_inc(o_free, 2)
            pe.wait_ge(owner_ready, 1)
            x_turn(0, 0)
            x_turn(1, 1)
            pe.wait_ge(w_split, NC)
            h_of(0, 0, expert(0))
            with pe.Fori(0, PRE // 2) as n:
                for s in range(2):
                    i, u = 2 * n + 1 + s, (1 + s) % 2
                    e_before, e = expert(i - 1), expert(i)
                    x_turn(i + 1, 1 - u)
                    h_turn(i - 1, 1 - u)
                    h_of(i, u, e)
                    o_of(i - 1, 1 - u, e_before)
            h_turn(PRE, PRE % 2)
            o_of(PRE, PRE % 2, expert(PRE))


def combined(nc, v):
    (D, E, SH, KD, GT, G, NG) = (v[n] for n in "D E SH KD GT G NG".split())
    ident, gsrc, slots, picked, r_dram = (v[n] for n in "ident gsrc slots picked r_dram".split())
    b2_mix = v["b2_mix"]
    x2_groups, n3_groups, out_groups = v["x2_groups"], v["n3_groups"], v["out_groups"]
    KS = SH // P
    with ExitStack() as ctx:
        def sb(name, shape, dt=F32):
            return ctx.enter_context(nc.sbuf_tensor(name, shape, dt))

        def sem(name):
            return ctx.enter_context(nc.semaphore(name))

        def bank(name):
            return ctx.enter_context(nc.psum_tensor(name, [P, 512], F32))

        sp_, f_, t_ = [bank(f"s_ps{i}") for i in range(2)], [bank(f"f_ps{i}") for i in range(2)], [bank(f"t_ps{i}") for i in range(2)]
        g_ = bank("g_ps")
        sb1 = sb("sb1c", [P, KS])
        half = sb("half3", [P, GT])
        n3 = [sb(f"n3_{i}", [P, GT, D]) for i in range(2)]
        x2 = [sb(f"x2_{i}", [P, GT, D]) for i in range(2)]
        r1, r2 = [[sb(f"{n}_{i}", [P, GT, D]) for i in range(2)] for n in ("r1", "r2")]
        idx = [sb(f"idxg{i}", [P, 2, GT], U32) for i in range(2)]
        n_hi, n_lo = [[sb(f"{n}{i}", [P, KD, G], F32R) for i in range(2)] for n in ("n_hi", "n_lo")]
        s_raw = [sb(f"s_raw{i}", [P, KD, SH]) for i in range(2)]
        s1_hi, s1_lo, s2_hi, s2_lo = (sb(n, [P, KD, SH], F32R) for n in ("s1_hi", "s1_lo", "s2_hi", "s2_lo"))
        hs = sb("hs", [P, KS, G])
        h_hi, h_lo = sb("hs_hi", [P, KS, G], F32R), sb("hs_lo", [P, KS, G], F32R)
        gs = [sb(f"gs{i}", [P, GT, 32]) for i in range(2)]
        gt = sb("gt", [32, G], F32R)
        f = sb("f", [P, GT, D])
        y = sb("y", [P, GT, D])
        st, mv, va, r, nm = (sb("f_st", [P, GT, 6]), sb("f_mv", [P, GT, 2]), sb("f_va", [P, GT]), sb("f_r", [P, GT]),
                             sb("f_nm", [P, GT]))
        small_in, half_set = sem("sb1_in"), sem("half3_set")
        sw_in, sw_hi, sw_split = [sem(f"sw_in{i}") for i in range(2)], sem("sw_hi"), sem("sw_split")
        n3_in, x2_in = [sem(f"n3_in{i}") for i in range(2)], [sem(f"x2_in{i}") for i in range(2)]
        rows_in = [sem(f"rows_in{i}") for i in range(2)]
        idx_set, gs_set, may_gather = sem("idxg_set"), sem("gs_set"), sem("may_gather3")
        t_full, t_free, n_hi_done = sem("t_full"), sem("t_free"), sem("n_hi_done")
        s_full, s_free, h_hi_done, h_split = sem("s_full"), sem("s_free"), sem("h_hi_done3"), sem("h_split3")
        g_full, g_ready = sem("g_full"), sem("g_ready")
        f_full, f_free, f_ready = sem("f_full"), sem("f_free"), sem("f_ready")
        st_done, mv_done, va_ready, r_ready, nm_ready, y_normed, y_ready, stored = (
            sem(n) for n in ("st_done", "mv_done", "va_ready", "r_ready", "nm3_ready", "y_normed", "y_ready", "stored"))

        block = ctx.enter_context(nc.Block())

        @block.sync
        def _(sp):
            sp.dma_start(n3[0][:, :, :], n3_groups[0]).then_inc(n3_in[0], 16)
            for i, w in enumerate((v["sw1"], v["sw2"])):
                sp.dma_start(s_raw[i][:, :, :], w.rearrange("(k p) h -> p k h", p=P)).then_inc(sw_in[i], 16)
            sp.dma_start(sb1[:, :], v["sb1"]).then_inc(small_in, 16)
            sp.dma_start(n3[1][:, :, :], n3_groups[1]).then_inc(n3_in[1], 16)
            for u in range(2):
                sp.dma_start(x2[u][:, :, :], x2_groups[u]).then_inc(x2_in[u], 16)

            def store(g):
                sp.wait_ge(y_ready, GT * (g + 1))
                sp.dma_start(out_groups[g], y[:, :, :]).then_inc(stored, 16)

            with sp.Fori(0, NG // 2 - 1) as n:
                for u in range(2):
                    g = 2 * n + u
                    sp.wait_ge(t_full, KD * (g + 1))
                    sp.dma_start(n3[u][:, :, :], n3_groups[g + 2]).then_inc(n3_in[u], 16)
                    store(g)
                    sp.dma_start(x2[u][:, :, :], x2_groups[g + 2]).then_inc(x2_in[u], 16)
            for u in range(2):
                store(NG - 2 + u)
            sp.wait_ge(stored, 16 * (NG + 1))

        @block.vector
        def _(dve):
            dve.memset(half[:, :], -0.5).then_inc(half_set, 1)
            dve.sem_inc(t_free, 2)
            dve.sem_inc(f_free, 2)

            def n_lo_parts(g, u):
                for k in range(KD):
                    dve.wait_ge(n_hi_done, KD * g + k + 1)
                    dve.tensor_tensor(n_lo[u][:, k, :], t_[k % 2][:, :], n_hi[u][:, k, :].bitcast(F32), ALU.subtract)\
                       .then_inc(t_free, 1)

            def h_lo_parts(g):
                for m in range(KS):
                    dve.wait_ge(h_hi_done, KS * g + m + 1)
                    dve.tensor_tensor(h_lo[:, m, :], hs[:, m, :], h_hi[:, m, :].bitcast(F32), ALU.subtract)\
                       .then_inc(h_split, 1)

            def sums(g, u):
                for j in range(GT):
                    t = GT * g + j
                    if j == 0:
                        dve.wait_ge(rows_in[u], 16 * 2 * GT * (g // 2 + 1))
                    dve.wait_ge(f_full, t + 1)
                    dve.scalar_tensor_tensor(f[:, j, :], r1[u][:, j, :], picked[:, 0, bass.ds(t, 1)], f_[j % 2][:, :],
                                             ALU.mult, ALU.add).then_inc(f_free, 1)
                    dve.wait_ge(f_free, 2 + t + 1)
                    dve.scalar_tensor_tensor(f[:, j, :], r2[u][:, j, :], picked[:, 1, bass.ds(t, 1)], f[:, j, :],
                                             ALU.mult, ALU.add).then_inc(f_ready, 1)
                    dve.wait_ge(f_ready, t + 1)
                    last = dve.bn_stats(st[:, j, :], f[:, j, :])
                last.then_inc(st_done, 1)
                need = value(dve, g + 1)
                dve.wait_ge(half_set, 1)
                dve.wait_ge(st_done, need)
                for j in range(GT):
                    last = dve.bn_aggr(mv[:, j, :], st[:, j, :])
                last.then_inc(mv_done, 1)
                dve.wait_ge(mv_done, g + 1)
                dve.tensor_scalar(va[:, :], mv[:, :, 1], EPS, None, ALU.add).then_inc(va_ready, 1)

            def shift(g):
                dve.wait_ge(r_ready, g + 1)
                dve.scalar_tensor_tensor(nm[:, :], mv[:, :, 0], -1.0, r[:, :], ALU.mult, ALU.mult).then_inc(nm_ready, 1)

            n_lo_parts(0, 0)
            for i, (hi, lo) in enumerate(((s1_hi, s1_lo), (s2_hi, s2_lo))):
                for k in range(KD):
                    dve.wait_ge(sw_hi, KD * i + k + 1)
                    dve.tensor_tensor(lo[:, k, :], s_raw[i][:, k, :], hi[:, k, :].bitcast(F32), ALU.subtract)\
                       .then_inc(sw_split, 1)
            with dve.Fori(0, NG // 2 - 1) as n:
                for u in range(2):
                    g = 2 * n + u
                    h_lo_parts(g)
                    n_lo_parts(g + 1, 1 - u)
                    sums(g, u)
                    shift(g)
            h_lo_parts(NG - 2)
            n_lo_parts(NG - 1, 1)
            sums(NG - 2, 0)
            shift(NG - 2)
            h_lo_parts(NG - 1)
            sums(NG - 1, 1)
            shift(NG - 1)

        @block.scalar
        def _(act):
            act.sem_inc(s_free, 2)
            act.wait_ge(small_in, 16)

            def n_hi_parts(g, u):
                for k in range(KD):
                    act.wait_ge(t_full, KD * g + k + 1)
                    act.activation(n_hi[u][:, k, :], t_[k % 2][:, :], ACT.Copy).then_inc(n_hi_done, 1)

            def gelu(g):
                for m in range(KS):
                    act.wait_ge(s_full, KS * g + m + 1)
                    act.activation(hs[:, m, :], sp_[m % 2][:, :], ACT.Gelu, bias=sb1[:, m:m + 1]).then_inc(s_free, 1)
                    act.wait_ge(s_free, 2 + KS * g + m + 1)
                    act.activation(h_hi[:, m, :], hs[:, m, :], ACT.Copy).then_inc(h_hi_done, 1)

            def gates(g):
                act.wait_ge(g_full, g + 1)
                act.activation(gt[:, :], g_[0:32, :], ACT.Copy).then_inc(g_ready, 1)

            def normed(g):
                act.wait_ge(nm_ready, g + 1)
                act.wait_ge(stored, 16 * (g + 1))
                for j in range(GT):
                    act.activation(y[:, j, :], f[:, j, :], ACT.Identity, bias=nm[:, j:j + 1], scale=r[:, j:j + 1])\
                       .then_inc(y_normed, 1)

            n_hi_parts(0, 0)
            for i, hi in enumerate((s1_hi, s2_hi)):
                act.wait_ge(sw_in[i], 16)
                for k in range(KD):
                    act.activation(hi[:, k, :], s_raw[i][:, k, :], ACT.Copy).then_inc(sw_hi, 1)
            with act.Fori(0, NG // 2 - 1) as n:
                for u in range(2):
                    g = 2 * n + u
                    gelu(g)
                    gates(g)
                    n_hi_parts(g + 1, 1 - u)
                    normed(g)
            gelu(NG - 2)
            gates(NG - 2)
            n_hi_parts(NG - 1, 1)
            normed(NG - 2)
            gelu(NG - 1)
            gates(NG - 1)
            normed(NG - 1)

        @block.gpsimd
        def _(pool):
            pool.sem_inc(stored, 16)
            pool.wait_ge(half_set, 1)

            def gather(g, u):
                pool.tensor_copy(gs[u][:, :, :], gsrc[:, bass.ds(GT * g, GT), :]).then_inc(gs_set, 1)
                pool.tensor_copy(idx[u][:, :, :], slots[:, :, bass.ds(GT * g, GT)]).then_inc(idx_set, 1)
                pool.wait_ge(idx_set, g + 1)
                pool.sem_inc(may_gather, 1)
                for j in range(GT):
                    for c, rr in ((0, r1), (1, r2)):
                        pool.indirect_dma_start(rr[u][:, j, :], None, r_dram,
                                                bass.IndirectOffsetOnAxis(idx[u][:, c, j:j + 1], 0))\
                            .then_inc(rows_in[u], 16)

            def finish(g, u):
                pool.wait_ge(va_ready, g + 1)
                pool.tensor_tensor(r[:, :], va[:, :], half[:, :], ALU.pow).then_inc(r_ready, 1)
                pool.wait_ge(x2_in[u], 16 * (g // 2 + 1))
                for j in range(GT):
                    pool.wait_ge(y_normed, GT * g + j + 1)
                    pool.tensor_tensor(y[:, j, :], y[:, j, :], x2[u][:, j, :], ALU.add).then_inc(y_ready, 1)

            gather(0, 0)
            gather(1, 1)
            with pool.Fori(0, NG // 2 - 1) as n:
                for u in range(2):
                    g = 2 * n + u
                    finish(g, u)
                    pool.wait_ge(f_ready, GT * (g + 1))
                    pool.sem_inc(may_gather, 1)
                    gather(g + 2, u)
            for u in range(2):
                finish(NG - 2 + u, u)

        @block.tensor
        def _(pe):
            def n3_turn(g, u):
                pe.wait_ge(n3_in[u], 16 * (g // 2 + 1))
                for k in range(KD):
                    pe.wait_ge(t_free, KD * g + k + 1)
                    for j in range(GT):
                        last = pe.transpose(t_[k % 2][:, j * P:(j + 1) * P], n3[u][:, j, k * P:(k + 1) * P], ident[:, :])
                    last.then_inc(t_full, 1)

            def shared_h(g, u):
                pe.wait_ge(t_free, 2 + KD * (g + 1))
                for m in range(KS):
                    pe.wait_ge(s_free, KS * g + m + 1)
                    s = slice(m * P, (m + 1) * P)
                    for k in range(KD):
                        pe.matmul(sp_[m % 2][:, :], s1_hi[:, k, s], n_hi[u][:, k, :], start=(k == 0), stop=False)
                        pe.matmul(sp_[m % 2][:, :], s1_hi[:, k, s], n_lo[u][:, k, :], start=False, stop=False)
                        last = pe.matmul(sp_[m % 2][:, :], s1_lo[:, k, s], n_hi[u][:, k, :], start=False,
                                         stop=(k == KD - 1))
                    last.then_inc(s_full, 1)

            def gates(g, u):
                pe.wait_ge(gs_set, g + 1)
                pe.wait_ge(g_ready, g + 1)
                for j in range(GT):
                    last = pe.transpose(g_[0:32, j * P:(j + 1) * P], gs[u][:, j, :], ident[:, :])
                last.then_inc(g_full, 1)

            def shared_o(g):
                pe.wait_ge(h_split, KS * (g + 1))
                pe.wait_ge(g_ready, 1 + g + 1)
                for j in range(GT):
                    pe.wait_ge(f_free, GT * g + j + 1)
                    s = slice(j * P, (j + 1) * P)
                    out = f_[j % 2][:, :]
                    for k in range(KS):
                        pe.matmul(out, h_hi[:, k, s], s2_hi[:, k, :], start=(k == 0), stop=False)
                        pe.matmul(out, h_hi[:, k, s], s2_lo[:, k, :], start=False, stop=False)
                        pe.matmul(out, h_lo[:, k, s], s2_hi[:, k, :], start=False, stop=False)
                    pe.matmul(out, gt[:, s], b2_mix[:, :], start=False, stop=True).then_inc(f_full, 1)

            pe.sem_inc(g_ready, 1)
            n3_turn(0, 0)
            pe.wait_ge(sw_split, 2 * KD)
            with pe.Fori(0, NG // 2 - 1) as n:
                for u in range(2):
                    g = 2 * n + u
                    shared_h(g, u)
                    gates(g, u)
                    n3_turn(g + 1, 1 - u)
                    shared_o(g)
            shared_h(NG - 2, 0)
            gates(NG - 2, 0)
            n3_turn(NG - 1, 1)
            shared_o(NG - 2)
            shared_h(NG - 1, 1)
            gates(NG - 1, 1)
            shared_o(NG - 1)


_NAMES = ["X", "ln_w", "ln_b", "W_in", "b_in", "W_out", "b_out"]
_FFN = ["gate_w", "w1", "b1", "w2", "b2", "shared_w1", "shared_b1", "shared_w2", "shared_b2"]


def _pairs_apart(n):
    return np.concatenate([np.arange(0, n // 2, 2), np.arange(1, n // 2, 2), np.arange(n // 2, n)])


def _angles(seq, n):
    rot = n // 2
    inv = (1.0 / np.float64(THETA) ** (np.arange(0, rot, 2) / rot)).astype(np.float32)
    a = np.arange(seq, dtype=np.float32)[:, None] * inv[None, :]
    return np.cos(a).astype(np.float32), np.sin(a).astype(np.float32)


def _columns(x):
    return np.moveaxis(x.reshape(*x.shape[:-1], -1, P), -1, 0)


def kernel(**inputs):
    import concourse.bacc as _bacc
    from concourse.bass_utils import run_bass_kernel_spmd as _run

    nc = _bacc.Bacc("TRN2", target_bir_lowering=False, num_devices=1)
    a = {k: np.asarray(x) for k, x in inputs.items()}
    Bn, S, D = a["L0_attn_X"].shape
    order = _pairs_apart(D)
    cols = np.concatenate([order + c * D for c in range(3)])
    host = {n: a[f"L0_attn_{n}"] for n in _NAMES}
    host["W_in"] = host["W_in"][:, cols]
    host["b_in"] = host["b_in"][cols]
    host["W_out"] = host["W_out"][order, :]
    host.update({n: a[f"L0_ffn_{n}"] for n in _FFN})
    for n in ("ln_w", "ln_b", "shared_b1"):
        host[n] = _columns(host[n])
    host["b_q"] = _columns(host["b_in"][:D])
    cos, sin = _angles(S, D)
    host["rope_tok"] = np.concatenate([cos, sin], axis=1)
    host["rope_feat"] = np.stack([cos.T, sin.T])
    host["identity"] = np.eye(P, dtype=np.float32)
    host["before"] = np.triu(np.ones((P, P), np.float32), 1)
    E = a["L0_ffn_b2"].shape[0]
    row = np.arange(32)
    host["bias_parts"] = np.stack([(row < 2 * E) | (row == 3 * E), ((row >= 2 * E) & (row < 3 * E)) | (row == 3 * E + 1)],
                                  axis=1).astype(np.float32)
    arrays, args = {}, []
    for name, x in host.items():
        x = np.ascontiguousarray(x)
        arrays[f"in_{name}"] = x
        args.append(nc.dram_tensor(f"in_{name}", x.shape, mybir.dt.from_np(x.dtype), kind="ExternalInput").ap())
    out = nc.dram_tensor("out_0", (Bn, S, D), F32, kind="ExternalOutput").ap()
    sandwich_kernel(nc, *args, out)
    r = _run(nc, [arrays], core_ids=[0])
    return r.results[0]["out_0"]
```

```python
from contextlib import ExitStack

import numpy as np

import concourse.bass as bass
from concourse import mybir

P = 128
F32 = mybir.dt.float32
F32R = mybir.dt.float32r
U32 = mybir.dt.uint32
I32 = mybir.dt.int32
AX = mybir.AxisListType
ALU = mybir.AluOpType
ACT = mybir.ActivationFunctionType
EPS = 1e-5
THETA = 10000.0


def sandwich_kernel(nc, X, ln_w, ln_b, W_in, b_in, W_out, b_out, gate_w, w1, b1, w2, b2,
                    sw1, sb1, sw2, sb2, b_q, rope_tok, rope_feat, identity, before, bias_parts,
                    out):
    B, S, D = X.shape
    E, _, H = w1.shape
    SH = sw1.shape[1]
    N = B * S
    KD = D // P
    GT = 4
    G = GT * P
    NG = N // G
    GB = NG // B
    NT = N // P
    R = P
    assert D == 4 * P and G == 512 and NG % 2 == 0 and GB % 2 == 0

    def grouped(ap):
        return ap.rearrange("(g t p) d -> g p t d", p=P, t=GT)

    x_groups = grouped(X.rearrange("b s d -> (b s) d"))
    out_groups = grouped(out.rearrange("b s d -> (b s) d"))
    x2_dram = nc.dram_tensor("x2_scratch", (N, D), F32, kind="Internal").ap()
    n3_dram = nc.dram_tensor("n3_scratch", (N, D), F32, kind="Internal").ap()
    KH = H // P
    NRT = 2 * NT + E
    r_dram = nc.dram_tensor("routed_scratch", ((NRT - 1) * P, D), F32, kind="Internal").ap()
    x2_groups, n3_groups = grouped(x2_dram), grouped(n3_dram)
    tok_groups = grouped(rope_tok)
    feat_groups = rope_feat.rearrange("c p (g t) -> g p c t", t=G)

    def col(ap):
        return ap.rearrange("(k p) -> p k", p=P)

    top = ExitStack()
    with top:
        def keep(name, shape, dt=F32):
            return top.enter_context(nc.sbuf_tensor(name, shape, dt))

        ident = keep("ident", [P, P])
        tops = keep("tops", [P, NT, 8])
        top_at = keep("top_at", [P, NT, 8], U32)

        attention(nc, locals())
        slots = keep("slots", [P, 2, NT], U32)
        picked = keep("picked", [P, 2, NT])
        gsrc = keep("gsrc", [P, NT, 32])
        gate_hi = keep("gate_hi", [P, NT, E], F32R)
        b2_mix = keep("b2_mix", [32, D], F32R)
        routed(nc, locals())
        combined(nc, locals())


def value(eng, x):
    return x if isinstance(x, int) else eng.snap(eng.to_reg(x))


def attention(nc, v):
    (B, S, D, E, KD, GT, G, NG, GB, NT, R) = (v[n] for n in "B S D E KD GT G NG GB NT R".split())
    x_groups, x2_groups, n3_groups = v["x_groups"], v["x2_groups"], v["n3_groups"]
    tok_groups, feat_groups, col = v["tok_groups"], v["feat_groups"], v["col"]
    ident, tops, top_at = v["ident"], v["tops"], v["top_at"]
    W_in, W_out, b_in = v["W_in"], v["W_out"], v["b_in"]

    with ExitStack() as ctx:
        def sb(name, shape, dt=F32, where=ctx):
            return where.enter_context(nc.sbuf_tensor(name, shape, dt))

        def sem(name):
            return ctx.enter_context(nc.semaphore(name))

        def bank(name):
            return ctx.enter_context(nc.psum_tensor(name, [P, 512], F32))

        mm = [bank(f"mm{i}") for i in range(4)]
        tp = [bank(f"tp{i}") for i in range(2)]
        gl = bank("gl")
        acol_ps = bank("acol_ps")

        wq_hi, wq_lo = sb("wq_hi", [P, KD, D], F32R), sb("wq_lo", [P, KD, D], F32R)
        wo_hi, wo_lo = sb("wo_hi", [P, B, KD, D], F32R), sb("wo_lo", [P, B, KD, D], F32R)
        gw = sb("gw", [P, KD, E])
        NSTAGE = 3
        stage = [sb(f"stage{i}", [P, D]) for i in range(NSTAGE)]
        lnw, lnb, bq = sb("lnw", [P, KD]), sb("lnb", [P, KD]), sb("bq", [P, KD])
        bkv, bo = sb("bkv", [P, 2, D]), sb("bo", [P, D])
        half = sb("half", [P, 8])
        ones = sb("ones", [P, 1])
        acc = sb("acc", [P, B, D])
        acol = sb("acol", [P, B, KD])

        xg = [sb(f"xg{i}", [P, GT, D]) for i in range(2)]
        hn = sb("hn", [P, GT, D])
        bst = sb("bst", [P, GT, 6])
        mv = [sb(f"mv{i}", [P, GT, 2]) for i in range(2)]
        vp = sb("vp", [P, 2, GT])
        rs = [sb(f"rs{i}", [P, 2, GT]) for i in range(2)]
        nm = [sb(f"nm{i}", [P, GT]) for i in range(2)]
        hb = [sb(f"hb{i}", [P, G]) for i in range(2)]
        h_hi = [sb(f"h_hi{i}", [P, KD, G], F32R) for i in range(2)]
        h_lo = [sb(f"h_lo{i}", [P, KD, G], F32R) for i in range(2)]

        with ExitStack() as first:
            wkv_hi = sb("wkv_hi", [P, 2, KD, D], F32R, first)
            wkv_lo = sb("wkv_lo", [P, 2, KD, D], F32R, first)
            rt = [sb(f"rt{i}", [P, GT, 2, R], where=first) for i in range(2)]
            kb = [sb(f"kb{i}", [P, D], where=first) for i in range(2)]
            vb = [sb(f"vb{i}", [P, D], where=first) for i in range(2)]
            sq = [sb(f"sq{i}", [P, D], where=first) for i in range(2)]
            ssq = [sb(f"ssq{i}", [P, 1], where=first) for i in range(2)]
            rn = [sb(f"rn{i}", [P, 1], where=first) for i in range(2)]
            rot = sb("rot", [P, 2, 2, R], where=first)
            prod = [sb(f"prod{i}", [P, D], where=first) for i in range(2)]
        rf = [sb(f"rf{i}", [P, 2, G]) for i in range(2)]
        qb = sb("qb", [P, KD, G])
        rc, rsn = sb("rc", [P, 2, G]), sb("rsn", [P, 2, G])
        q_hi, q_lo = sb("q_hi", [P, KD, G], F32R), sb("q_lo", [P, KD, G], F32R)
        n1 = sb("n1", [P, GT, D])
        z = sb("z", [P, GT, D])
        n3 = sb("n3", [P, GT, D])
        n3t = sb("n3t", [P, KD, G])
        zst, zmv = sb("zst", [P, GT, 6]), sb("zmv", [P, GT, 2])
        zv, zr, znm = sb("zv", [P, GT]), sb("zr", [P, GT]), sb("znm", [P, GT])
        xst, xmv = sb("xst", [P, GT, 6]), sb("xmv", [P, GT, 2])
        xv, xr, xnm = sb("xv", [P, GT]), sb("xr", [P, GT]), sb("xnm", [P, GT])
        lg = sb("lg", [P, GT, E])
        mx, mi = sb("mx", [P, GT, 8]), sb("mi", [P, GT, 8], U32)

        consts_in = sem("consts_in")
        half_set, ones_set = sem("half_set"), sem("ones_set")
        x_in = [sem(f"x_in{i}") for i in range(2)]
        rt_in = [sem(f"rt_in{i}") for i in range(2)]
        rf_in = [sem(f"rf_in{i}") for i in range(2)]
        raw_in = [sem(f"raw_in{i}") for i in range(NSTAGE)]
        w_hi_done, w_split = sem("w_hi_done"), sem("w_split")
        stats_done, aggr_done, var_ready, rs_ready = sem("stats_done"), sem("aggr_done"), sem("var_ready"), sem("rs_ready")
        nm_ready, h_normed = sem("nm_ready"), sem("h_normed")
        tp_full, tp_free = sem("tp_full"), sem("tp_free")
        h_hi_done, h_split = sem("h_hi_done"), sem("h_split")
        kv_full, kv_free = sem("kv_full"), sem("kv_free")
        k_parts, k_rotated = sem("k_parts"), sem("k_rotated")
        ssq_ready, rn_ready = sem("ssq_ready"), sem("rn_ready")
        prod_ready, acc_done = sem("prod_ready"), sem("acc_done")
        acol_full, acol_ready = sem("acol_full"), sem("acol_ready")
        a_over = sem("a_over")
        q_full, q_free = sem("q_full"), sem("q_free")
        q_biased = q_free
        q_cos, q_sin, q_rotated = sem("q_cos"), sem("q_sin"), sem("q_rotated")
        q_hi_done, q_split = sem("q_hi_done"), sem("q_split")
        n1_raw, n1_ready = sem("n1_raw"), sem("n1_ready")
        y_full, y_free = sem("y_full"), sem("y_free")
        zst_done, zmv_done, zv_ready, zr_ready, znm_ready, zn_ready = (
            sem("zst_done"), sem("zmv_done"), sem("zv_ready"), sem("zr_ready"), sem("znm_ready"), sem("zn_ready"))
        x2_ready, xst_done, xmv_done, xv_ready, xr_ready, xnm_ready, n3_ready = (
            sem("x2_ready"), sem("xst_done"), sem("xmv_done"), sem("xv_ready"), sem("xr_ready"), sem("xnm_ready"),
            sem("n3_ready"))
        x2_stored, n3_stored = sem("x2_stored"), sem("n3_stored")
        n3t_ready, gl_full, lg_ready, mx_ready, mi_ready, tops_kept = (
            sem("n3t_ready"), sem("gl_full"), sem("lg_ready"), sem("mx_ready"), sem("mi_ready"), sem("tops_kept"))

        chunks = [(W_in[k * P:(k + 1) * P, (1 + c) * D:(2 + c) * D], wkv_hi[:, c, k, :], wkv_lo[:, c, k, :], None)
                  for c in range(2) for k in range(KD)]
        N_KV = len(chunks)
        chunks += [(W_in[k * P:(k + 1) * P, 0:D], wq_hi[:, k, :], wq_lo[:, k, :], None) for k in range(KD)]
        N_Q = len(chunks)
        chunks += [(W_out[k * P:(k + 1) * P, :], wo_hi[:, b, k, :], wo_lo[:, b, k, :], (b, k))
                   for b in range(B) for k in range(KD)]
        N_ALL = len(chunks)
        NB_A = 4

        def turned(g):
            if isinstance(g, int) and g in (0, NG):
                return KD * (NG + 1) + (0 if g == 0 else 2 * KD * (NG - 1))
            return KD * NG + 2 * KD * g

        block = ctx.enter_context(nc.Block())

        @block.sync
        def _(sp):
            def load_chunk(n):
                if n >= NSTAGE:
                    sp.wait_ge(w_split, n - NSTAGE + 1)
                sp.dma_start(stage[n % NSTAGE][:, :], chunks[n][0]).then_inc(raw_in[n % NSTAGE], 16)

            sp.dma_start(xg[0][:, :, :], x_groups[0]).then_inc(x_in[0], 16)
            sp.dma_start(ident[:, :], v["identity"]).then_inc(consts_in, 16)
            sp.dma_start(lnw[:, :], v["ln_w"]).then_inc(consts_in, 16)
            sp.dma_start(lnb[:, :], v["ln_b"]).then_inc(consts_in, 16)
            for n in range(NSTAGE):
                load_chunk(n)
            sp.dma_start(bq[:, :], v["b_q"]).then_inc(consts_in, 16)
            sp.dma_start(bkv[:, :, :], b_in[D:3 * D].rearrange("(c d) -> c d", c=2).partition_broadcast(P))\
              .then_inc(consts_in, 16)
            sp.dma_start(bo[:, :], v["b_out"].partition_broadcast(P)).then_inc(consts_in, 16)
            sp.dma_start(gw[:, :, :], v["gate_w"].rearrange("(k p) e -> p k e", p=P)).then_inc(consts_in, 16)
            sp.dma_start(rt[0][:, :, :, :], tok_groups[0].rearrange("p t (c r) -> p t c r", c=2)).then_inc(rt_in[0], 16)
            for n in range(NSTAGE, N_KV):
                load_chunk(n)
            sp.dma_start(xg[1][:, :, :], x_groups[1]).then_inc(x_in[1], 16)
            sp.dma_start(rt[1][:, :, :, :], tok_groups[1 % GB].rearrange("p t (c r) -> p t c r", c=2))\
              .then_inc(rt_in[1], 16)
            with sp.Fori(1, NG // 2) as i:
                for u in range(2):
                    g = 2 * i + u
                    sp.wait_ge(h_normed, g - 1)
                    sp.dma_start(xg[u][:, :, :], x_groups[g]).then_inc(x_in[u], 16)
                    sp.wait_ge(k_rotated, GT * (g - 1))
                    sp.dma_start(rt[u][:, :, :, :], tok_groups[g % GB].rearrange("p t (c r) -> p t c r", c=2))\
                      .then_inc(rt_in[u], 16)
            for u in range(2):
                sp.wait_ge(h_normed, NG - 1 + u)
                sp.dma_start(xg[u][:, :, :], x_groups[u]).then_inc(x_in[u], 16)
            for n in range(N_KV, N_Q):
                load_chunk(n)
            sp.wait_ge(a_over, 4)
            for u in range(2):
                sp.dma_start(rf[u][:, :, :], feat_groups[u]).then_inc(rf_in[u], 16)
            for n in range(N_Q, N_ALL):
                load_chunk(n)

            def stores(g, u):
                sp.wait_ge(x2_ready, GT * (g + 1))
                sp.dma_start(x2_groups[g], z[:, :, :]).then_inc(x2_stored, 16)

            def store_n3(g):
                sp.wait_ge(n3_ready, GT * (g + 1))
                sp.dma_start(n3_groups[g], n3[:, :, :]).then_inc(n3_stored, 16)

            with sp.Fori(0, NG // 2 - 1) as i:
                for u in range(2):
                    g = 2 * i + u
                    stores(g, u)
                    sp.dma_start(xg[u][:, :, :], x_groups[g + 2]).then_inc(x_in[u], 16)
                    sp.wait_ge(q_sin, g + 1)
                    sp.wait_ge(q_cos, g + 1)
                    sp.dma_start(rf[u][:, :, :], feat_groups[(g + 2) % GB]).then_inc(rf_in[u], 16)
                    store_n3(g)
            for u in range(2):
                stores(NG - 2 + u, u)
                store_n3(NG - 2 + u)
            sp.wait_ge(x2_stored, 16 * (NG + 1))
            sp.wait_ge(n3_stored, 16 * (NG + 1))

        @block.vector
        def _(dve):
            def split(n):
                raw, (_, hi, lo, bk) = stage[n % NSTAGE], chunks[n]
                dve.wait_ge(w_hi_done, n + 1)
                if bk is None:
                    dve.tensor_tensor(lo, raw[:, :], hi.bitcast(F32), ALU.subtract).then_inc(w_split, 1)
                else:
                    b, k = bk
                    dve.scalar_tensor_tensor(lo, raw[:, :], acol[:, b, k:k + 1], hi.bitcast(F32),
                                             ALU.mult, ALU.subtract).then_inc(w_split, 1)

            def front_stats(f, u, loads):
                dve.wait_ge(x_in[u], 16 * loads)
                for j in range(GT):
                    last = dve.bn_stats(bst[:, j, :], xg[u][:, j, :])
                last.then_inc(stats_done, 1)
                need = value(dve, f + 1)
                dve.wait_ge(half_set, 1)
                dve.wait_ge(stats_done, need)
                for j in range(GT):
                    last = dve.bn_aggr(mv[u][:, j, :], bst[:, j, :])
                last.then_inc(aggr_done, 1)
                dve.wait_ge(aggr_done, f + 1)
                dve.tensor_scalar(vp[:, 0, :], mv[u][:, :, 1], 1.0 + EPS, EPS * EPS, ALU.mult, ALU.add)
                dve.tensor_scalar(vp[:, 1, :], mv[u][:, :, 1], EPS, None, ALU.add).then_inc(var_ready, 1)

            def front_norm(f, u):
                dve.wait_ge(rs_ready, f + 1)
                if not (isinstance(f, int) and f == 0):
                    dve.wait_ge(tp_full, tp_uses(f))
                for j in range(GT):
                    last = dve.tensor_scalar(hn[:, j, :], xg[u][:, j, :], mv[u][:, j, 0:1], rs[u][:, 0, j:j + 1],
                                             ALU.subtract, ALU.mult)
                last.then_inc(h_normed, 1)

            def tp_uses(f):
                return KD * f

            dve.sem_inc(kv_free, NB_A)
            dve.sem_inc(y_free, 2)
            dve.sem_inc(prod_ready, 2)
            dve.memset(half[:, :], -0.5).then_inc(half_set, 1)
            dve.memset(ones[:, :], 1.0).then_inc(ones_set, 1)
            front_stats(0, 0, 1)
            front_norm(0, 0)
            for n in range(N_KV):
                split(n)
            dve.wait_ge(consts_in, 16 * 7)

            def k_tile(g, u, j):
                t = GT * g + j
                dve.wait_ge(prod_ready, t + 1)
                dve.wait_ge(kv_full, 2 * t + 1)
                kj = kb[j % 2]
                dve.tensor_tensor(kj[:, :], mm[2 * j % NB_A][:, :], bkv[:, 0, :], ALU.add).then_inc(kv_free, 1)
                if j == 0:
                    dve.wait_ge(rt_in[u], 16 * (g // 2 + 1))
                dve.wait_ge(kv_free, NB_A + 2 * t + 1)
                pairs = kj[:, 0:2 * R].rearrange("p (h r) -> p h r", h=2)
                for c in range(2):
                    last = dve.tensor_tensor(rot[:, c, :, :], pairs,
                                             rt[u][:, j, c:c + 1, :].to_broadcast([P, 2, R]), ALU.mult)
                last.then_inc(k_parts, 1)
                dve.wait_ge(k_parts, t + 1)
                dve.tensor_tensor(kj[:, 0:R], rot[:, 0, 0, :], rot[:, 1, 1, :], ALU.subtract)
                dve.tensor_tensor(kj[:, R:2 * R], rot[:, 0, 1, :], rot[:, 1, 0, :], ALU.add).then_inc(k_rotated, 1)

            def v_tile(g, j):
                t = GT * g + j
                dve.wait_ge(kv_full, 2 * t + 2)
                dve.tensor_tensor(vb[j % 2][:, :], mm[(2 * j + 1) % NB_A][:, :], bkv[:, 1, :], ALU.add)\
                   .then_inc(kv_free, 1)

            def kv_prod(g, j):
                t = GT * g + j
                dve.wait_ge(rn_ready, t + 1)
                dve.wait_ge(kv_free, NB_A + 2 * t + 2)
                dve.wait_ge(acc_done, t + 1)
                dve.scalar_tensor_tensor(prod[j % 2][:, :], kb[j % 2][:, :], rn[j % 2][:, 0:1], vb[j % 2][:, :],
                                         ALU.mult, ALU.mult).then_inc(prod_ready, 1)

            with dve.Fori(0, NG // 2) as i:
                for u in range(2):
                    g = 2 * i + u
                    front_stats(g + 1, 1 - u, i + 1 + u)
                    k_tile(g, u, 0)
                    v_tile(g, 0)
                    k_tile(g, u, 1)
                    front_norm(g + 1, 1 - u)
                    kv_prod(g, 0)
                    v_tile(g, 1)
                    k_tile(g, u, 2)
                    kv_prod(g, 1)
                    v_tile(g, 2)
                    k_tile(g, u, 3)
                    kv_prod(g, 2)
                    v_tile(g, 3)
                    kv_prod(g, 3)
            dve.wait_ge(prod_ready, 2 + NT)
            dve.sem_inc(a_over, 1)

            for n in range(N_KV, N_Q):
                split(n)
            dve.wait_ge(acol_full, 1)
            dve.tensor_copy(acol[:, :, :], acol_ps[:, 0:B * KD].rearrange("p (b k) -> p b k", b=B))\
               .then_inc(acol_ready, 1)
            dve.wait_ge(a_over, 4)

            def rotate_q(g, u):
                dve.wait_ge(rf_in[u], 16 * (g // 2 + 1))
                dve.wait_ge(q_biased, 2 + KD * g + 2)
                dve.tensor_tensor(rc[:, :, :], qb[:, 0:2, :], rf[u][:, 0:1, :].to_broadcast([P, 2, G]), ALU.mult)\
                   .then_inc(q_cos, 1)
                dve.wait_ge(q_cos, g + 1)
                dve.wait_ge(q_sin, g + 1)
                dve.tensor_tensor(qb[:, 0, :], rc[:, 0, :], rsn[:, 1, :], ALU.subtract)
                dve.tensor_tensor(qb[:, 1, :], rc[:, 1, :], rsn[:, 0, :], ALU.add).then_inc(q_rotated, 1)

            def split_q(g):
                for n, h in enumerate((1, 0)):
                    dve.wait_ge(q_hi_done, 2 * g + n + 1)
                    s = slice(2 * h, 2 * h + 2)
                    dve.tensor_tensor(q_lo[:, s, :], qb[:, s, :], q_hi[:, s, :].bitcast(F32), ALU.subtract)\
                       .then_inc(q_split, 1)

            def token_tiles(g, u, js):
                for j in js:
                    if j == 0:
                        dve.wait_ge(x2_stored, 16 * (g + 1))
                        if not (isinstance(g, int) and g == 0):
                            dve.wait_ge(n3_ready, GT * g)
                    dve.wait_ge(y_full, GT * g + j + 1)
                    dve.wait_ge(n1_ready, GT * g + j + 1)
                    dve.tensor_tensor(z[:, j, :], mm[2 + j % 2][:, :], n1[:, j, :], ALU.add).then_inc(y_free, 1)
                    dve.wait_ge(y_free, 2 + GT * g + j + 1)
                    last = dve.bn_stats(zst[:, j, :], z[:, j, :])
                if js[-1] == GT - 1:
                    last.then_inc(zst_done, 1)

            def z_moments(g):
                need = value(dve, g + 1)
                dve.wait_ge(half_set, 1)
                dve.wait_ge(zst_done, need)
                for j in range(GT):
                    last = dve.bn_aggr(zmv[:, j, :], zst[:, j, :])
                last.then_inc(zmv_done, 1)
                dve.wait_ge(zmv_done, g + 1)
                dve.tensor_scalar(zv[:, :], zmv[:, :, 1], EPS, None, ALU.add).then_inc(zv_ready, 1)

            def z_shift(g):
                dve.wait_ge(zr_ready, g + 1)
                dve.scalar_tensor_tensor(znm[:, :], zmv[:, :, 0], -1.0, zr[:, :], ALU.mult, ALU.mult)\
                   .then_inc(znm_ready, 1)

            def x2_tiles(g, u):
                for j in range(GT):
                    dve.wait_ge(zn_ready, GT * g + j + 1)
                    dve.tensor_tensor(z[:, j, :], z[:, j, :], xg[u][:, j, :], ALU.add).then_inc(x2_ready, 1)
                    dve.wait_ge(x2_ready, GT * g + j + 1)
                    last = dve.bn_stats(xst[:, j, :], z[:, j, :])
                last.then_inc(xst_done, 1)
                need = value(dve, g + 1)
                dve.wait_ge(half_set, 1)
                dve.wait_ge(xst_done, need)
                for j in range(GT):
                    last = dve.bn_aggr(xmv[:, j, :], xst[:, j, :])
                last.then_inc(xmv_done, 1)
                dve.wait_ge(xmv_done, g + 1)
                dve.tensor_scalar(xv[:, :], xmv[:, :, 1], EPS, None, ALU.add).then_inc(xv_ready, 1)

            def x2_shift(g):
                dve.wait_ge(xr_ready, g + 1)
                dve.scalar_tensor_tensor(xnm[:, :], xmv[:, :, 0], -1.0, xr[:, :], ALU.mult, ALU.mult)\
                   .then_inc(xnm_ready, 1)

            def front_shift(f, u):
                dve.wait_ge(rs_ready, f + 1)
                dve.scalar_tensor_tensor(nm[u][:, :], mv[u][:, :, 0], -1.0, rs[u][:, 1, :], ALU.mult, ALU.mult)\
                   .then_inc(nm_ready, 1)

            def gate(g):
                dve.wait_ge(gl_full, g + 1)
                dve.tensor_copy(lg[:, :, :], gl[:, 0:GT * E].rearrange("p (t e) -> p t e", t=GT)).then_inc(lg_ready, 1)
                need = value(dve, g + 1)
                dve.wait_ge(half_set, 1)
                dve.wait_ge(lg_ready, need)
                for j in range(GT):
                    last = dve.max(mx[:, j, :], lg[:, j, :])
                last.then_inc(mx_ready, 1)
                need = value(dve, g + 1)
                dve.wait_ge(half_set, 1)
                dve.wait_ge(mx_ready, need)
                for j in range(GT):
                    last = dve.max_index(mi[:, j, :], mx[:, j, :], lg[:, j, :])
                last.then_inc(mi_ready, 1)
                dve.tensor_copy(tops[:, bass.ds(GT * g, GT), :], mx[:, :, :])
                dve.wait_ge(mi_ready, g + 1)
                dve.tensor_copy(top_at[:, bass.ds(GT * g, GT), :], mi[:, :, :]).then_inc(tops_kept, 1)

            front_shift(NG, 0)
            rotate_q(0, 0)
            split_q(0)
            for n in range(N_Q, N_ALL):
                split(n)

            def group(g, u, first=False, last=False):
                if not last:
                    front_stats(NG + g + 1, 1 - u, NG // 2 + 1 + (g + 1) // 2)
                token_tiles(g, u, [0])
                if not last:
                    dve.wait_ge(rs_ready, NG + g + 2)
                    for j in range(GT):
                        norm = dve.tensor_scalar(hn[:, j, :], xg[1 - u][:, j, :], mv[1 - u][:, j, 0:1],
                                                 rs[1 - u][:, 0, j:j + 1], ALU.subtract, ALU.mult)
                    norm.then_inc(h_normed, 1)
                    front_shift(NG + g + 1, 1 - u)
                token_tiles(g, u, [1, 2, 3])
                z_moments(g)
                if not first:
                    gate(g - 2)
                z_shift(g)
                x2_tiles(g, u)
                if not last:
                    rotate_q(g + 1, 1 - u)
                x2_shift(g)
                if not last:
                    split_q(g + 1)

            for g in range(2):
                group(g, g, first=True)
            with dve.Fori(1, NG // 2 - 1) as i:
                for u in range(2):
                    group(2 * i + u, u)
            group(NG - 2, 0)
            group(NG - 1, 1, last=True)
            gate(NG - 2)
            gate(NG - 1)

        @block.scalar
        def _(act):
            def hi_part(n):
                raw, (_, hi, _, bk) = stage[n % NSTAGE], chunks[n]
                act.wait_ge(raw_in[n % NSTAGE], 16 * (n // NSTAGE + 1))
                if bk is None:
                    act.activation(hi, raw[:, :], ACT.Copy).then_inc(w_hi_done, 1)
                else:
                    b, k = bk
                    act.wait_ge(acol_ready, 1)
                    act.activation(hi, raw[:, :], ACT.Identity, scale=acol[:, b, k:k + 1]).then_inc(w_hi_done, 1)

            def front_split(f, u, n0, reader=None):
                for k in range(KD):
                    act.wait_ge(tp_full, n0 + k + 1)
                    if not isinstance(f, int) or f > 0 or k >= 2:
                        act.wait_ge(h_split, KD * f + k - 1)
                    act.activation(hb[k % 2][:, :], tp[k % 2][:, :], ACT.Identity, bias=lnb[:, k:k + 1],
                                   scale=lnw[:, k:k + 1]).then_inc(tp_free, 1)
                    if k == 0 and reader is not None:
                        act.wait_ge(*reader)
                    act.wait_ge(tp_free, 2 + n0 + k + 1)
                    act.activation(h_hi[u][:, k, :], hb[k % 2][:, :], ACT.Copy).then_inc(h_hi_done, 1)

            act.sem_inc(tp_free, 2)
            act.sem_inc(q_free, 2)
            act.wait_ge(consts_in, 16 * 7)
            front_split(0, 0, 0)
            for n in range(N_KV):
                hi_part(n)

            def norm_k(g, j):
                t = GT * g + j
                act.wait_ge(k_rotated, t + 1)
                act.activation(sq[j % 2][:, :], kb[j % 2][:, :], ACT.Square, accum_out=ssq[j % 2][:, 0:1])\
                   .then_inc(ssq_ready, 1)

            with act.Fori(0, NG // 2) as i:
                for u in range(2):
                    g = 2 * i + u
                    norm_k(g, 0)
                    norm_k(g, 1)
                    norm_k(g, 2)
                    front_split(g + 1, 1 - u, KD * (g + 1), (kv_full, 2 * GT * g + 1))
                    norm_k(g, 3)
            act.wait_ge(ssq_ready, NT)
            act.sem_inc(a_over, 1)

            def bias_q(g, ms):
                for m in ms:
                    act.wait_ge(q_full, KD * g + m + 1)
                    act.activation(qb[:, m, :], mm[m % 2][:, :], ACT.Identity, bias=bq[:, m:m + 1]).then_inc(q_free, 1)

            def q_hi_parts(g):
                for h in (1, 0):
                    if h:
                        act.wait_ge(q_free, 2 + KD * (g + 1))
                    else:
                        act.wait_ge(q_rotated, g + 1)
                    s = slice(2 * h, 2 * h + 2)
                    act.activation(q_hi[:, s, :], qb[:, s, :], ACT.Copy).then_inc(q_hi_done, 1)

            def first_norm(g, u):
                act.wait_ge(nm_ready, g + 1)
                act.wait_ge(y_free, 2 + GT * g)
                for j in range(GT):
                    act.activation(n1[:, j, :], xg[u][:, j, :], ACT.Identity, bias=nm[u][:, j:j + 1],
                                   scale=rs[u][:, 1, j:j + 1]).then_inc(n1_raw, 1)

            def norm_z(g):
                act.wait_ge(znm_ready, g + 1)
                for j in range(GT):
                    act.activation(z[:, j, :], z[:, j, :], ACT.Identity, bias=znm[:, j:j + 1],
                                   scale=zr[:, j:j + 1]).then_inc(zn_ready, 1)

            def norm_x2(g):
                act.wait_ge(xnm_ready, g + 1)
                act.wait_ge(n3_stored, 16 * (g + 1))
                for j in range(GT):
                    act.activation(n3[:, j, :], z[:, j, :], ACT.Identity, bias=xnm[:, j:j + 1],
                                   scale=xr[:, j:j + 1]).then_inc(n3_ready, 1)

            def n3_columns(g, n0):
                for k in range(KD):
                    act.wait_ge(tp_full, n0 + k + 1)
                    act.activation(n3t[:, k, :], tp[k % 2][:, :], ACT.Copy).then_inc(tp_free, 1)

            for n in range(N_KV, N_Q):
                hi_part(n)
            act.wait_ge(a_over, 4)
            first_norm(0, 0)
            bias_q(0, range(KD))
            q_hi_parts(0)
            for n in range(N_Q, N_ALL):
                hi_part(n)

            def group(g, u, first=False, last=False):
                n0 = turned(g)
                if not last:
                    front_split(NG + g + 1, 1 - u, n0, (q_full, KD * g + 1))
                    n0 = n0 + KD
                if not first:
                    n3_columns(g - 1, n0)
                norm_z(g)
                if not last:
                    bias_q(g + 1, (0, 1))
                    first_norm(g + 1, 1 - u)
                    bias_q(g + 1, (2, 3))
                    q_hi_parts(g + 1)
                norm_x2(g)

            group(0, 0, first=True)
            with act.Fori(0, NG // 2 - 1) as i:
                for s in range(2):
                    group(2 * i + 1 + s, 1 - s)
            group(NG - 1, 1, last=True)
            n3_columns(NG - 1, turned(NG))

        @block.gpsimd
        def _(pool):
            def front_rs(f, u):
                pool.wait_ge(var_ready, f + 1)
                pool.tensor_tensor(rs[u][:, :, :], vp[:, :, :], half[:, 0:2 * GT].rearrange("p (c t) -> p c t", c=2),
                                   ALU.pow).then_inc(rs_ready, 1)

            def front_lo(f, u):
                for k in range(KD):
                    pool.wait_ge(h_hi_done, KD * f + k + 1)
                    pool.tensor_tensor(h_lo[u][:, k, :], hb[k % 2][:, :], h_hi[u][:, k, :].bitcast(F32), ALU.subtract)\
                        .then_inc(h_split, 1)

            for b in range(B):
                pool.memset(acc[:, b, :], 0.0).then_inc(acc_done, 1)
            pool.sem_inc(x2_stored, 16)
            pool.sem_inc(n3_stored, 16)
            pool.wait_ge(half_set, 1)
            front_rs(0, 0)
            front_lo(0, 0)

            def rnorm(g, j):
                pool.wait_ge(ssq_ready, GT * g + j + 1)
                pool.tensor_tensor(rn[j % 2][:, :], ssq[j % 2][:, :], half[:, 0:1], ALU.pow).then_inc(rn_ready, 1)

            def accumulate(g, j):
                t = GT * g + j
                pool.wait_ge(prod_ready, 2 + t + 1)
                need = value(pool, B + t)
                offset = value(pool, g // GB)
                a = acc[:, bass.ds(offset, 1), :]
                pool.wait_ge(half_set, 1)
                pool.wait_ge(acc_done, need)
                pool.tensor_tensor(a, a, prod[j % 2][:, :].rearrange("p (o d) -> p o d", o=1), ALU.add)\
                    .then_inc(acc_done, 1)

            with pool.Fori(0, NG // 2) as i:
                for u in range(2):
                    g = 2 * i + u
                    front_rs(g + 1, 1 - u)
                    rnorm(g, 0)
                    rnorm(g, 1)
                    accumulate(g, 0)
                    rnorm(g, 2)
                    accumulate(g, 1)
                    front_lo(g + 1, 1 - u)
                    rnorm(g, 3)
                    accumulate(g, 2)
                    accumulate(g, 3)
            pool.wait_ge(acc_done, B + NT)
            pool.sem_inc(a_over, 1)
            pool.wait_ge(a_over, 4)

            def q_times_sin(g, u):
                pool.wait_ge(rf_in[u], 16 * (g // 2 + 1))
                pool.wait_ge(q_biased, 2 + KD * g + 2)
                if not isinstance(g, int) or g > 0:
                    pool.wait_ge(q_rotated, g)
                pool.tensor_tensor(rsn[:, :, :], qb[:, 0:2, :], rf[u][:, 1:2, :].to_broadcast([P, 2, G]), ALU.mult)\
                    .then_inc(q_sin, 1)

            def add_b_out(g):
                for j in range(GT):
                    pool.wait_ge(n1_raw, GT * g + j + 1)
                    pool.tensor_tensor(n1[:, j, :], n1[:, j, :], bo[:, :], ALU.add).then_inc(n1_ready, 1)

            def token_rsqrt(dst, src, need, ready, g):
                pool.wait_ge(need, g + 1)
                pool.tensor_tensor(dst[:, :], src[:, :], half[:, 0:GT], ALU.pow).then_inc(ready, 1)

            q_times_sin(0, 0)
            add_b_out(0)

            def group(g, u, last):
                if not last:
                    front_rs(NG + g + 1, 1 - u)
                    front_lo(NG + g + 1, 1 - u)
                token_rsqrt(zr, zv, zv_ready, zr_ready, g)
                if not last:
                    q_times_sin(g + 1, 1 - u)
                token_rsqrt(xr, xv, xv_ready, xr_ready, g)
                if not last:
                    add_b_out(g + 1)

            with pool.Fori(0, NG // 2 - 1) as i:
                for u in range(2):
                    group(2 * i + u, u, False)
            for u in range(2):
                group(NG - 2 + u, u, u == 1)

        @block.tensor
        def _(pe):
            def transposes(src, n0):
                for k in range(KD):
                    pe.wait_ge(tp_free, n0 + k + 1)
                    for j in range(GT):
                        last = pe.transpose(tp[k % 2][:, j * P:(j + 1) * P], src[:, j, k * P:(k + 1) * P], ident[:, :])
                    last.then_inc(tp_full, 1)

            def product(dst, hi, lo, w_hi, w_lo):
                for k in range(KD):
                    pe.matmul(dst, hi(k), w_hi(k), start=(k == 0), stop=False)
                    pe.matmul(dst, hi(k), w_lo(k), start=False, stop=False)
                    last = pe.matmul(dst, lo(k), w_hi(k), start=False, stop=(k == KD - 1))
                return last

            pe.wait_ge(consts_in, 16 * 7)
            pe.wait_ge(h_normed, 1)
            transposes(hn, 0)

            def kv(g, u, j, c):
                n = 2 * (GT * g + j) + c
                s = slice(j * P, (j + 1) * P)
                pe.wait_ge(kv_free, n + 1)
                product(mm[(2 * j + c) % NB_A][:, :], lambda k: h_hi[u][:, k, s], lambda k: h_lo[u][:, k, s],
                        lambda k: wkv_hi[:, c, k, :], lambda k: wkv_lo[:, c, k, :]).then_inc(kv_full, 1)

            pe.wait_ge(w_split, KD)
            with pe.Fori(0, NG // 2) as i:
                for u in range(2):
                    g = 2 * i + u
                    pe.wait_ge(h_split, KD * (g + 1))
                    for j in range(GT):
                        if j == 3:
                            pe.wait_ge(h_normed, g + 2)
                            transposes(hn, KD * (g + 1))
                        kv(g, u, j, 0)
                        if u == 0 and j == 0:
                            pe.wait_ge(w_split, N_KV)
                        kv(g, u, j, 1)
            pe.sem_inc(a_over, 1)

            pe.wait_ge(ones_set, 1)
            pe.wait_ge(acc_done, B + NT)
            for b in range(B):
                for k in range(KD):
                    n = b * KD + k
                    last = pe.matmul(acol_ps[:, n:n + 1], acc[:, b, k * P:(k + 1) * P], ones[:, :],
                                     start=True, stop=True)
            last.then_inc(acol_full, 1)

            def q(g, u):
                for m in range(KD):
                    pe.wait_ge(q_free, KD * g + m + 1)
                    if m == 0:
                        pe.wait_ge(h_split, KD * (NG + g + 1))
                    s = slice(m * P, (m + 1) * P)
                    product(mm[m % 2][:, :], lambda k: wq_hi[:, k, s], lambda k: wq_lo[:, k, s],
                            lambda k: h_hi[u][:, k, :], lambda k: h_lo[u][:, k, :]).then_inc(q_full, 1)

            def y(g, js):
                pe.wait_ge(q_split, 2 * (g + 1))
                for j in js:
                    pe.wait_ge(y_free, GT * g + j + 1)
                    s = slice(j * P, (j + 1) * P)
                    b = g // GB
                    w = lambda t, k: t[:, bass.ds(b, 1), k, :].rearrange("p o d -> p (o d)")
                    product(mm[2 + j % 2][:, :], lambda k: q_hi[:, k, s], lambda k: q_lo[:, k, s],
                            lambda k: w(wo_hi, k), lambda k: w(wo_lo, k)).then_inc(y_full, 1)

            def n3_turn(g, n0):
                pe.wait_ge(n3_ready, GT * (g + 1))
                transposes(n3, n0)

            def gate(g, n0):
                pe.wait_ge(tp_free, 2 + n0 + KD)
                if not isinstance(g, int) or g > 0:
                    pe.wait_ge(lg_ready, g)
                for j in range(GT):
                    for k in range(KD):
                        last = pe.matmul(gl[:, j * E:(j + 1) * E], n3t[:, k, j * P:(j + 1) * P], gw[:, k, :],
                                         start=(k == 0), stop=(k == KD - 1))
                last.then_inc(gl_full, 1)

            pe.wait_ge(w_split, N_Q)
            q(0, 0)
            pe.wait_ge(w_split, N_ALL)

            def group(g, u, first=False, last=False):
                n0 = turned(g)
                y(g, (0, 1))
                if not last:
                    pe.wait_ge(h_normed, NG + g + 2)
                    transposes(hn, n0)
                    n0 = n0 + KD
                y(g, (2, 3))
                if not first:
                    n3_turn(g - 1, n0)
                if not last:
                    q(g + 1, 1 - u)
                if not first:
                    gate(g - 1, n0)

            group(0, 0, first=True)
            with pe.Fori(0, NG // 2 - 1) as i:
                for s in range(2):
                    group(2 * i + 1 + s, 1 - s)
            group(NG - 1, 1, last=True)
            n3_turn(NG - 1, turned(NG))
            gate(NG - 1, turned(NG))


def routed(nc, v):
    (D, E, H, SH, KD, GT, NG, NT, NRT, KH) = (v[n] for n in "D E H SH KD GT NG NT NRT KH".split())
    ident, tops, top_at, gsrc, slots, picked = (v[n] for n in "ident tops top_at gsrc slots picked".split())
    b2_mix = v["b2_mix"]
    n3_dram, r_dram = v["n3_dram"], v["r_dram"]
    with ExitStack() as ctx:
        def sb(name, shape, dt=F32):
            return ctx.enter_context(nc.sbuf_tensor(name, shape, dt))

        def sem(name):
            return ctx.enter_context(nc.semaphore(name))

        xt_ps, th_ps, h_ps, o_ps = ([ctx.enter_context(nc.psum_tensor(f"{n}{i}", [P, 512], F32)) for i in range(2)]
                                    for n in ("xt_ps", "th_ps", "h_ps", "o_ps"))
        rank_ps, total_ps, ids_ps = h_ps[0], h_ps[1], o_ps[0]
        w1_hi, w1_lo = sb("w1_hi", [P, E, KD, H], F32R), sb("w1_lo", [P, E, KD, H], F32R)
        w2_hi, w2_lo = sb("w2_hi", [P, E, KH, D], F32R), sb("w2_lo", [P, E, KH, D], F32R)
        NST = 4
        NX = 4
        HT = 4
        CH = D
        raw = [sb(f"raw{i}", [P, CH]) for i in range(NST)]

        def flat(t, e, ks):
            return t[:, e, ks, :].rearrange("p k h -> p (k h)")

        chunks = []
        for e in range(E):
            for src, hi, lo, K_, per in ((v["w1"], w1_hi, w1_lo, KD, CH // H), (v["w2"], w2_hi, w2_lo, KH, CH // D)):
                for k in range(0, K_, per):
                    ks = slice(k, k + per)
                    chunks.append((src[e].rearrange("(k p) h -> p k h", p=P)[:, ks, :], flat(hi, e, ks), flat(lo, e, ks)))
        NC = len(chunks)

        b1_mix = sb("b1_mix", [2, E * H], F32R)
        ones_r = sb("ones_r", [2, P], F32R)
        owner, ids = sb("owner", [P, NRT], I32), sb("ids", [P, NRT], U32)
        g1, g2 = picked[:, 0, :], picked[:, 1, :]

        with ExitStack() as early:
            def eb(name, shape, dt=F32):
                return early.enter_context(nc.sbuf_tensor(name, shape, dt))

            b1_raw, b2_raw = eb("b1_raw", [2, E * H]), eb("b2_raw", [32, D])
            sel1, sel2 = eb("sel1", [2, 2]), eb("sel2", [32, 2])
            ones_f, upper = eb("ones_f", [P, P]), eb("upper", [P, P])
            at_f = eb("at_f", [P, NT, 2])
            iota_e, iota_a, iota_q = eb("iota_e", [P, E]), eb("iota_a", [P, NRT]), eb("iota_q", [P, P])
            iota_c, token = eb("iota_c", [P, NT]), eb("token", [P, NT])
            m1, m2, ms, mk = (eb(n, [P, E, NT]) for n in ("m1", "m2", "ms", "mk"))
            total, upto, slot, more = (eb(n, [P, E, NT]) for n in ("total", "upto", "slot", "more"))
            tiles, tiles_to, base, one_e = (eb(n, [P, E]) for n in ("tiles", "tiles_to", "base", "one_e"))
            slot_f, slot_i = eb("slot_f", [P, 2, NT]), eb("slot_i", [P, 2, NT], I32)
            a_i, q_i = eb("a_i", [P, 2, NT], I32), eb("q_i", [P, 2, NT], I32)
            a_f, q_f = eb("a_f", [P, 2, NT]), eb("q_f", [P, 2, NT])
            owner_cmp, owner_f = eb("owner_cmp", [P, NRT, E]), eb("owner_f", [P, NRT])
            hot_q, hot_a = [[eb(f"{n}{i}", [P, HT, w], F32R) for i in range(2)] for n, w in (("hot_q", P), ("hot_a", NRT))]
            zero_q, zero_a = eb("zero_q", [P, P], F32R), eb("zero_a", [P, NRT], F32R)
            gd, gm = eb("gd", [P, NT]), eb("gm", [P, NT, E])
        idx = [sb(f"idx{i}", [P, 1], U32) for i in range(NX)]
        xr = [sb(f"xr{i}", [P, D]) for i in range(NX)]
        x_hi, x_lo = [[sb(f"{n}{i}", [P, D], F32R) for i in range(2)] for n in ("x_hi", "x_lo")]
        hg = [sb(f"hg{i}", [P, H]) for i in range(2)]
        g_hi, g_lo = [[sb(f"{n}{i}", [P, H], F32R) for i in range(2)] for n in ("g_hi", "g_lo")]
        ro = [sb(f"ro{i}", [P, D]) for i in range(2)]

        raw_in = [sem(f"wraw_in{i}") for i in range(NST)]
        w_hi_done, w_split = sem("ww_hi_done"), sem("ww_split")
        small_in, zeros_set, iotas_set, step = sem("small_in"), sem("zeros_set"), sem("iotas_set"), sem("route_step")
        marks_ready, counts_full, slots_known, gap_ready, exp_ready = (
            sem("marks_ready"), sem("counts_full"), sem("slots_known"), sem("gap_ready"), sem("exp_ready"))
        hot_marked, hot_ready, hot_used, ids_full, ids_ready, owner_ready = (
            sem("hot_marked"), sem("hot_ready"), sem("hot_used"), sem("ids_full"), sem("ids_ready"), sem("owner_ready"))
        idx_set, row_in, may_gather = sem("idx_set"), [sem(f"row_in{i}") for i in range(NX)], sem("may_gather")
        xt_full, xt_free, x_hi_done = sem("xt_full"), sem("xt_free"), sem("x_hi_done")
        h_full, h_free = sem("h_full"), sem("h_free")
        th_full, th_free, g_hi_done = sem("th_full"), sem("th_free"), sem("g_hi_done")
        o_full, o_free = sem("o_full"), sem("o_free")
        r_stored = [sem(f"r_stored{i}") for i in range(2)]
        PRE = NRT - 2

        block = ctx.enter_context(nc.Block())

        @block.sync
        def _(sp):
            def load_chunk(n):
                if n >= NST:
                    sp.wait_ge(w_split, n - NST + 1)
                src = chunks[n][0]
                sp.dma_start(raw[n % NST][:, :].rearrange("p (k h) -> p k h", k=src.shape[1]), src)\
                  .then_inc(raw_in[n % NST], 16)

            for n in range(NST):
                load_chunk(n)
            b1_row = v["b1"].rearrange("e h -> (e h)").partition_broadcast(2)
            sb2_row = v["sb2"].partition_broadcast(2)
            sp.dma_start(b1_raw[:, :], b1_row).then_inc(small_in, 16)
            sp.wait_ge(zeros_set, 1)
            for r in range(3):
                sp.dma_start(b2_raw[r * E:(r + 1) * E, :], v["b2"]).then_inc(small_in, 16)
            sp.dma_start(b2_raw[3 * E:3 * E + 2, :], sb2_row).then_inc(small_in, 16)
            sp.dma_start(sel1[:, :], v["identity"][0:2, 0:2]).then_inc(small_in, 16)
            sp.dma_start(sel2[:, :], v["bias_parts"]).then_inc(small_in, 16)
            sp.dma_start(upper[:, :], v["before"]).then_inc(small_in, 16)
            for n in range(NST, NC):
                load_chunk(n)

            def store(i, u):
                sp.wait_ge(o_free, 2 + i + 1)
                sp.dma_start(r_dram[bass.ds(i * P, P), :], ro[u][:, :]).then_inc(r_stored[u], 16)

            with sp.Fori(0, NRT // 2 - 1) as n:
                for u in range(2):
                    store(2 * n + u, u)
            store(NRT - 2, 0)
            sp.wait_ge(r_stored[0], 16 * (NRT // 2 + 1))
            sp.wait_ge(r_stored[1], 16 * (NRT // 2))

        @block.vector
        def _(dve):
            count = [0]

            def done(ins):
                count[0] += 1
                ins.then_inc(step, 1)
                dve.wait_ge(step, count[0])

            def bc(ap, shape):
                return ap.to_broadcast(shape)

            def by_expert(ap):
                return bc(ap.rearrange("p (e o) -> p e o", o=1), [P, E, NT])

            dve.memset(b2_raw[:, :], 0.0).then_inc(zeros_set, 1)
            dve.memset(zero_q[:, :].bitcast(F32), 0.0)
            dve.memset(zero_a[:, :].bitcast(F32), 0.0)
            dve.memset(ones_r[:, :].bitcast(F32), 1.0)
            dve.memset(ones_f[:, :], 1.0)
            dve.memset(one_e[:, :], 1.0)
            dve.memset(gsrc[:, :, :], 0.0)
            done(dve.memset(mk[:, :, :], 1.0))
            dve.memset(mk[:, :, 0:1], 0.0)
            dve.memset(gsrc[:, :, 3 * E:3 * E + 2], 1.0)
            done(dve.tensor_copy(at_f[:, :, :], top_at[:, :, 0:2]))
            dve.wait_ge(iotas_set, 5)
            for m, c in ((m1, 0), (m2, 1)):
                at = at_f[:, :, c].rearrange("p (o t) -> p o t", o=1)
                last = dve.tensor_tensor(m[:, :, :], by_expert(iota_e[:, :]), bc(at, [P, E, NT]), ALU.is_equal)
            done(last)
            dve.tensor_tensor(ms[:, :, :], m1[:, :, :], m2[:, :, :], ALU.add).then_inc(marks_ready, 1)
            dve.tensor_tensor(gd[:, :], tops[:, :, 1], tops[:, :, 0], ALU.subtract).then_inc(gap_ready, 1)
            dve.wait_ge(small_in, 16 * 8)
            for mix, raw_, sel in ((b1_mix[:, :], b1_raw[:, :], sel1), (b2_mix[:, :], b2_raw[:, :], sel2)):
                done(dve.tensor_copy(mix, raw_))
                done(dve.tensor_tensor(raw_, raw_, mix.bitcast(F32), ALU.subtract))
                done(dve.tensor_scalar(mix, mix.bitcast(F32), sel[:, 0:1], None, ALU.mult))
                done(dve.scalar_tensor_tensor(mix, raw_, sel[:, 1:2], mix.bitcast(F32), ALU.mult, ALU.add))
            dve.wait_ge(counts_full, 1)
            done(dve.tensor_copy(total[:, :, :], total_ps[:, 0:E * NT].rearrange("p (e t) -> p e t", e=E)))
            done(dve.tensor_tensor_scan(upto[:, :, :].rearrange("p e t -> p (e t)"),
                                        mk[:, :, :].rearrange("p e t -> p (e t)"),
                                        total[:, :, :].rearrange("p e t -> p (e t)"), 0.0, ALU.mult, ALU.add))
            done(dve.tensor_tensor(more[:, :, :], bc(upto[:, :, NT - 1:NT], [P, E, NT]),
                                   bc(iota_c[:, :].rearrange("p (o t) -> p o t", o=1), [P, E, NT]), ALU.is_gt))
            done(dve.tensor_reduce(tiles[:, :], more[:, :, :], AX.X, ALU.add))
            done(dve.tensor_tensor_scan(tiles_to[:, :], one_e[:, :], tiles[:, :], 0.0, ALU.mult, ALU.add))
            done(dve.tensor_tensor(base[:, :], tiles_to[:, :], tiles[:, :], ALU.subtract))
            dve.tensor_tensor(upto[:, :, :], upto[:, :, :], total[:, :, :], ALU.subtract)
            done(dve.tensor_scalar(base[:, :], base[:, :], float(P), None, ALU.mult))
            done(dve.tensor_tensor(slot[:, :, :], rank_ps[:, 0:E * NT].rearrange("p (e t) -> p e t", e=E),
                                   upto[:, :, :], ALU.add))
            done(dve.tensor_tensor(slot[:, :, :], slot[:, :, :], by_expert(base[:, :]), ALU.add))
            dve.tensor_tensor(ms[:, :, :], m1[:, :, :], slot[:, :, :], ALU.mult)
            done(dve.tensor_tensor(upto[:, :, :], m2[:, :, :], slot[:, :, :], ALU.mult))
            dve.tensor_reduce(slot_f[:, 0, :], ms[:, :, :].rearrange("p e t -> p t e"), AX.X, ALU.add)
            done(dve.tensor_reduce(slot_f[:, 1, :], upto[:, :, :].rearrange("p e t -> p t e"), AX.X, ALU.add))
            dve.tensor_copy(slots[:, :, :], slot_f[:, :, :])
            done(dve.tensor_copy(slot_i[:, :, :], slot_f[:, :, :]))
            dve.tensor_scalar(a_i[:, :, :], slot_i[:, :, :], 7, None, ALU.arith_shift_right)
            done(dve.tensor_scalar(q_i[:, :, :], slot_i[:, :, :], P - 1, None, ALU.bitwise_and))
            dve.tensor_copy(a_f[:, :, :], a_i[:, :, :])
            done(dve.tensor_copy(q_f[:, :, :], q_i[:, :, :]))
            done(dve.tensor_tensor(owner_cmp[:, :, :], bc(iota_a[:, :].rearrange("p (a o) -> p a o", o=1), [P, NRT, E]),
                                   bc(tiles_to[:, :].rearrange("p (o e) -> p o e", o=1), [P, NRT, E]), ALU.is_ge))
            done(dve.tensor_reduce(owner_f[:, :], owner_cmp[:, :, :], AX.X, ALU.add))
            dve.tensor_scalar(owner[:, :], owner_f[:, :], float(E - 1), None, ALU.min).then_inc(owner_ready, 1)
            dve.sem_inc(hot_used, 2)

            def along(x, w):
                return bc(x.rearrange("p (t o) -> p t o", o=1), [P, HT, w])

            def per_tile(x, w):
                return bc(x.rearrange("p (o w) -> p o w", o=1), [P, HT, w])

            with dve.Fori(0, NT // HT) as t:
                ts = bass.ds(HT * t, HT)
                for c in range(2):
                    dve.wait_ge(hot_used, 2 * t + c + 1)
                    dve.tensor_tensor(hot_a[c][:, :, :], per_tile(iota_a[:, :], NRT), along(a_f[:, c, ts], NRT),
                                      ALU.is_equal).then_inc(hot_marked, 1)
                    dve.tensor_tensor(hot_q[c][:, :, :], per_tile(iota_q[:, :], P), along(q_f[:, c, ts], P), ALU.is_equal)
                    dve.wait_ge(hot_marked, 2 * t + c + 1)
                    dve.tensor_tensor(hot_a[c][:, :, :], hot_a[c][:, :, :].bitcast(F32), along(token[:, ts], NRT),
                                      ALU.mult).then_inc(hot_ready, 1)
            dve.wait_ge(exp_ready, 1)
            done(dve.tensor_scalar(g2, gd[:, :], 1.0, None, ALU.add))
            done(dve.reciprocal(g1, g2))
            done(dve.tensor_tensor(g2, gd[:, :], g1, ALU.mult))
            by_token = lambda m: m[:, :, :].rearrange("p e t -> p t e")
            spread = lambda x: bc(x.rearrange("p (t o) -> p t o", o=1), [P, NT, E])
            dve.tensor_tensor(gm[:, :, :], by_token(m1), spread(g1), ALU.mult)
            done(dve.tensor_tensor(owner_cmp[:, 0:NT, :], by_token(m2), spread(g2), ALU.mult))
            done(dve.tensor_tensor(gm[:, :, :], gm[:, :, :], owner_cmp[:, 0:NT, :], ALU.add))
            done(dve.tensor_copy(v["gate_hi"][:, :, :], gm[:, :, :]))
            dve.tensor_copy(gsrc[:, :, 0:E], v["gate_hi"][:, :, :].bitcast(F32))
            dve.tensor_copy(gsrc[:, :, 2 * E:3 * E], v["gate_hi"][:, :, :].bitcast(F32))
            dve.tensor_tensor(gsrc[:, :, E:2 * E], gm[:, :, :], v["gate_hi"][:, :, :].bitcast(F32), ALU.subtract)
            dve.wait_ge(ids_full, 1)
            dve.tensor_copy(ids[:, :], ids_ps[:, 0:NRT]).then_inc(ids_ready, 1)

            def x_lo_part(i, u):
                dve.wait_ge(x_hi_done, i + 1)
                dve.tensor_tensor(x_lo[u][:, :], xt_ps[u][:, :], x_hi[u][:, :].bitcast(F32), ALU.subtract)\
                   .then_inc(xt_free, 1)

            def g_lo_part(i, u):
                dve.wait_ge(g_hi_done, i + 1)
                dve.tensor_tensor(g_lo[u][:, :], th_ps[u][:, 0:H], g_hi[u][:, :].bitcast(F32), ALU.subtract)\
                   .then_inc(th_free, 1)

            def o_out(i, u):
                dve.wait_ge(r_stored[u], 16 * (i // 2 + 1))
                dve.wait_ge(o_full, i + 1)
                dve.tensor_copy(ro[u][:, :], o_ps[u][:, :]).then_inc(o_free, 1)

            x_lo_part(0, 0)
            x_lo_part(1, 1)
            with dve.Fori(0, PRE // 2) as n:
                for s in range(2):
                    i, u = 2 * n + 1 + s, (1 + s) % 2
                    g_lo_part(i - 1, 1 - u)
                    x_lo_part(i + 1, 1 - u)
                    o_out(i - 1, 1 - u)
            g_lo_part(PRE, PRE % 2)
            o_out(PRE, PRE % 2)

        @block.scalar
        def _(act):
            def hi_part(n):
                act.wait_ge(raw_in[n % NST], 16 * (n // NST + 1))
                act.activation(chunks[n][1], raw[n % NST][:, :], ACT.Copy).then_inc(w_hi_done, 1)

            act.sem_inc(h_free, 2)
            act.wait_ge(gap_ready, 1)
            act.activation(gd[:, :], gd[:, :], ACT.Exp).then_inc(exp_ready, 1)
            for n in range(NC):
                hi_part(n)

            def x_hi_part(i, u):
                act.wait_ge(xt_full, i + 1)
                act.activation(x_hi[u][:, :], xt_ps[u][:, :], ACT.Copy).then_inc(x_hi_done, 1)

            def gelu(i, u):
                act.wait_ge(h_full, i + 1)
                act.activation(hg[u][:, :], h_ps[u][:, 0:H], ACT.Gelu).then_inc(h_free, 1)

            def g_hi_part(i, u):
                act.wait_ge(th_full, i + 1)
                act.activation(g_hi[u][:, :], th_ps[u][:, 0:H], ACT.Copy).then_inc(g_hi_done, 1)

            x_hi_part(0, 0)
            x_hi_part(1, 1)
            gelu(0, 0)
            with act.Fori(0, PRE // 2) as n:
                for s in range(2):
                    i, u = 2 * n + 1 + s, (1 + s) % 2
                    g_hi_part(i - 1, 1 - u)
                    x_hi_part(i + 1, 1 - u)
                    gelu(i, u)
            g_hi_part(PRE, PRE % 2)

        @block.gpsimd
        def _(pool):
            small = dict(allow_small_or_imprecise_dtypes=True)
            pool.iota(iota_e[:, :], [[1, E]], base=0, channel_multiplier=0, **small).then_inc(iotas_set, 1)
            pool.iota(iota_a[:, :], [[1, NRT]], base=0, channel_multiplier=0, **small).then_inc(iotas_set, 1)
            pool.iota(iota_q[:, :], [[1, P]], base=0, channel_multiplier=0, **small).then_inc(iotas_set, 1)
            pool.iota(iota_c[:, :], [[P, NT]], base=0, channel_multiplier=0, **small).then_inc(iotas_set, 1)
            pool.iota(token[:, :], [[P, NT]], base=0, channel_multiplier=1, **small).then_inc(iotas_set, 1)
            pool.sem_inc(r_stored[0], 16)
            pool.sem_inc(r_stored[1], 16)
            for n, (_, hi, lo) in enumerate(chunks):
                pool.wait_ge(w_hi_done, n + 1)
                pool.tensor_tensor(lo, raw[n % NST][:, :], hi.bitcast(F32), ALU.subtract).then_inc(w_split, 1)
            pool.wait_ge(ids_ready, 1)

            def gather(i, u):
                pool.tensor_copy(idx[u][:, :], ids[:, bass.ds(i, 1)]).then_inc(idx_set, 1)
                pool.wait_ge(idx_set, i + 1)
                pool.sem_inc(may_gather, 1)
                pool.indirect_dma_start(xr[u][:, :], None, n3_dram,
                                        bass.IndirectOffsetOnAxis(idx[u][:, 0:1], 0)).then_inc(row_in[u], 16)

            for i in range(NX):
                gather(i, i)
            with pool.Fori(1, NRT // NX) as n:
                for u in range(NX):
                    i = NX * n + u
                    pool.wait_ge(xt_full, i - NX + 1)
                    pool.sem_inc(may_gather, 1)
                    gather(i, u)

        @block.tensor
        def _(pe):
            pe.wait_ge(small_in, 16 * 8)
            pe.wait_ge(marks_ready, 1)
            marks = ms[:, :, :].rearrange("p e t -> p (e t)")
            pe.matmul(rank_ps[:, 0:E * NT], upper[:, :], marks, start=True, stop=True)
            pe.matmul(total_ps[:, 0:E * NT], ones_f[:, :], marks, start=True, stop=True).then_inc(counts_full, 1)
            pe.matmul(ids_ps[:, 0:NRT], zero_q[:, :], zero_a[:, :], start=True, stop=False)
            with pe.Fori(0, NT // HT) as t:
                for c in range(2):
                    pe.wait_ge(hot_ready, 2 * t + c + 1)
                    for j in range(HT):
                        last = pe.matmul(ids_ps[:, 0:NRT], hot_q[c][:, j, :], hot_a[c][:, j, :], start=False, stop=False)
                    last.then_inc(hot_used, 1)
            pe.matmul(ids_ps[:, 0:NRT], zero_q[:, :], zero_a[:, :], start=False, stop=True).then_inc(ids_full, 1)

            def x_turn(i, u, c):
                pe.wait_ge(row_in[c], 16 * (i // NX + 1))
                if not isinstance(i, int) or i >= 2:
                    pe.wait_ge(xt_free, i - 1)
                for k in range(KD):
                    last = pe.transpose(xt_ps[u][:, k * P:(k + 1) * P], xr[c][:, k * P:(k + 1) * P], ident[:, :])
                last.then_inc(xt_full, 1)

            def h_of(i, u, e):
                pe.wait_ge(xt_free, i + 1)
                pe.wait_ge(h_free, i + 1)
                out = h_ps[u][:, 0:H]
                w = lambda t, k: t[:, bass.ds(e, 1), k, :].rearrange("p o h -> p (o h)")
                for k in range(KD):
                    s = slice(k * P, (k + 1) * P)
                    pe.matmul(out, x_hi[u][:, s], w(w1_hi, k), start=(k == 0), stop=False)
                    pe.matmul(out, x_hi[u][:, s], w(w1_lo, k), start=False, stop=False)
                    pe.matmul(out, x_lo[u][:, s], w(w1_hi, k), start=False, stop=False)
                pe.matmul(out, ones_r[:, :], b1_mix[:, bass.ds(e * H, H)], start=False, stop=True).then_inc(h_full, 1)

            def h_turn(i, u):
                pe.wait_ge(h_free, 2 + i + 1)
                pe.wait_ge(th_free, i + 1)
                for k in range(KH):
                    last = pe.transpose(th_ps[u][:, k * P:(k + 1) * P], hg[u][:, k * P:(k + 1) * P], ident[:, :])
                last.then_inc(th_full, 1)

            def o_of(i, u, e):
                pe.wait_ge(th_free, 2 + i + 1)
                pe.wait_ge(o_free, i + 1)
                w = lambda t, k: t[:, bass.ds(e, 1), k, :].rearrange("p o d -> p (o d)")
                for k in range(KH):
                    s = slice(k * P, (k + 1) * P)
                    pe.matmul(o_ps[u][:, :], g_hi[u][:, s], w(w2_hi, k), start=(k == 0), stop=False)
                    pe.matmul(o_ps[u][:, :], g_hi[u][:, s], w(w2_lo, k), start=False, stop=False)
                    last = pe.matmul(o_ps[u][:, :], g_lo[u][:, s], w(w2_hi, k), start=False, stop=(k == KH - 1))
                last.then_inc(o_full, 1)

            def expert(i):
                return pe.value_load(owner[0:1, bass.ds(i, 1)], min_val=0, max_val=E - 1)

            pe.sem_inc(th_free, 2)
            pe.sem_inc(o_free, 2)
            pe.wait_ge(owner_ready, 1)
            x_turn(0, 0, 0)
            x_turn(1, 1, 1)
            pe.wait_ge(w_split, NC)
            h_of(0, 0, expert(0))

            def routed_step(i, phase, e_before):
                u, e = phase % 2, expert(i)
                h_turn(i - 1, 1 - u)
                x_turn(i + 1, 1 - u, (phase + 1) % NX)
                h_of(i, u, e)
                o_of(i - 1, 1 - u, e_before)
                return e

            e = expert(0)
            for i in range(1, 3):
                e = routed_step(i, i, e)
            with pe.Fori(0, PRE // NX) as n:
                e = expert(NX * n + 2)
                for s in range(3, 3 + NX):
                    e = routed_step(NX * n + s, s % NX, e)
            h_turn(PRE, PRE % 2)
            o_of(PRE, PRE % 2, expert(PRE))


def combined(nc, v):
    (D, E, SH, KD, GT, G, NG) = (v[n] for n in "D E SH KD GT G NG".split())
    ident, gsrc, slots, picked, r_dram = (v[n] for n in "ident gsrc slots picked r_dram".split())
    b2_mix = v["b2_mix"]
    x2_groups, n3_groups, out_groups = v["x2_groups"], v["n3_groups"], v["out_groups"]
    KS = SH // P
    with ExitStack() as ctx:
        def sb(name, shape, dt=F32):
            return ctx.enter_context(nc.sbuf_tensor(name, shape, dt))

        def sem(name):
            return ctx.enter_context(nc.semaphore(name))

        def bank(name):
            return ctx.enter_context(nc.psum_tensor(name, [P, 512], F32))

        sp_, f_, t_ = [bank(f"s_ps{i}") for i in range(2)], [bank(f"f_ps{i}") for i in range(2)], [bank(f"t_ps{i}") for i in range(2)]
        g_ = bank("g_ps")
        sb1 = sb("sb1c", [P, KS])
        half = sb("half3", [P, GT])
        n3 = [sb(f"n3_{i}", [P, GT, D]) for i in range(2)]
        x2 = [sb(f"x2_{i}", [P, GT, D]) for i in range(2)]
        r1, r2 = [[sb(f"{n}_{i}", [P, GT, D]) for i in range(2)] for n in ("r1", "r2")]
        idx = [sb(f"idxg{i}", [P, 2, GT], U32) for i in range(2)]
        n_hi, n_lo = [[sb(f"{n}{i}", [P, KD, G], F32R) for i in range(2)] for n in ("n_hi", "n_lo")]
        s_raw = [sb(f"s_raw{i}", [P, KD, SH]) for i in range(2)]
        s1_hi, s1_lo, s2_hi, s2_lo = (sb(n, [P, KD, SH], F32R) for n in ("s1_hi", "s1_lo", "s2_hi", "s2_lo"))
        hs = sb("hs", [P, KS, G])
        h_hi, h_lo = sb("hs_hi", [P, KS, G], F32R), sb("hs_lo", [P, KS, G], F32R)
        gs = [sb(f"gs{i}", [P, GT, 32]) for i in range(2)]
        gt = sb("gt", [32, G], F32R)
        f = sb("f", [P, GT, D])
        y = sb("y", [P, GT, D])
        st, mv, va, r, nm = (sb("f_st", [P, GT, 6]), sb("f_mv", [P, GT, 2]), sb("f_va", [P, GT]), sb("f_r", [P, GT]),
                             sb("f_nm", [P, GT]))
        small_in, half_set = sem("sb1_in"), sem("half3_set")
        sw_in, sw_hi, sw_split = [sem(f"sw_in{i}") for i in range(2)], sem("sw_hi"), sem("sw_split")
        n3_in, x2_in = [sem(f"n3_in{i}") for i in range(2)], [sem(f"x2_in{i}") for i in range(2)]
        rows_in = [sem(f"rows_in{i}") for i in range(2)]
        idx_set, gs_set, may_gather = sem("idxg_set"), sem("gs_set"), sem("may_gather3")
        t_full, t_free, n_hi_done = sem("t_full"), sem("t_free"), sem("n_hi_done")
        s_full, s_free, h_hi_done, h_split = sem("s_full"), sem("s_free"), sem("h_hi_done3"), sem("h_split3")
        g_full, g_ready = sem("g_full"), sem("g_ready")
        f_full, f_free, f_ready = sem("f_full"), sem("f_free"), sem("f_ready")
        st_done, mv_done, va_ready, r_ready, nm_ready, y_normed, y_ready, stored = (
            sem(n) for n in ("st_done", "mv_done", "va_ready", "r_ready", "nm3_ready", "y_normed", "y_ready", "stored"))

        block = ctx.enter_context(nc.Block())

        @block.sync
        def _(sp):
            sp.dma_start(n3[0][:, :, :], n3_groups[0]).then_inc(n3_in[0], 16)
            for i, w in enumerate((v["sw1"], v["sw2"])):
                sp.dma_start(s_raw[i][:, :, :], w.rearrange("(k p) h -> p k h", p=P)).then_inc(sw_in[i], 16)
            sp.dma_start(sb1[:, :], v["sb1"]).then_inc(small_in, 16)
            sp.dma_start(n3[1][:, :, :], n3_groups[1]).then_inc(n3_in[1], 16)
            for u in range(2):
                sp.dma_start(x2[u][:, :, :], x2_groups[u]).then_inc(x2_in[u], 16)

            def store(g):
                sp.wait_ge(y_ready, GT * (g + 1))
                sp.dma_start(out_groups[g], y[:, :, :]).then_inc(stored, 16)

            with sp.Fori(0, NG // 2 - 1) as n:
                for u in range(2):
                    g = 2 * n + u
                    sp.wait_ge(t_full, KD * (g + 1))
                    sp.dma_start(n3[u][:, :, :], n3_groups[g + 2]).then_inc(n3_in[u], 16)
                    store(g)
                    sp.dma_start(x2[u][:, :, :], x2_groups[g + 2]).then_inc(x2_in[u], 16)
            for u in range(2):
                store(NG - 2 + u)
            sp.wait_ge(stored, 16 * (NG + 1))

        @block.vector
        def _(dve):
            dve.memset(half[:, :], -0.5).then_inc(half_set, 1)
            dve.sem_inc(t_free, 2)
            dve.sem_inc(f_free, 2)

            def n_lo_parts(g, u, ks):
                for k in ks:
                    dve.wait_ge(n_hi_done, KD * g + k + 1)
                    dve.tensor_tensor(n_lo[u][:, k, :], t_[k % 2][:, :], n_hi[u][:, k, :].bitcast(F32), ALU.subtract)\
                       .then_inc(t_free, 1)

            def h_lo_parts(g, ms):
                for m in ms:
                    dve.wait_ge(h_hi_done, KS * g + m + 1)
                    dve.tensor_tensor(h_lo[:, m, :], hs[:, m, :], h_hi[:, m, :].bitcast(F32), ALU.subtract)\
                       .then_inc(h_split, 1)

            def sums(g, u):
                for j in range(GT):
                    t = GT * g + j
                    if j == 0:
                        dve.wait_ge(rows_in[u], 16 * 2 * GT * (g // 2 + 1))
                        if not (isinstance(g, int) and g == 0):
                            dve.wait_ge(y_normed, GT * g)
                    dve.wait_ge(f_full, t + 1)
                    dve.scalar_tensor_tensor(f[:, j, :], r1[u][:, j, :], picked[:, 0, bass.ds(t, 1)], f_[j % 2][:, :],
                                             ALU.mult, ALU.add).then_inc(f_free, 1)
                    dve.wait_ge(f_free, 2 + t + 1)
                    dve.scalar_tensor_tensor(f[:, j, :], r2[u][:, j, :], picked[:, 1, bass.ds(t, 1)], f[:, j, :],
                                             ALU.mult, ALU.add).then_inc(f_ready, 1)
                    dve.wait_ge(f_ready, t + 1)
                    last = dve.bn_stats(st[:, j, :], f[:, j, :])
                last.then_inc(st_done, 1)
                need = value(dve, g + 1)
                dve.wait_ge(half_set, 1)
                dve.wait_ge(st_done, need)
                for j in range(GT):
                    last = dve.bn_aggr(mv[:, j, :], st[:, j, :])
                last.then_inc(mv_done, 1)
                dve.wait_ge(mv_done, g + 1)
                dve.tensor_scalar(va[:, :], mv[:, :, 1], EPS, None, ALU.add).then_inc(va_ready, 1)

            def shift(g):
                dve.wait_ge(r_ready, g + 1)
                dve.scalar_tensor_tensor(nm[:, :], mv[:, :, 0], -1.0, r[:, :], ALU.mult, ALU.mult).then_inc(nm_ready, 1)

            n_lo_parts(0, 0, range(KD))
            for i, (hi, lo) in enumerate(((s1_hi, s1_lo), (s2_hi, s2_lo))):
                for k in range(KD):
                    dve.wait_ge(sw_hi, KD * i + k + 1)
                    dve.tensor_tensor(lo[:, k, :], s_raw[i][:, k, :], hi[:, k, :].bitcast(F32), ALU.subtract)\
                       .then_inc(sw_split, 1)

            def group(g, u, last=False):
                h_lo_parts(g, range(KS - 1))
                if not last:
                    n_lo_parts(g + 1, 1 - u, (0, 1))
                h_lo_parts(g, (KS - 1,))
                if not last:
                    n_lo_parts(g + 1, 1 - u, (2, 3))
                sums(g, u)
                shift(g)

            group(0, 0)
            with dve.Fori(0, NG // 2 - 1) as n:
                for s in range(2):
                    group(2 * n + 1 + s, 1 - s)
            group(NG - 1, 1, last=True)

        @block.scalar
        def _(act):
            act.sem_inc(s_free, 2)
            act.wait_ge(small_in, 16)

            def n_hi_parts(g, u, ks):
                for k in ks:
                    act.wait_ge(t_full, KD * g + k + 1)
                    act.activation(n_hi[u][:, k, :], t_[k % 2][:, :], ACT.Copy).then_inc(n_hi_done, 1)

            def gelu(g, ms):
                for m in ms:
                    act.wait_ge(s_full, KS * g + m + 1)
                    act.activation(hs[:, m, :], sp_[m % 2][:, :], ACT.Gelu, bias=sb1[:, m:m + 1]).then_inc(s_free, 1)
                    act.wait_ge(s_free, 2 + KS * g + m + 1)
                    act.activation(h_hi[:, m, :], hs[:, m, :], ACT.Copy).then_inc(h_hi_done, 1)

            def gates(g):
                act.wait_ge(g_full, g + 1)
                act.activation(gt[:, :], g_[0:32, :], ACT.Copy).then_inc(g_ready, 1)

            def normed(g, js):
                act.wait_ge(nm_ready, g + 1)
                act.wait_ge(stored, 16 * (g + 1))
                for j in js:
                    act.activation(y[:, j, :], f[:, j, :], ACT.Identity, bias=nm[:, j:j + 1], scale=r[:, j:j + 1])\
                       .then_inc(y_normed, 1)

            n_hi_parts(0, 0, range(KD))
            for i, hi in enumerate((s1_hi, s2_hi)):
                act.wait_ge(sw_in[i], 16)
                for k in range(KD):
                    act.activation(hi[:, k, :], s_raw[i][:, k, :], ACT.Copy).then_inc(sw_hi, 1)

            def group(g, u, first=False, last=False):
                gelu(g, (0, 1))
                if not first:
                    normed(g - 1, (0, 1))
                gelu(g, range(2, KS - 1))
                if not last:
                    n_hi_parts(g + 1, 1 - u, (0, 1))
                gelu(g, (KS - 1,))
                gates(g)
                if not last:
                    n_hi_parts(g + 1, 1 - u, (2, 3))
                if not first:
                    normed(g - 1, (2, 3))

            group(0, 0, first=True)
            with act.Fori(0, NG // 2 - 1) as n:
                for s in range(2):
                    group(2 * n + 1 + s, 1 - s)
            group(NG - 1, 1, last=True)
            normed(NG - 1, range(GT))

        @block.gpsimd
        def _(pool):
            pool.sem_inc(stored, 16)
            pool.wait_ge(half_set, 1)

            def gather(g, u):
                pool.tensor_copy(gs[u][:, :, :], gsrc[:, bass.ds(GT * g, GT), :]).then_inc(gs_set, 1)
                pool.tensor_copy(idx[u][:, :, :], slots[:, :, bass.ds(GT * g, GT)]).then_inc(idx_set, 1)
                pool.wait_ge(idx_set, g + 1)
                pool.sem_inc(may_gather, 1)
                for j in range(GT):
                    for c, rr in ((0, r1), (1, r2)):
                        pool.indirect_dma_start(rr[u][:, j, :], None, r_dram,
                                                bass.IndirectOffsetOnAxis(idx[u][:, c, j:j + 1], 0))\
                            .then_inc(rows_in[u], 16)

            def finish(g, u):
                pool.wait_ge(va_ready, g + 1)
                pool.tensor_tensor(r[:, :], va[:, :], half[:, :], ALU.pow).then_inc(r_ready, 1)
                pool.wait_ge(x2_in[u], 16 * (g // 2 + 1))
                for j in range(GT):
                    pool.wait_ge(y_normed, GT * g + j + 1)
                    pool.tensor_tensor(y[:, j, :], y[:, j, :], x2[u][:, j, :], ALU.add).then_inc(y_ready, 1)

            gather(0, 0)
            gather(1, 1)
            with pool.Fori(0, NG // 2 - 1) as n:
                for u in range(2):
                    g = 2 * n + u
                    finish(g, u)
                    pool.wait_ge(f_ready, GT * (g + 1))
                    pool.sem_inc(may_gather, 1)
                    gather(g + 2, u)
            for u in range(2):
                finish(NG - 2 + u, u)

        @block.tensor
        def _(pe):
            def n3_turn(g, u, ks):
                pe.wait_ge(n3_in[u], 16 * (g // 2 + 1))
                for k in ks:
                    pe.wait_ge(t_free, KD * g + k + 1)
                    for j in range(GT):
                        last = pe.transpose(t_[k % 2][:, j * P:(j + 1) * P], n3[u][:, j, k * P:(k + 1) * P], ident[:, :])
                    last.then_inc(t_full, 1)

            def shared_h(g, u, ms):
                if ms[0] == 0:
                    pe.wait_ge(t_free, 2 + KD * (g + 1))
                for m in ms:
                    pe.wait_ge(s_free, KS * g + m + 1)
                    s = slice(m * P, (m + 1) * P)
                    for k in range(KD):
                        pe.matmul(sp_[m % 2][:, :], s1_hi[:, k, s], n_hi[u][:, k, :], start=(k == 0), stop=False)
                        pe.matmul(sp_[m % 2][:, :], s1_hi[:, k, s], n_lo[u][:, k, :], start=False, stop=False)
                        last = pe.matmul(sp_[m % 2][:, :], s1_lo[:, k, s], n_hi[u][:, k, :], start=False,
                                         stop=(k == KD - 1))
                    last.then_inc(s_full, 1)

            def gates(g, u):
                pe.wait_ge(gs_set, g + 1)
                pe.wait_ge(g_ready, g + 1)
                for j in range(GT):
                    last = pe.transpose(g_[0:32, j * P:(j + 1) * P], gs[u][:, j, :], ident[:, :])
                last.then_inc(g_full, 1)

            def shared_o(g):
                pe.wait_ge(h_split, KS * (g + 1))
                pe.wait_ge(g_ready, 1 + g + 1)
                for j in range(GT):
                    pe.wait_ge(f_free, GT * g + j + 1)
                    s = slice(j * P, (j + 1) * P)
                    out = f_[j % 2][:, :]
                    for k in range(KS):
                        pe.matmul(out, h_hi[:, k, s], s2_hi[:, k, :], start=(k == 0), stop=False)
                        pe.matmul(out, h_hi[:, k, s], s2_lo[:, k, :], start=False, stop=False)
                        pe.matmul(out, h_lo[:, k, s], s2_hi[:, k, :], start=False, stop=False)
                    pe.matmul(out, gt[:, s], b2_mix[:, :], start=False, stop=True).then_inc(f_full, 1)

            pe.sem_inc(g_ready, 1)
            n3_turn(0, 0, range(KD))
            pe.wait_ge(sw_split, 2 * KD)

            def group(g, u, last=False):
                shared_h(g, u, range(KS - 1))
                if not last:
                    n3_turn(g + 1, 1 - u, (0, 1))
                shared_h(g, u, (KS - 1,))
                gates(g, u)
                if not last:
                    n3_turn(g + 1, 1 - u, (2, 3))
                shared_o(g)

            with pe.Fori(0, NG // 2 - 1) as n:
                for u in range(2):
                    group(2 * n + u, u)
            group(NG - 2, 0)
            group(NG - 1, 1, last=True)


_NAMES = ["X", "ln_w", "ln_b", "W_in", "b_in", "W_out", "b_out"]
_FFN = ["gate_w", "w1", "b1", "w2", "b2", "shared_w1", "shared_b1", "shared_w2", "shared_b2"]


def _pairs_apart(n):
    return np.concatenate([np.arange(0, n // 2, 2), np.arange(1, n // 2, 2), np.arange(n // 2, n)])


def _angles(seq, n):
    rot = n // 2
    inv = (1.0 / np.float64(THETA) ** (np.arange(0, rot, 2) / rot)).astype(np.float32)
    a = np.arange(seq, dtype=np.float32)[:, None] * inv[None, :]
    return np.cos(a).astype(np.float32), np.sin(a).astype(np.float32)


def _columns(x):
    return np.moveaxis(x.reshape(*x.shape[:-1], -1, P), -1, 0)


def kernel(**inputs):
    import concourse.bacc as _bacc
    from concourse.bass_utils import run_bass_kernel_spmd as _run

    nc = _bacc.Bacc("TRN2", target_bir_lowering=False, num_devices=1)
    a = {k: np.asarray(x) for k, x in inputs.items()}
    Bn, S, D = a["L0_attn_X"].shape
    order = _pairs_apart(D)
    cols = np.concatenate([order + c * D for c in range(3)])
    host = {n: a[f"L0_attn_{n}"] for n in _NAMES}
    host["W_in"] = host["W_in"][:, cols]
    host["b_in"] = host["b_in"][cols]
    host["W_out"] = host["W_out"][order, :]
    host.update({n: a[f"L0_ffn_{n}"] for n in _FFN})
    for n in ("ln_w", "ln_b", "shared_b1"):
        host[n] = _columns(host[n])
    host["b_q"] = _columns(host["b_in"][:D])
    cos, sin = _angles(S, D)
    host["rope_tok"] = np.concatenate([cos, sin], axis=1)
    host["rope_feat"] = np.stack([cos.T, sin.T])
    host["identity"] = np.eye(P, dtype=np.float32)
    host["before"] = np.triu(np.ones((P, P), np.float32), 1)
    E = a["L0_ffn_b2"].shape[0]
    row = np.arange(32)
    host["bias_parts"] = np.stack([(row < 2 * E) | (row == 3 * E), ((row >= 2 * E) & (row < 3 * E)) | (row == 3 * E + 1)],
                                  axis=1).astype(np.float32)
    arrays, args = {}, []
    for name, x in host.items():
        x = np.ascontiguousarray(x)
        arrays[f"in_{name}"] = x
        args.append(nc.dram_tensor(f"in_{name}", x.shape, mybir.dt.from_np(x.dtype), kind="ExternalInput").ap())
    out = nc.dram_tensor("out_0", (Bn, S, D), F32, kind="ExternalOutput").ap()
    sandwich_kernel(nc, *args, out)
    r = _run(nc, [arrays], core_ids=[0])
    return r.results[0]["out_0"]
```
